# Optimizing a Trainium2 kernel written in Bass

```python
import numpy as np
import jax
import jax.numpy as jnp

def _softmax(x, axis=-1):
    return jax.nn.softmax(x, axis=axis)

def _gelu(x):
    return jax.nn.gelu(x, approximate=True)

def _silu(x):
    return jax.nn.silu(x)

def _sigmoid(x):
    return jax.nn.sigmoid(x)

def _layernorm(x, axis=-1, eps=1e-05):
    m = jnp.mean(x, axis=axis, keepdims=True)
    v = jnp.var(x, axis=axis, keepdims=True)
    return (x - m) / jnp.sqrt(v + eps)

def _scatter_add(tgt, idx, src, axis=0):
    return tgt.at[idx].add(src)

def _segment_sum(src, seg, n):
    return jax.ops.segment_sum(src, seg, n)
kernel_name = 'mk_early_fusion_d1_tok_img768_r4_edd465'

def setup_inputs(seed: int=0):
    np.random.seed(seed)
    _w = jnp.asarray

    def _rec_inputs():
        import jax
        import jax.numpy as jnp
        _rk = jax.random.key(seed)
        x = 7.57192e-06 + 1.00007 * jax.random.normal(jax.random.fold_in(_rk, 1), (32, 112, 112, 3), jnp.float32)
        txt = -0.0429142 + 10 * jax.random.normal(jax.random.fold_in(_rk, 2), (32, 32, 192), jnp.float32)
        return (x, txt)
    x, txt = _rec_inputs()

    def _L0_tok_setup():
        import jax, jax.numpy as jnp
        import numpy as np
        PATCH = 16
        DIM = 192
        EPS = 0.001

        def _shifts(x):
            zw = jnp.zeros_like(x[:, :, :1, :])
            right = jnp.concatenate([zw, x[:, :, :-1, :]], axis=2)
            left = jnp.concatenate([x[:, :, 1:, :], zw], axis=2)
            zh = jnp.zeros_like(x[:, :1, :, :])
            down = jnp.concatenate([zh, x[:, :-1, :, :]], axis=1)
            up = jnp.concatenate([x[:, 1:, :, :], zh], axis=1)
            return [right, left, down, up]

        def _patchify(x, p):
            b, H, W, C = x.shape
            hh, ww = (H // p, W // p)
            x = x.reshape(b, hh, p, ww, p, C)
            x = x.transpose(0, 1, 3, 2, 4, 5)
            return x.reshape(b, hh * ww, p * p * C)
        key = jax.random.key(seed)
        k1, k2 = jax.random.split(key)
        b, H, Wd, C = (64, 224, 224, 3)
        F = PATCH * PATCH * 5 * C
        x = jax.random.normal(k1, (b, H, Wd, C), dtype=jnp.float32)
        gamma = jnp.ones((F,), dtype=jnp.float32)
        beta = jnp.zeros((F,), dtype=jnp.float32)
        W = jax.random.normal(k2, (F, DIM), dtype=jnp.float32)
        bb = jnp.zeros((DIM,), dtype=jnp.float32)
        return {'x': x, 'gamma': gamma, 'beta': beta, 'W': W, 'b': bb}
    _L0_tok_all = _L0_tok_setup()
    _L0_tok_in = {k: v for k, v in _L0_tok_all.items() if k in ('gamma', 'beta', 'W', 'b')}
    del _L0_tok_all

    def _L0_attn_setup():
        import jax, jax.numpy as jnp
        import numpy as np
        NUM_HEADS = 12
        key = jax.random.key(seed)
        k1, k2, k3 = jax.random.split(key, 3)
        B, N, C = (8, 256, 192)
        x = jax.random.normal(k1, (B, N, C), dtype=jnp.float32)
        w_qkv = jax.random.normal(k2, (3 * C, C), dtype=jnp.float32) * C ** (-0.5)
        w_proj = jax.random.normal(k3, (C, C), dtype=jnp.float32) * C ** (-0.5)
        b_proj = jnp.zeros((C,), dtype=jnp.float32)
        return {'x': x, 'w_qkv': w_qkv, 'w_proj': w_proj, 'b_proj': b_proj}
    _L0_attn_all = _L0_attn_setup()
    _L0_attn_in = {k: v for k, v in _L0_attn_all.items() if k in ('w_qkv', 'w_proj', 'b_proj')}
    del _L0_attn_all

    def _L0_ffn_setup():
        import jax, jax.numpy as jnp
        import numpy as np
        B, N, DIM, HEADS = (4, 256, 192, 12)
        HIDDEN, E, TOPK = (768, 8, 2)
        EPS = 1e-05

        def _layernorm(x, g, b):
            mu = jnp.mean(x, axis=-1, keepdims=True)
            var = jnp.var(x, axis=-1, keepdims=True)
            return (x - mu) * jax.lax.rsqrt(var + EPS) * g + b
        key = jax.random.key(seed)
        ks = jax.random.split(key, 10)
        s = 0.02
        return {'x': jax.random.normal(ks[0], (B, N, DIM), dtype=jnp.float32), 'ln1_g': jnp.ones((DIM,), jnp.float32), 'ln1_b': jnp.zeros((DIM,), jnp.float32), 'qkv_w': jax.random.normal(ks[1], (3 * DIM, DIM), jnp.float32) * s, 'proj_w': jax.random.normal(ks[2], (DIM, DIM), jnp.float32) * s, 'proj_b': jnp.zeros((DIM,), jnp.float32), 'ln2_g': jnp.ones((DIM,), jnp.float32), 'ln2_b': jnp.zeros((DIM,), jnp.float32), 'gate_w': jax.random.normal(ks[3], (E, DIM), jnp.float32) * s, 'gate_b': jnp.zeros((E,), jnp.float32), 'w1': jax.random.normal(ks[4], (E, HIDDEN, DIM), jnp.float32) * s, 'b1': jnp.zeros((E, HIDDEN), jnp.float32), 'w2': jax.random.normal(ks[5], (E, DIM, HIDDEN), jnp.float32) * s, 'b2': jnp.zeros((E, DIM), jnp.float32)}
    _L0_ffn_all = _L0_ffn_setup()
    _L0_ffn_in = {k: v for k, v in _L0_ffn_all.items() if k in ('ln1_g', 'ln1_b', 'qkv_w', 'proj_w', 'proj_b', 'ln2_g', 'ln2_b', 'gate_w', 'gate_b', 'w1', 'b1', 'w2', 'b2')}
    del _L0_ffn_all
    return {'x': x, 'txt': txt, 'L0_tok_gamma': _L0_tok_in['gamma'], 'L0_tok_beta': _L0_tok_in['beta'], 'L0_tok_W': _L0_tok_in['W'], 'L0_tok_b': _L0_tok_in['b'], 'L0_attn_w_qkv': _L0_attn_in['w_qkv'], 'L0_attn_w_proj': _L0_attn_in['w_proj'], 'L0_attn_b_proj': _L0_attn_in['b_proj'], 'L0_ffn_ln1_g': _L0_ffn_in['ln1_g'], 'L0_ffn_ln1_b': _L0_ffn_in['ln1_b'], 'L0_ffn_qkv_w': _L0_ffn_in['qkv_w'], 'L0_ffn_proj_w': _L0_ffn_in['proj_w'], 'L0_ffn_proj_b': _L0_ffn_in['proj_b'], 'L0_ffn_ln2_g': _L0_ffn_in['ln2_g'], 'L0_ffn_ln2_b': _L0_ffn_in['ln2_b'], 'L0_ffn_gate_w': _L0_ffn_in['gate_w'], 'L0_ffn_gate_b': _L0_ffn_in['gate_b'], 'L0_ffn_w1': _L0_ffn_in['w1'], 'L0_ffn_b1': _L0_ffn_in['b1'], 'L0_ffn_w2': _L0_ffn_in['w2'], 'L0_ffn_b2': _L0_ffn_in['b2']}

def reference(x, txt, L0_tok_gamma, L0_tok_beta, L0_tok_W, L0_tok_b, L0_attn_w_qkv, L0_attn_w_proj, L0_attn_b_proj, L0_ffn_ln1_g, L0_ffn_ln1_b, L0_ffn_qkv_w, L0_ffn_proj_w, L0_ffn_proj_b, L0_ffn_ln2_g, L0_ffn_ln2_b, L0_ffn_gate_w, L0_ffn_gate_b, L0_ffn_w1, L0_ffn_b1, L0_ffn_w2, L0_ffn_b2):
    import jax
    import jax.numpy as jnp

    def _L0_tok_ref(x, gamma, beta, W, b):
        import jax, jax.numpy as jnp
        import numpy as np
        PATCH = 16
        DIM = 192
        EPS = 0.001

        def _shifts(x):
            zw = jnp.zeros_like(x[:, :, :1, :])
            right = jnp.concatenate([zw, x[:, :, :-1, :]], axis=2)
            left = jnp.concatenate([x[:, :, 1:, :], zw], axis=2)
            zh = jnp.zeros_like(x[:, :1, :, :])
            down = jnp.concatenate([zh, x[:, :-1, :, :]], axis=1)
            up = jnp.concatenate([x[:, 1:, :, :], zh], axis=1)
            return [right, left, down, up]

        def _patchify(x, p):
            b, H, W, C = x.shape
            hh, ww = (H // p, W // p)
            x = x.reshape(b, hh, p, ww, p, C)
            x = x.transpose(0, 1, 3, 2, 4, 5)
            return x.reshape(b, hh * ww, p * p * C)
        x5 = jnp.concatenate([x] + _shifts(x), axis=-1)
        tokens = _patchify(x5, PATCH)
        mu = jnp.mean(tokens, axis=-1, keepdims=True)
        var = jnp.mean(jnp.square(tokens - mu), axis=-1, keepdims=True)
        ln = (tokens - mu) * jax.lax.rsqrt(var + EPS) * gamma + beta
        return jnp.einsum('bnf,fd->bnd', ln, W) + b

    def _L0_attn_ref(x, w_qkv, w_proj, b_proj):
        import jax, jax.numpy as jnp
        import numpy as np
        NUM_HEADS = 12
        B, N, C = x.shape
        H = NUM_HEADS
        Dh = C // H
        scale = Dh ** (-0.5)
        qkv = jnp.einsum('bnc,dc->bnd', x, w_qkv)
        qkv = qkv.reshape(B, N, 3, H, Dh).transpose(2, 0, 3, 1, 4)
        q, k, v = (qkv[0], qkv[1], qkv[2])
        attn = jnp.einsum('bhnd,bhmd->bhnm', q, k) * scale
        attn = jax.nn.softmax(attn, axis=-1)
        out = jnp.einsum('bhnm,bhmd->bhnd', attn, v)
        out = out.transpose(0, 2, 1, 3).reshape(B, N, C)
        out = jnp.einsum('bnc,dc->bnd', out, w_proj) + b_proj
        return out

    def _L0_ffn_ref(x, ln1_g, ln1_b, qkv_w, proj_w, proj_b, ln2_g, ln2_b, gate_w, gate_b, w1, b1, w2, b2):
        import jax, jax.numpy as jnp
        import numpy as np
        B, N, DIM, HEADS = (4, 256, 192, 12)
        HIDDEN, E, TOPK = (768, 8, 2)
        EPS = 1e-05

        def _layernorm(x, g, b):
            mu = jnp.mean(x, axis=-1, keepdims=True)
            var = jnp.var(x, axis=-1, keepdims=True)
            return (x - mu) * jax.lax.rsqrt(var + EPS) * g + b
        b, n, d = x.shape
        hd = d // HEADS
        scale = hd ** (-0.5)
        h = _layernorm(x, ln1_g, ln1_b)
        qkv = h @ qkv_w.T
        qkv = qkv.reshape(b, n, 3, HEADS, hd).transpose(2, 0, 3, 1, 4)
        q, k, v = (qkv[0], qkv[1], qkv[2])
        attn = jax.nn.softmax(jnp.einsum('bhnd,bhmd->bhnm', q, k) * scale, axis=-1)
        a = jnp.einsum('bhnm,bhmd->bhnd', attn, v)
        a = a.transpose(0, 2, 1, 3).reshape(b, n, d)
        a = a @ proj_w.T + proj_b
        x = x + a
        h2 = _layernorm(x, ln2_g, ln2_b)
        t = h2.reshape(-1, d)
        T = t.shape[0]
        logits = t @ gate_w.T + gate_b
        top_val, top_idx = jax.lax.top_k(logits, TOPK)
        score = jax.nn.softmax(top_val, axis=-1)
        cw = jnp.zeros((T, E), t.dtype).at[jnp.arange(T)[:, None], top_idx].add(score)
        out = jnp.zeros_like(t)
        for e in range(E):
            he = jax.nn.gelu(t @ w1[e].T + b1[e], approximate=False)
            ye = he @ w2[e].T + b2[e]
            out = out + cw[:, e:e + 1] * ye
        return x + out.reshape(b, n, d)
    h = _L0_tok_ref(x, L0_tok_gamma, L0_tok_beta, L0_tok_W, L0_tok_b)
    h = jnp.concatenate([h, txt], axis=1)
    h = h + _L0_attn_ref(_layernorm(h, axis=-1), L0_attn_w_qkv, L0_attn_w_proj, L0_attn_b_proj)
    h = h + _L0_ffn_ref(_layernorm(h, axis=-1), L0_ffn_ln1_g, L0_ffn_ln1_b, L0_ffn_qkv_w, L0_ffn_proj_w, L0_ffn_proj_b, L0_ffn_ln2_g, L0_ffn_ln2_b, L0_ffn_gate_w, L0_ffn_gate_b, L0_ffn_w1, L0_ffn_b1, L0_ffn_w2, L0_ffn_b2)
    return h

_drawn_inputs = setup_inputs


def setup_inputs(seed=0):
    import zlib

    import numpy as np

    out = dict(_drawn_inputs(seed))
    spreads = {'L0_tok_gamma': (1.0, 0.2),
     'L0_tok_beta': (0.0, 0.1),
     'L0_tok_b': (0.0, 0.8),
     'L0_attn_b_proj': (0.0, 2.0),
     'L0_ffn_ln1_g': (1.0, 0.6),
     'L0_ffn_ln1_b': (0.0, 0.8),
     'L0_ffn_proj_b': (0.0, 2.0),
     'L0_ffn_ln2_g': (1.0, 0.6),
     'L0_ffn_ln2_b': (0.0, 0.8),
     'L0_ffn_gate_b': (0.0, 0.8),
     'L0_ffn_b1': (0.0, 2.0),
     'L0_ffn_b2': (0.0, 2.0)}
    factors = {'L0_attn_w_qkv': 8.0,
     'L0_attn_w_proj': 8.0,
     'L0_ffn_qkv_w': 8.0,
     'L0_ffn_proj_w': 8.0,
     'L0_ffn_gate_w': 8.0,
     'L0_ffn_w1': 8.0,
     'L0_ffn_w2': 8.0}
    for name, (base, spread) in spreads.items():
        noise = np.random.default_rng([zlib.crc32(name.encode()), seed]).standard_normal(out[name].shape)
        drawn = base * np.exp(spread * noise) if base else spread * noise
        out[name] = jnp.asarray(drawn.astype(out[name].dtype))
    for name, factor in factors.items():
        out[name] = (out[name] * factor).astype(out[name].dtype)
    return out
```

```python
from contextlib import ExitStack

import concourse.bass as bass
from concourse import mybir

ALU = mybir.AluOpType
ACT = mybir.ActivationFunctionType
AX = mybir.AxisListType
F32 = mybir.dt.float32
U32 = mybir.dt.uint32
I32 = mybir.dt.int32

IMAGES = 32
SIDE = 7
PATCHES = SIDE * SIDE
TEXT = 32
SEQ = PATCHES + TEXT
DIM = 192
KC = 96
CHUNKS = DIM // KC
HEADS = 12
HEAD = DIM // HEADS
ROWS = 4
GROUPS = HEADS // ROWS
SLOT = 32

PATCH = 16
CHANNELS = 3
CENTER = PATCH * PATCH * CHANNELS
HALO = 4 * PATCH * CHANNELS
FEATURES = CENTER + HALO
SHIFTS = 5
COPIED = SHIFTS * CENTER
CENTER_CHUNKS = CENTER // KC
FEATURE_CHUNKS = FEATURES // KC
PAIR = 2 * PATCHES
PAIRS = IMAGES // 2
BN = 6

EXPERTS = 8
TOP = 2
HIDDEN = 768
HIDDEN_CHUNKS = HIDDEN // 128
TOKENS = IMAGES * SEQ
TILE = 128
REGION = TOKENS + TILE
TILES = (TOP * TOKENS + EXPERTS * (TILE - 1)) // TILE
ROW = DIM + 2
NOWHERE = 1 << 20
LOGIT_AT, RANK_AT = 200, 216
BLOCKS = 2
EPS = 1e-5
CONSTS = 7
ROUTE_LOADS = 8
COMBINE = 8


def build(nc, t):
    with ExitStack() as ctx:
        def sb(name, shape, dt=F32):
            return ctx.enter_context(nc.sbuf_tensor(name, shape, dt))

        def sem(name):
            return ctx.enter_context(nc.semaphore(name))

        stream = sb("stream", [SEQ, IMAGES, DIM])
        ident = sb("ident", [128, 128])
        ones = sb("ones", [128, 128])
        half = sb("half", [128, PAIRS])
        minus_one = sb("minus_one", [128, 1])
        eps = sb("eps", [128, 1])
        tick = sb("tick", [1, 1])

        arena_a = sb("arena_a", [128, SHIFTS * CENTER_CHUNKS * DIM])
        arena_b = sb("arena_b", [128, SHIFTS * CENTER_CHUNKS * DIM])
        w_center = arena_a[0:KC, :].rearrange("k (s c d) -> k s c d", s=SHIFTS, c=CENTER_CHUNKS)
        w_halo = sb("w_halo", [KC, FEATURE_CHUNKS - CENTER_CHUNKS, DIM])
        gain = sb("gain", [KC, SHIFTS * CENTER_CHUNKS + 2])
        shift = sb("shift", [KC, SHIFTS * CENTER_CHUNKS + 2])
        w_scaled = arena_b[0:KC, :].rearrange("k (s c d) -> k s c d", s=SHIFTS, c=CENTER_CHUNKS)
        w_fold = sb("w_fold", [KC, FEATURE_CHUNKS, DIM])
        b_row = sb("b_row", [1, DIM])
        bias_row = sb("bias_row", [1, DIM])
        colsum = sb("colsum", [PAIR, DIM])
        bias_all = sb("bias_all", [PAIR, DIM])
        arena_c = sb("arena_c", [128, 2 * (ROW + 3 * DIM + CHUNKS * TILE)])
        arena_d = sb("arena_d", [128, 2 * FEATURE_CHUNKS * PAIR])
        pix = arena_c[0:PAIR, 0:2 * FEATURES].rearrange("t (p f) -> t p f", p=2)
        pixT = arena_d[0:KC, :].rearrange("k (p c t) -> k p c t", p=2, c=FEATURE_CHUNKS)
        bn_c = sb("bn_c", [PAIR, 2, 2 * BN])
        bn_h = sb("bn_h", [PAIR, 2, BN])
        bn_e = sb("bn_e", [PAIR, 2, 2 * BN])
        mv_k = sb("mv_k", [PAIR, 2, 3, 2])
        mv = sb("mv", [PAIR, PAIRS, 3, 2])
        stat = sb("stat", [PAIR, 8, PAIRS])
        raw = sb("raw", [PAIR, PAIRS, DIM])

        w_qk = sb("w_qk", [KC, BLOCKS, CHUNKS, 2, GROUPS, 128])
        w_v = sb("w_v", [KC, BLOCKS, CHUNKS, DIM])
        w_p = sb("w_p", [KC + 1, BLOCKS, CHUNKS, DIM])
        k_one = sb("k_one", [128, 1])
        bn_x = sb("bn_x", [SEQ, 2, BN])
        mv_x = sb("mv_x", [SEQ, 2, 2])
        veps = sb("veps", [SEQ, 2, 1])
        rstd = sb("rstd", [SEQ, 2, 1])
        rstd2 = sb("rstd2", [SEQ, 2, 1])
        nmr = sb("nmr", [SEQ, 2, 1])
        scale2 = sb("scale2", [SEQ, 2, 1])
        nmr2 = sb("nmr2", [SEQ, 2, 1])
        xn = sb("xn", [SEQ, 2, DIM])
        aT = sb("aT", [KC, 2, CHUNKS, SEQ])
        qk = sb("qk", [128, 2, 2, GROUPS, SEQ])
        v1 = sb("v1", [SEQ, 2, HEADS, HEAD + 1])
        mpad = sb("mpad", [SEQ, 2, GROUPS, ROWS, SLOT])
        qm = sb("qm", [128, 2, GROUPS, SEQ])
        probs = sb("probs", [SEQ, 2, ROWS, GROUPS, SEQ])
        rec = sb("rec", [SEQ, 2, HEADS, 1])
        o = sb("o", [SEQ, 2, HEADS, HEAD])
        oT = sb("oT", [KC + 1, CHUNKS, SEQ])

        inner = sb("inner", [SEQ, IMAGES, DIM])
        affine = sb("affine", [KC, 2, 2, CHUNKS])
        w_gate = sb("w_gate", [KC + 1, CHUNKS, EXPERTS])
        bn_t = sb("bn_t", [SEQ, 2, BN])
        mv_t = sb("mv_t", [SEQ, 2, 2])
        rstd_t = sb("rstd_t", [SEQ, IMAGES, 1])
        nmr_t = sb("nmr_t", [SEQ, IMAGES, 1])
        rstd_s = sb("rstd_s", [SEQ, 2, 1])
        mr_s = sb("mr_s", [SEQ, 2, 1])
        nmr_s = sb("nmr_s", [SEQ, 2, 1])
        veps_t = sb("veps_t", [SEQ, 2, 1])
        xh = sb("xh", [SEQ, 2, DIM])
        tT = sb("tT", [KC + 1, CHUNKS, SEQ])
        before = sb("before", [SEQ, SEQ])
        iota = sb("iota", [SEQ, TOP, EXPERTS])
        region = sb("region", [SEQ, EXPERTS])
        logit = sb("logit", [SEQ, 2, EXPERTS])
        best = sb("best", [SEQ, 2, 8])
        best_at = sb("best_at", [SEQ, 2, 8], U32)
        chosen = sb("chosen", [SEQ, 2, TOP])
        mask = sb("mask", [SEQ, 2, TOP, EXPERTS])
        hits = sb("hits", [SEQ, 2, EXPERTS])
        seen = sb("seen", [SEQ, 2, EXPERTS])
        gap = sb("gap", [SEQ, 2, 1])
        egap = sb("egap", [SEQ, 2, 1])
        esum = sb("esum", [SEQ, 2, 1])
        place = sb("place", [SEQ, 2, EXPERTS])
        placed = sb("placed", [SEQ, 2, TOP, EXPERTS])
        slot_f = sb("slot_f", [SEQ, 2, TOP])
        slot = sb("slot", [SEQ, 2, TOP], U32)
        dest = sb("dest", [SEQ, TOP])
        rows = sb("rows", [SEQ, 2, TOP, ROW])

        padding = sb("padding", [TILE, ROW])
        cnt = sb("cnt", [1, EXPERTS])
        cnt_i = sb("cnt_i", [1, EXPERTS], I32)
        need = sb("need", [1, EXPERTS])
        need_i = sb("need_i", [1, EXPERTS], I32)
        upto = sb("upto", [1, 2, EXPERTS])
        jota = sb("jota", [1, TILES])
        past = sb("past", [1, TILES, EXPERTS])
        tile_e = sb("tile_e", [1, TILES])
        tile_s = sb("tile_s", [1, TILES])
        tile_l = sb("tile_l", [1, TILES])
        expert_i = sb("expert_i", [1, TILES], I32)
        row_i = sb("row_i", [1, TILES], I32)

        e1 = arena_b[0:KC + 1, 0:2 * CHUNKS * HIDDEN].rearrange("k (p c n) -> k p c n", p=2, c=CHUNKS)
        e2 = arena_b[:, 2 * CHUNKS * HIDDEN:2 * CHUNKS * HIDDEN + 2 * HIDDEN_CHUNKS * DIM]\
            .rearrange("k (p c n) -> k p c n", p=2, c=HIDDEN_CHUNKS)
        at = 0
        tiles = []
        for width in (ROW, DIM, DIM, DIM):
            tiles.append(arena_c[:, at:at + 2 * width].rearrange("t (p d) -> t p d", p=2))
            at += 2 * width
        picked, eb, y, ys = tiles
        pT = arena_c[0:KC + 1, at:at + 2 * CHUNKS * TILE].rearrange("k (p c t) -> k p c t", p=2, c=CHUNKS)
        hid = arena_d[:, 0:2 * HIDDEN].rearrange("h (p c t) -> h p c t", p=2, c=HIDDEN_CHUNKS)
        got = arena_a[0:SEQ, 0:2 * TOP * COMBINE * DIM].rearrange("s (p k b d) -> s p k b d", p=2, k=TOP, b=COMBINE)

        ps_s = ctx.enter_context(nc.psum_tensor("ps_s", [128, ROWS, 512], F32))
        ps_q = ctx.enter_context(nc.psum_tensor("ps_q", [128, 512], F32))
        ps_a = ctx.enter_context(nc.psum_tensor("ps_a", [128, 512], F32))
        ps_o = ctx.enter_context(nc.psum_tensor("ps_o", [128, 512], F32))
        ps_v = ctx.enter_context(nc.psum_tensor("ps_v", [128, 512], F32))

        consts = sem("consts")
        ident_zero = sem("ident_zero")
        mpad_zero = sem("mpad_zero")
        small_in = sem("small_in")
        w_in = sem("w_in")
        pix_in = [sem(f"pix_in{p}") for p in range(2)]
        pixT_in = [sem(f"pixT_in{p}") for p in range(2)]
        pix_used = sem("pix_used")
        attn_in = sem("attn_in")
        text_in = sem("text_in")
        scaled = sem("scaled")
        scaled_pool = sem("scaled_pool")
        folded = sem("folded")
        bias_ps = sem("bias_ps")
        bias_out = sem("bias_out")
        sums_ps = sem("sums_ps")
        sums_out = sem("sums_out")
        emb_ps = sem("emb_ps")
        emb_raw = sem("emb_raw")
        dve_step = sem("dve_step")
        var_ready = sem("var_ready")
        rstd_ready = sem("rstd_ready")
        emb_done = sem("emb_done")
        emb_moved = [sem(f"emb_moved{p}") for p in range(2)]

        stats_ready = sem("stats_ready")
        pool_step = sem("pool_step")
        norm_ready = sem("norm_ready")
        xn_ready = sem("xn_ready")
        aT_ps = sem("aT_ps")
        aT_ready = sem("aT_ready")
        qk_ps = sem("qk_ps")
        qk_ready = sem("qk_ready")
        v_ps = sem("v_ps")
        v_ready = sem("v_ready")
        s_ps = sem("s_ps")
        max_ready = sem("max_ready")
        mT_ps = sem("mT_ps")
        qm_ready = sem("qm_ready")
        st_ps = sem("st_ps")
        p_ready = sem("p_ready")
        av_ps = sem("av_ps")
        o_ready = sem("o_ready")
        oT_ps = sem("oT_ps")
        oT_ready = sem("oT_ready")
        pr_ps = sem("pr_ps")
        res_done = sem("res_done")

        bn_done = sem("bn_done")
        rec_done = sem("rec_done")
        route_in = sem("route_in")
        bn_t_done = sem("bn_t_done")
        stats_t = sem("stats_t")
        root_t = sem("root_t")
        kept = sem("kept")
        xh_ready = sem("xh_ready")
        tT_ps = sem("tT_ps")
        tT_ready = sem("tT_ready")
        logit_ps = sem("logit_ps")
        rank_ps = sem("rank_ps")
        logit_read = sem("logit_read")
        rank_read = sem("rank_read")
        route_step = sem("route_step")
        gap_ready = sem("gap_ready")
        egap_ready = sem("egap_ready")
        hits_ready = sem("hits_ready")
        rows_filled = sem("rows_filled")
        slots_ready = sem("slots_ready")
        place_step = sem("place_step")
        slot_step = sem("slot_step")
        att_done = sem("att_done")
        scattered = [sem(f"scattered{p}") for p in range(2)]
        total_ps = sem("total_ps")
        table_step = sem("table_step")
        tables = sem("tables")
        padded = sem("padded")
        picked_in = [sem(f"picked_in{p}") for p in range(2)]
        expert_in = [sem(f"expert_in{p}") for p in range(2)]
        pT_ps = sem("pT_ps")
        pT_ready = sem("pT_ready")
        h_ps = sem("h_ps")
        h_ready = sem("h_ready")
        y_ps = sem("y_ps")
        y_added = sem("y_added")
        ys_ready = sem("ys_ready")
        ticked = sem("ticked")
        ys_out = [sem(f"ys_out{p}") for p in range(2)]
        got_in = [sem(f"got_in{p}") for p in range(2)]
        summed = sem("summed")
        summing = sem("summing")
        out_done = sem("out_done")

        block = ctx.enter_context(nc.Block())

        def pipeline(eng, step, lags):
            first, last = lags + lags % 2, IMAGES - 2
            for n in range(first):
                step(n, n % 2, n)
            with eng.Fori(first // 2, last // 2) as pair:
                step(pair * 2, 0, None)
                step(pair * 2 + 1, 1, None)
            for n in range(last, IMAGES + lags):
                step(n, n % 2, n)

        def runs(known, lag):
            return known is None or 0 <= known - lag < IMAGES

        def lag_of(block):
            return (2, 5)[block]

        @block.sync
        def _(sp):
            sp.dma_start(gain[:, :], t["gain"]).then_inc(small_in, 16)
            sp.dma_start(shift[:, :], t["shift"]).then_inc(small_in, 16)
            sp.dma_start(b_row[:, :], t["tok_b"]).then_inc(small_in, 16)
            sp.dma_start(w_halo[:, :, :], t["w_halo"]).then_inc(w_in, 16)
            sp.dma_start(w_center[:, :, :, :], t["w_center"]).then_inc(w_in, 16)

            def load(k, p, known):
                if known is None or known >= 2:
                    sp.wait_ge(pix_used, k - 1)
                    sp.wait_ge(emb_ps, k - 1)
                sp.dma_start(pix[:, p, :], t["pix"][k]).then_inc(pix_in[p], 16)
                sp.dma_start(pixT[:, p, :, :], t["pixT"][k]).then_inc(pixT_in[p], 16)

            for name, tile in (("affine", affine), ("gate", w_gate), ("before", before), ("iota", iota),
                               ("region", region), ("dest", dest), ("padding", padding), ("jota", jota)):
                sp.dma_start(tile[:], t[name]).then_inc(route_in, 16)
            for k in range(2):
                load(k, k, k)
            with sp.Fori(1, PAIRS // 2) as pair:
                k = pair * 2
                load(k, 0, None)
                load(k + 1, 1, None)

            def move(k, p, known):
                sp.wait_ge(emb_done, k + 1)
                for half_ in range(2):
                    sp.dma_start(stream[0:PATCHES, 2 * k + half_, :],
                                 raw[half_ * PATCHES:(half_ + 1) * PATCHES, k, :]).then_inc(emb_moved[p], 16)

            for k in range(2):
                move(k, k, k)
            with sp.Fori(1, PAIRS // 2) as pair:
                k = pair * 2
                move(k, 0, None)
                move(k + 1, 1, None)
            sp.wait_ge(tables, 3)
            sp.wait_ge(route_in, 16 * ROUTE_LOADS)
            for e in range(EXPERTS):
                count = sp.value_load(cnt_i[0:1, e:e + 1], min_val=0, max_val=TOKENS)
                sp.dma_start(t["routed"][bass.ds(count + e * REGION, TILE), :], padding[:, :]).then_inc(padded, 16)
            sp.dma_start(t["routed"][EXPERTS * REGION:EXPERTS * REGION + TILE, :], padding[:, :]).then_inc(padded, 16)
            sp.wait_ge(padded, 16 * (EXPERTS + 1))
            for p in range(2):
                sp.wait_ge(scattered[p], 16 * TOP * IMAGES // 2)

            def fetch(j, p, known):
                row = sp.value_load(row_i[0:1, bass.ds(j, 1)], min_val=0, max_val=EXPERTS * REGION)
                expert = sp.value_load(expert_i[0:1, bass.ds(j, 1)], min_val=0, max_val=EXPERTS - 1)
                if known is None or known >= 2:
                    sp.wait_ge(ys_out[p], 8 * (j - p))
                sp.dma_start(picked[:, p, :], t["routed"][bass.ds(row, TILE), :]).then_inc(picked_in[p], 16)
                sp.dma_start(e1[:, p], t["e1"][expert]).then_inc(expert_in[p], 16)
                sp.dma_start(e2[:, p], t["e2"][expert]).then_inc(expert_in[p], 16)
                sp.dma_start(eb[:, p], t["eb"][expert].to_broadcast([TILE, DIM])).then_inc(expert_in[p], 16)

            for j in range(2):
                fetch(j, j, j)
            with sp.Fori(1, TILES // 2) as pair:
                fetch(pair * 2, 0, None)
                fetch(pair * 2 + 1, 1, None)

            for p in range(2):
                sp.wait_ge(ys_out[p], 16 * TILES // 2)
            for c in range(IMAGES // COMBINE):
                if c >= 2:
                    sp.wait_ge(summed, c - 1)
                for k in range(TOP):
                    sp.dma_start(got[:, c % 2, k], t["results"][k * TOKENS:(k + 1) * TOKENS, :]
                                 .rearrange("(b s) d -> s b d", s=SEQ)[:, c * COMBINE:(c + 1) * COMBINE, :])\
                        .then_inc(got_in[c % 2], 16)
            for c in range(IMAGES // COMBINE):
                sp.wait_ge(summed, c + 1)
                sp.dma_start(t["out"][c * COMBINE:(c + 1) * COMBINE].rearrange("b s d -> s b d"),
                             stream[:, c * COMBINE:(c + 1) * COMBINE, :]).then_inc(out_done, 16)
            sp.wait_ge(out_done, 16 * (IMAGES // COMBINE))

        @block.gpsimd
        def _(pool):
            nc.gpsimd.memset(ident[:, :], 0.0).then_inc(ident_zero, 1)
            nc.gpsimd.memset(ones[:, :], 1.0).then_inc(consts, 1)
            nc.gpsimd.memset(half[:, :], -0.5).then_inc(consts, 1)
            nc.gpsimd.memset(tick[:, :], 0.0).then_inc(ticked, 1)
            nc.gpsimd.memset(minus_one[:, :], -1.0).then_inc(consts, 1)
            nc.gpsimd.memset(eps[:, :], EPS).then_inc(consts, 1)
            pool.wait_ge(ident_zero, 1)
            nc.gpsimd.affine_select(out=ident[:, :], in_=ident[:, :], compare_op=ALU.not_equal, fill=1.0,
                                    base=0, pattern=[[-1, 128]], channel_multiplier=1).then_inc(consts, 1)
            nc.gpsimd.memset(k_one[:, :], 0.0).then_inc(mpad_zero, 1)
            nc.gpsimd.memset(mpad[:, :, :, :, :], 0.0).then_inc(mpad_zero, 1)
            nc.gpsimd.memset(v1[:, :, :, HEAD:HEAD + 1], 1.0).then_inc(mpad_zero, 1)
            pool.wait_ge(mpad_zero, 5)
            for r in range(ROWS):
                nc.gpsimd.affine_select(out=k_one[:, :], in_=k_one[:, :], compare_op=ALU.not_equal, fill=1.0,
                                        base=-(SLOT * r + HEAD), pattern=[[0, 1]],
                                        channel_multiplier=1).then_inc(mpad_zero, 1)
                pool.wait_ge(mpad_zero, 6 + r)
            pool.wait_ge(small_in, 48)
            pool.wait_ge(w_in, 32)
            n = SHIFTS * CENTER_CHUNKS
            nc.gpsimd.tensor_tensor(w_fold[:, CENTER_CHUNKS:, :], w_halo[:, :, :],
                                    gain[:, n:n + 2].unsqueeze(2).to_broadcast([KC, 2, DIM]), ALU.mult)\
                .then_inc(scaled_pool, 1)
            for s in (3, 4):
                nc.gpsimd.tensor_tensor(w_scaled[:, s], w_center[:, s],
                                        gain[:, s * CENTER_CHUNKS:(s + 1) * CENTER_CHUNKS].unsqueeze(2)
                                        .to_broadcast([KC, CENTER_CHUNKS, DIM]), ALU.mult).then_inc(scaled_pool, 1)
            pool.wait_ge(scaled_pool, 3)
            nc.gpsimd.tensor_tensor(w_scaled[:, 3], w_scaled[:, 3], w_scaled[:, 4], ALU.add).then_inc(scaled_pool, 1)
            pool.wait_ge(var_ready, 1)
            nc.gpsimd.tensor_tensor(stat[:, 7, :], stat[:, 6, :], half[0:PAIR, :], ALU.pow).then_inc(rstd_ready, 1)

            nc.gpsimd.memset(seen[:, :, :], 0.0).then_inc(consts, 1)
            pool_incs = [0]
            tt = nc.gpsimd.tensor_tensor

            def norm(block, i, p, known):
                base = block * IMAGES
                per = (3, 8)[block]
                at = pool_incs[0] + i * per
                steps = 0

                def then(instruction):
                    nonlocal steps
                    steps += 1
                    instruction.then_inc(pool_step, 1)
                    pool.wait_ge(pool_step, at + steps)

                if known is None or known + base >= 2:
                    pool.wait_ge(xn_ready, i + base - 1)
                pool.wait_ge(stats_ready, i + base + 1)
                then(tt(veps[:, p], mv_x[:, p, 1:2], eps[0:SEQ, :], ALU.add))
                then(tt(rstd[:, p], veps[:, p], half[0:SEQ, 0:1], ALU.pow))
                then(tt(veps[:, p], mv_x[:, p, 0:1], rstd[:, p], ALU.mult))
                last = tt(nmr[:, p], veps[:, p], minus_one[0:SEQ, :], ALU.mult)
                if block:
                    then(last)
                    then(tt(veps[:, p], mv_x[:, p, 1:2], rstd[:, p], ALU.mult))
                    then(tt(veps[:, p], veps[:, p], rstd[:, p], ALU.mult))
                    then(tt(veps[:, p], veps[:, p], eps[0:SEQ, :], ALU.add))
                    then(tt(rstd2[:, p], veps[:, p], half[0:SEQ, 0:1], ALU.pow))
                    tt(scale2[:, p], rstd[:, p], rstd2[:, p], ALU.mult)
                    last = tt(nmr2[:, p], nmr[:, p], rstd2[:, p], ALU.mult)
                last.then_inc(norm_ready, 1)

            for i in range(2):
                norm(0, i, i, i)
            with pool.Fori(1, IMAGES // 2) as pair:
                norm(0, pair * 2, 0, None)
                norm(0, pair * 2 + 1, 1, None)
            pool_incs[0] += 3 * IMAGES

            def root(i, p):
                pool.wait_ge(stats_t, i + 1)
                tt(veps_t[:, p], mv_t[:, p, 1:2], eps[0:SEQ, :], ALU.add).then_inc(root_t, 1)
                pool.wait_ge(root_t, 4 * i + 1)
                tt(rstd_s[:, p], veps_t[:, p], half[0:SEQ, 0:1], ALU.pow).then_inc(root_t, 1)
                pool.wait_ge(root_t, 4 * i + 2)
                tt(mr_s[:, p], mv_t[:, p, 0:1], rstd_s[:, p], ALU.mult).then_inc(root_t, 1)
                pool.wait_ge(root_t, 4 * i + 3)

            def keep(i, p):
                tt(nmr_t[:, i], mr_s[:, p], minus_one[0:SEQ, :], ALU.mult)
                tt(rstd_t[:, i], rstd_s[:, p], ones[0:SEQ, 0:1], ALU.mult).then_inc(kept, 1)
                tt(stream[:, i, :], stream[:, i, :], inner[:, i, :], ALU.add).then_inc(res_done, 1)

            norm(1, 0, 0, 0)

            def step(n, p, known):
                if runs(known, -1):
                    norm(1, n + 1, 1 - p, None if known is None else known + 1)
                if runs(known, 2):
                    root(n - 2, p)
                if runs(known, 5):
                    pool.wait_ge(slots_ready, n - 4)
                    pool.wait_ge(rows_filled, n - 4)
                if runs(known, 2):
                    tt(nmr_s[:, p], mr_s[:, p], minus_one[0:SEQ, :], ALU.mult).then_inc(root_t, 1)
                    keep(n - 2, p)
                if runs(known, 5):
                    for k in range(TOP):
                        nc.gpsimd.indirect_dma_start(
                            out=t["routed"], out_offset=bass.IndirectOffsetOnAxis(ap=slot[:, 1 - p, k:k + 1], axis=0),
                            in_=rows[:, 1 - p, k, :], in_offset=None).then_inc(scattered[1 - p], 16)

            pipeline(pool, step, 5)

            def send(j, p):
                pool.wait_ge(ys_ready, j + 1)
                pool.wait_ge(ticked, j + 1)
                tt(tick[:, :], minus_one[0:1, :], eps[0:1, :], ALU.mult).then_inc(ticked, 1)
                nc.gpsimd.indirect_dma_start(
                    out=t["results"],
                    out_offset=bass.IndirectOffsetOnAxis(ap=picked[:, p, DIM + 1:DIM + 2].bitcast(U32), axis=0),
                    in_=ys[:, p, :], in_offset=None, bounds_check=TOP * TOKENS - 1, oob_is_err=False)\
                    .then_inc(ys_out[p], 16)

            with pool.Fori(0, TILES // 2) as pair:
                send(pair * 2, 0)
                send(pair * 2 + 1, 1)

        @block.scalar
        def _(act):
            act.dma_start(stream[PATCHES:SEQ, :, :], t["txt"]).then_inc(text_in, 16)
            for b in range(BLOCKS):
                act.dma_start(w_qk[:, b], t["qk"][b]).then_inc(attn_in, 16)
                act.dma_start(w_v[:, b], t["v"][b]).then_inc(attn_in, 16)
                act.dma_start(w_p[:, b], t["p"][b]).then_inc(attn_in, 16)
            act.wait_ge(bias_ps, 1)
            nc.scalar.copy(bias_row[:, :], ps_o[0:1, 0:DIM]).then_inc(bias_out, 1)
            act.wait_ge(sums_ps, 1)
            nc.scalar.copy(colsum[:, :], ps_v[0:PAIR, 0:DIM]).then_inc(sums_out, 1)
            nc.scalar.copy(bias_all[:, :], ps_v[0:PAIR, DIM:2 * DIM]).then_inc(sums_out, 1)

            def stage(k, p):
                act.wait_ge(emb_ps, k + 1)
                nc.scalar.copy(raw[:, k, :], (ps_q, ps_a)[p][0:PAIR, 0:DIM]).then_inc(emb_raw, 1)

            with act.Fori(0, PAIRS // 2) as pair:
                k = pair * 2
                stage(k, 0)
                stage(k + 1, 1)
            act.wait_ge(mpad_zero, 9)

            def normalize(block, i, p):
                act.wait_ge(norm_ready, i + block * IMAGES + 1)
                if block == 0:
                    nc.scalar.activation(xn[:, p], stream[:, i, :], ACT.Identity,
                                         bias=nmr[:, p], scale=rstd[:, p]).then_inc(xn_ready, 1)
                    return
                nc.scalar.activation(inner[:, i, :], stream[:, i, :], ACT.Identity,
                                     bias=nmr[:, p], scale=rstd[:, p])
                nc.scalar.activation(xn[:, p], stream[:, i, :], ACT.Identity,
                                     bias=nmr2[:, p], scale=scale2[:, p]).then_inc(xn_ready, 1)

            def step(block, n, p, known):
                base = block * IMAGES
                if runs(known, 0):
                    act.wait_ge(aT_ps, n + base + 1)
                    src = ps_a[0:KC, 0:CHUNKS * SEQ].rearrange("k (c s) -> k c s", c=CHUNKS)
                    if block == 0:
                        nc.scalar.copy(aT[:, p], src).then_inc(aT_ready, 1)
                    else:
                        for c in range(CHUNKS):
                            last = nc.scalar.activation(aT[:, p, c], src[:, c], ACT.Identity,
                                                        bias=affine[:, 0, 1, c:c + 1], scale=affine[:, 0, 0, c:c + 1])
                        last.then_inc(aT_ready, 1)
                if runs(known, 1):
                    act.wait_ge(st_ps, n + base)
                    nc.scalar.activation(probs[:, 1 - p], ps_s[0:SEQ, :, 0:GROUPS * SEQ]
                                         .rearrange("k r (g q) -> k r g q", g=GROUPS),
                                         ACT.Exp, scale=HEAD ** -0.5).then_inc(p_ready, 1)
                if runs(known, 2):
                    act.wait_ge(oT_ps, n + base - 1)
                    nc.scalar.copy(oT[0:KC], ps_o[0:KC, 0:CHUNKS * SEQ].rearrange("k (c s) -> k c s", c=CHUNKS))\
                        .then_inc(oT_ready, 1)
                if block and runs(known, 4):
                    act.wait_ge(gap_ready, n - 3)
                    nc.scalar.activation(egap[:, p], gap[:, p], ACT.Exp).then_inc(egap_ready, 1)
                if runs(known, 0):
                    act.wait_ge(qk_ps, n + base + 1)
                    nc.scalar.activation(qk[:, p], ps_q[:, 0:2 * GROUPS * SEQ]
                                         .rearrange("k (a g s) -> k a g s", a=2, g=GROUPS),
                                         ACT.Identity, bias=k_one[:, :]).then_inc(qk_ready, 1)
                if runs(known, -1):
                    normalize(block, n + 1, 1 - p)
                if block and runs(known, 3):
                    act.wait_ge(tT_ps, n - 2)
                    src = ps_a[0:KC, 0:CHUNKS * SEQ].rearrange("k (c s) -> k c s", c=CHUNKS)
                    for c in range(CHUNKS):
                        last = nc.scalar.activation(tT[0:KC, c], src[:, c], ACT.Identity,
                                                    bias=affine[:, 1, 1, c:c + 1], scale=affine[:, 1, 0, c:c + 1])
                    last.then_inc(tT_ready, 1)
                if block and runs(known, 4):
                    i = n - 4
                    if known is None or known >= 6:
                        act.wait_ge(scattered[p], 16 * (i - p))
                    act.wait_ge(kept, i + 1)
                    for k in range(TOP):
                        last = nc.scalar.activation(rows[:, p, k, 0:DIM], inner[:, i, :], ACT.Identity,
                                                    bias=nmr_t[:, i], scale=rstd_t[:, i])
                    last.then_inc(rows_filled, 1)
                if block and runs(known, 2):
                    i = n - 2
                    act.wait_ge(root_t, 4 * i + 4)
                    nc.scalar.activation(xh[:, p], inner[:, i, :], ACT.Identity,
                                         bias=nmr_s[:, p], scale=rstd_s[:, p]).then_inc(xh_ready, 1)

            act.wait_ge(route_in, 16 * ROUTE_LOADS)
            for b in range(BLOCKS):
                normalize(b, 0, 0)
                pipeline(act, lambda n, p, known: step(b, n, p, known), lag_of(b))

            def expert(j, p):
                act.wait_ge(pT_ps, j + 1)
                for c in range(CHUNKS):
                    last = nc.scalar.activation(pT[0:KC, p, c], ps_a[0:KC, c * TILE:(c + 1) * TILE], ACT.Identity,
                                                bias=affine[:, 1, 1, c:c + 1], scale=affine[:, 1, 0, c:c + 1])
                last.then_inc(pT_ready, 1)
                act.wait_ge(h_ps, j + 1)
                nc.scalar.activation(hid[:, p], ps_s[:, 2 * p:2 * p + 2, :].rearrange("h a n -> h (a n)")
                                     [:, 0:HIDDEN].rearrange("h (c n) -> h c n", c=HIDDEN_CHUNKS),
                                     ACT.Gelu).then_inc(h_ready, 1)

            with act.Fori(0, TILES // 2) as pair:
                expert(pair * 2, 0)
                expert(pair * 2 + 1, 1)

        @block.vector
        def _(dve):
            steps = [0]

            def then(instruction):
                instruction.then_inc(dve_step, 1)
                steps[0] += 1
                dve.wait_ge(dve_step, steps[0])

            nc.vector.memset(oT[KC:KC + 1, :, :], 1.0).then_inc(mpad_zero, 1)
            nc.vector.memset(tT[KC:KC + 1, :, :], 1.0).then_inc(mpad_zero, 1)
            dve.wait_ge(small_in, 48)
            dve.wait_ge(w_in, 32)
            for s in range(3):
                then(nc.vector.tensor_tensor(w_scaled[:, s], w_center[:, s],
                                             gain[:, s * CENTER_CHUNKS:(s + 1) * CENTER_CHUNKS].unsqueeze(2)
                                             .to_broadcast([KC, CENTER_CHUNKS, DIM]), ALU.mult))
                if s:
                    then(nc.vector.tensor_tensor(w_scaled[:, 0], w_scaled[:, 0], w_scaled[:, s], ALU.add))
            dve.wait_ge(scaled_pool, 4)
            nc.vector.tensor_tensor(w_fold[:, 0:CENTER_CHUNKS], w_scaled[:, 0], w_scaled[:, 3], ALU.add)\
                .then_inc(folded, 1)

            def statistics(k, p, base, known):
                dve.wait_ge(pix_in[p], 8 * (k - p) + 16)
                tile = pix[:, p, :]
                own = tile[:, 0:CENTER].rearrange("t (r c) -> t r c", r=PATCH)
                for h in range(2):
                    nc.vector.bn_stats(bn_c[:, p, h * BN:(h + 1) * BN], tile[:, h * CENTER // 2:(h + 1) * CENTER // 2])\
                        .then_inc(dve_step, 1)
                nc.vector.bn_stats(bn_h[:, p, :], tile[:, CENTER:FEATURES]).then_inc(dve_step, 1)
                nc.vector.bn_stats(bn_e[:, p, 0:BN], own[:, 0:PATCH:PATCH - 1, :]).then_inc(dve_step, 1)
                nc.vector.bn_stats(bn_e[:, p, BN:2 * BN], own.rearrange("t r (w c) -> t r w c", c=CHANNELS)
                                   [:, :, 0:PATCH:PATCH - 1, :]).then_inc(pix_used, 1)
                dve.wait_ge(dve_step, base + 4)
                dve.wait_ge(pix_used, k + 1)
                if known is None or known >= 1:
                    nc.vector.tensor_copy(mv[:, k - 1], mv_k[:, 1 - p]).then_inc(dve_step, 1)
                nc.vector.bn_aggr(mv_k[:, p, 0], bn_c[:, p, :]).then_inc(dve_step, 1)
                nc.vector.bn_aggr(mv_k[:, p, 1], bn_h[:, p, :]).then_inc(dve_step, 1)
                nc.vector.bn_aggr(mv_k[:, p, 2], bn_e[:, p, :]).then_inc(dve_step, 1)

            base = steps[0]
            for k in range(2):
                statistics(k, k, max(8 * k - 1, 0) + base, k)
            with dve.Fori(1, PAIRS // 2) as pair:
                k = pair * 2
                statistics(k, 0, k * 8 + (base - 1), None)
                statistics(k + 1, 1, k * 8 + (base + 7), None)
            steps[0] += 8 * PAIRS - 1
            dve.wait_ge(dve_step, steps[0])
            then(nc.vector.tensor_copy(mv[:, PAIRS - 1], mv_k[:, 1]))
            m_c, v_c = mv[:, :, 0, 0], mv[:, :, 0, 1]
            m_h, v_h = mv[:, :, 1, 0], mv[:, :, 1, 1]
            m_e, v_e = mv[:, :, 2, 0], mv[:, :, 2, 1]
            d_h, d_e, d, nmean, var = (stat[:, j, :] for j in range(5))
            share = HALO / COPIED
            then(nc.vector.tensor_tensor(d_h, m_h, m_c, ALU.subtract))
            then(nc.vector.tensor_tensor(d_e, m_e, m_c, ALU.subtract))
            then(nc.vector.tensor_tensor(d, m_h, m_e, ALU.subtract))
            then(nc.vector.scalar_tensor_tensor(out=nmean, in0=d, scalar=-share, in1=m_c,
                                                op0=ALU.mult, op1=ALU.subtract))
            then(nc.vector.tensor_tensor(d_h, d_h, d_h, ALU.mult))
            then(nc.vector.tensor_tensor(d_e, d_e, d_e, ALU.mult))
            then(nc.vector.tensor_tensor(d_h, d_h, v_h, ALU.add))
            then(nc.vector.tensor_tensor(d_e, d_e, v_e, ALU.add))
            then(nc.vector.tensor_tensor(d_h, d_h, d_e, ALU.subtract))
            then(nc.vector.scalar_tensor_tensor(out=var, in0=d_h, scalar=share, in1=v_c, op0=ALU.mult, op1=ALU.add))
            then(nc.vector.tensor_scalar(d, d, share, None, ALU.mult))
            then(nc.vector.tensor_tensor(d, d, d, ALU.mult))
            then(nc.vector.tensor_tensor(var, var, d, ALU.subtract))
            nc.vector.tensor_scalar(stat[:, 6, :], var, 1e-3, None, ALU.add).then_inc(var_ready, 1)
            dve.wait_ge(rstd_ready, 1)
            dve.wait_ge(sums_out, 2)

            def finish(k):
                dve.wait_ge(emb_raw, k + 1)
                nc.vector.scalar_tensor_tensor(out=raw[:, k, :], in0=colsum[:, :], scalar=stat[:, 3:4, k],
                                               in1=raw[:, k, :], op0=ALU.mult, op1=ALU.add).then_inc(dve_step, 1)
                dve.wait_ge(dve_step, k + 1 + steps[0])
                nc.vector.scalar_tensor_tensor(out=raw[:, k, :], in0=raw[:, k, :], scalar=stat[:, 7:8, k],
                                               in1=bias_all[:, :], op0=ALU.mult, op1=ALU.add).then_inc(emb_done, 1)

            with dve.Fori(0, PAIRS // 2) as pair:
                k = pair * 2
                finish(k)
                finish(k + 1)
            steps[0] += PAIRS

            def experts(i, p):
                base = 4 * i
                nc.vector.max(best[:, p], logit[:, p]).then_inc(route_step, 1)
                dve.wait_ge(route_step, base + 1)
                nc.vector.tensor_tensor(gap[:, p], best[:, p, 1:2], best[:, p, 0:1], ALU.subtract).then_inc(gap_ready, 1)
                nc.vector.max_index(best_at[:, p], best[:, p], logit[:, p]).then_inc(route_step, 1)
                dve.wait_ge(route_step, base + 2)
                nc.vector.tensor_copy(chosen[:, p], best_at[:, p, 0:TOP]).then_inc(route_step, 1)
                dve.wait_ge(route_step, base + 3)
                nc.vector.tensor_tensor(mask[:, p], iota[:, :, :], chosen[:, p].unsqueeze(2)
                                        .to_broadcast([SEQ, TOP, EXPERTS]), ALU.is_equal).then_inc(route_step, 1)
                dve.wait_ge(route_step, base + 4)
                nc.vector.tensor_tensor(hits[:, p], mask[:, p, 0], mask[:, p, 1], ALU.add).then_inc(hits_ready, 1)

            def place_rows(i, p, known):
                dve.wait_ge(rank_read, 2 * i + 2)
                nc.vector.tensor_tensor(placed[:, p], mask[:, p], place[:, p].unsqueeze(1)
                                        .to_broadcast([SEQ, TOP, EXPERTS]), ALU.mult).then_inc(place_step, 1)
                dve.wait_ge(egap_ready, i + 1)
                nc.vector.tensor_scalar(esum[:, p], egap[:, p], 1.0, None, ALU.add).then_inc(place_step, 1)
                dve.wait_ge(place_step, 4 * i + 1)
                nc.vector.tensor_reduce(slot_f[:, p], placed[:, p], AX.X, ALU.add).then_inc(place_step, 1)
                if known is None or known >= 2:
                    dve.wait_ge(scattered[p], 16 * (i - p))
                dve.wait_ge(place_step, 4 * i + 2)
                nc.vector.reciprocal(rows[:, p, 0, DIM:DIM + 1], esum[:, p]).then_inc(place_step, 1)
                dve.wait_ge(place_step, 4 * i + 4)
                nc.vector.tensor_tensor(rows[:, p, 1, DIM:DIM + 1], rows[:, p, 0, DIM:DIM + 1], egap[:, p], ALU.mult)\
                    .then_inc(slot_step, 1)
                nc.vector.tensor_copy(rows[:, p, :, DIM + 1].bitcast(U32), dest[:, :]).then_inc(slot_step, 1)
                nc.vector.tensor_copy(slot[:, p], slot_f[:, p]).then_inc(slot_step, 1)
                dve.wait_ge(slot_step, 3 * i + 3)
                nc.vector.tensor_scalar(dest[:, :], dest[:, :], float(SEQ), None, ALU.add).then_inc(slots_ready, 1)

            nc.vector.memset(pT[KC:KC + 1, :, :, :], 1.0).then_inc(consts, 1)
            dve.wait_ge(emb_moved[0], 16 * PAIRS)
            dve.wait_ge(emb_moved[1], 16 * PAIRS)
            dve.wait_ge(text_in, 16)
            dve.wait_ge(mpad_zero, 9)
            dve.wait_ge(consts, CONSTS)
            dve.wait_ge(route_in, 16 * ROUTE_LOADS)

            def step(block, n, p, known):
                base = block * IMAGES
                if runs(known, 0):
                    dve.wait_ge(v_ps, n + base + 1)
                    nc.vector.tensor_copy(v1[:, p, :, 0:HEAD], ps_v[0:SEQ, 0:DIM].rearrange("s (h d) -> s h d", h=HEADS))\
                        .then_inc(v_ready, 1)
                if runs(known, -1) and (known is None or known + base >= 1):
                    dve.wait_ge(norm_ready, n + base)
                if runs(known, 2):
                    dve.wait_ge(pr_ps, n + base - 1)
                    to = (stream, inner)[block][:, n - 2, :]
                    nc.vector.tensor_tensor(to, to, ps_o[0:SEQ, 0:DIM], ALU.add).then_inc(att_done, 1)
                if runs(known, -1):
                    nc.vector.bn_stats(bn_x[:, 1 - p, :], stream[:, n + 1, :]).then_inc(bn_done, 1)
                    dve.wait_ge(bn_done, n + base + 2)
                if block and runs(known, 2):
                    dve.wait_ge(att_done, n + base - 1)
                if runs(known, 0):
                    dve.wait_ge(s_ps, n + base + 1)
                    nc.vector.tensor_reduce(mpad[:, p, :, :, HEAD].rearrange("q g r -> q r g"),
                                            ps_s[0:SEQ, :, 0:GROUPS * SEQ].rearrange("q r (g k) -> q r g k", g=GROUPS),
                                            AX.X, ALU.max, negate=True).then_inc(max_ready, 1)
                if runs(known, -1):
                    nc.vector.bn_aggr(mv_x[:, 1 - p, :], bn_x[:, 1 - p, :]).then_inc(stats_ready, 1)
                if block and runs(known, 2):
                    i = n - 2
                    nc.vector.bn_stats(bn_t[:, p, :], inner[:, i, :]).then_inc(bn_t_done, 1)
                    dve.wait_ge(bn_t_done, i + 1)
                    if known is None or known >= 4:
                        dve.wait_ge(kept, i - 1)
                if runs(known, 0):
                    dve.wait_ge(mT_ps, n + base + 1)
                    nc.vector.tensor_tensor(qm[:, p], ps_v[:, 0:GROUPS * SEQ].rearrange("k (g s) -> k g s", g=GROUPS),
                                            qk[:, p, 0], ALU.add).then_inc(qm_ready, 1)
                if block and runs(known, 2):
                    nc.vector.bn_aggr(mv_t[:, p, :], bn_t[:, p, :]).then_inc(stats_t, 1)
                if runs(known, 1):
                    dve.wait_ge(av_ps, n + base)
                    av = ps_q[0:SEQ, 0:HEADS * (HEAD + 1)].rearrange("s (h d) -> s h d", h=HEADS)
                    nc.vector.reciprocal(rec[:, 1 - p], av[:, :, HEAD:HEAD + 1]).then_inc(rec_done, 1)
                    dve.wait_ge(rec_done, n + base)
                    nc.vector.tensor_tensor(o[:, 1 - p], av[:, :, 0:HEAD],
                                            rec[:, 1 - p].to_broadcast([SEQ, HEADS, HEAD]), ALU.mult)\
                        .then_inc(o_ready, 1)
                if block and runs(known, 4):
                    dve.wait_ge(rank_ps, n - 3)
                if block and runs(known, 3):
                    dve.wait_ge(logit_ps, n - 2)
                    nc.vector.tensor_copy(logit[:, 1 - p], ps_a[0:SEQ, LOGIT_AT:LOGIT_AT + EXPERTS])\
                        .then_inc(logit_read, 1)
                if block and runs(known, 4):
                    nc.vector.tensor_tensor(place[:, p], ps_a[0:SEQ, RANK_AT:RANK_AT + EXPERTS], region[:, :], ALU.add)\
                        .then_inc(rank_read, 1)
                if block and runs(known, 3):
                    dve.wait_ge(logit_read, n - 2)
                if block and runs(known, 4):
                    nc.vector.tensor_tensor(seen[:, 1 - p], seen[:, p], hits[:, p], ALU.add).then_inc(rank_read, 1)
                if block and runs(known, 3):
                    experts(n - 3, 1 - p)
                if block and runs(known, 4):
                    place_rows(n - 4, p, None if known is None else known - 4)

            for b in range(BLOCKS):
                base = b * IMAGES
                if b:
                    dve.wait_ge(att_done, base)
                    dve.wait_ge(norm_ready, base)
                nc.vector.bn_stats(bn_x[:, 0, :], stream[:, 0, :]).then_inc(bn_done, 1)
                dve.wait_ge(bn_done, base + 1)
                nc.vector.bn_aggr(mv_x[:, 0, :], bn_x[:, 0, :]).then_inc(stats_ready, 1)
                pipeline(dve, lambda n, p, known: step(b, n, p, known), lag_of(b))

            count = [0]

            def then(instruction):
                count[0] += 1
                instruction.then_inc(table_step, 1)
                dve.wait_ge(table_step, count[0])

            dve.wait_ge(total_ps, 1)
            then(nc.vector.tensor_copy(cnt[:, :], ps_v[0:1, 0:EXPERTS]))
            nc.vector.tensor_copy(cnt_i[:, :], cnt[:, :]).then_inc(tables, 1)
            then(nc.vector.tensor_scalar(need[:, :], cnt[:, :], float(TILE - 1), None, ALU.add))
            then(nc.vector.tensor_copy(need_i[:, :], need[:, :]))
            then(nc.vector.tensor_scalar(need_i[:, :], need_i[:, :], 7, None, ALU.arith_shift_right))
            then(nc.vector.tensor_copy(need[:, :], need_i[:, :]))
            a, b = 0, 1
            then(nc.vector.tensor_copy(upto[:, a], need[:, :]))
            for d in (1, 2, 4):
                then(nc.vector.tensor_copy(upto[:, b, 0:d], upto[:, a, 0:d]))
                then(nc.vector.tensor_tensor(upto[:, b, d:], upto[:, a, d:], upto[:, a, 0:EXPERTS - d], ALU.add))
                a, b = b, a
            wide = [1, TILES, EXPERTS]
            then(nc.vector.tensor_tensor(past[:, :, :], upto[:, a].unsqueeze(1).to_broadcast(wide),
                                         jota[:, :].unsqueeze(2).to_broadcast(wide), ALU.is_le))
            then(nc.vector.tensor_reduce(tile_e[:, :], past[:, :, :], AX.X, ALU.add))
            then(nc.vector.tensor_tensor(past[:, :, :], past[:, :, :], need[:, :].unsqueeze(1).to_broadcast(wide),
                                         ALU.mult))
            then(nc.vector.tensor_reduce(tile_s[:, :], past[:, :, :], AX.X, ALU.add))
            then(nc.vector.tensor_tensor(tile_l[:, :], jota[:, :], tile_s[:, :], ALU.subtract))
            then(nc.vector.tensor_scalar(tile_s[:, :], tile_e[:, :], float(EXPERTS), float(TILE), ALU.is_lt, ALU.mult))
            then(nc.vector.tensor_tensor(tile_l[:, :], tile_l[:, :], tile_s[:, :], ALU.mult))
            then(nc.vector.tensor_scalar(tile_s[:, :], tile_e[:, :], float(REGION), None, ALU.mult))
            then(nc.vector.tensor_tensor(tile_l[:, :], tile_l[:, :], tile_s[:, :], ALU.add))
            nc.vector.tensor_copy(row_i[:, :], tile_l[:, :]).then_inc(tables, 1)
            then(nc.vector.tensor_scalar(tile_e[:, :], tile_e[:, :], float(EXPERTS - 1), None, ALU.min))
            nc.vector.tensor_copy(expert_i[:, :], tile_e[:, :]).then_inc(tables, 1)

            def scale(j, p, known):
                dve.wait_ge(y_ps, j + 1)
                dve.wait_ge(expert_in[p], 24 * (j - p) + 48)
                dve.wait_ge(picked_in[p], 8 * (j - p) + 16)
                nc.vector.tensor_tensor(y[:, p], (ps_q, ps_o)[p][:, 0:DIM], eb[:, p], ALU.add).then_inc(y_added, 1)
                dve.wait_ge(y_added, j + 1)
                if known is None or known >= 2:
                    dve.wait_ge(ys_out[p], 8 * (j - p))
                nc.vector.tensor_scalar(ys[:, p], y[:, p], picked[:, p, DIM:DIM + 1], None, ALU.mult)\
                    .then_inc(ys_ready, 1)

            for j in range(2):
                scale(j, j, j)
            with dve.Fori(1, TILES // 2) as pair:
                scale(pair * 2, 0, None)
                scale(pair * 2 + 1, 1, None)

            dve.wait_ge(res_done, IMAGES)
            for c in range(IMAGES // COMBINE):
                dve.wait_ge(got_in[c % 2], 32 * (c // 2 + 1))
                to = stream[:, c * COMBINE:(c + 1) * COMBINE, :]
                nc.vector.tensor_tensor(to, to, got[:, c % 2, 0], ALU.add).then_inc(summing, 1)
                dve.wait_ge(summing, c + 1)
                nc.vector.tensor_tensor(to, to, got[:, c % 2, 1], ALU.add).then_inc(summed, 1)

        @block.tensor
        def _(pe):
            pe.wait_ge(small_in, 48)
            pe.wait_ge(w_in, 32)
            pe.wait_ge(consts, 5)
            row = ps_o[0:1, 0:DIM]
            for s in range(SHIFTS):
                for c in range(CENTER_CHUNKS):
                    j = s * CENTER_CHUNKS + c
                    pe.matmul(row, shift[:, j:j + 1], w_center[:, s, c, :], start=(j == 0), stop=False)
            for c in range(2):
                j = SHIFTS * CENTER_CHUNKS + c
                pe.matmul(row, shift[:, j:j + 1], w_halo[:, c, :], start=False, stop=False)
            pe.matmul(row, ones[0:1, 0:1], b_row[:, :], start=False, stop=True).then_inc(bias_ps, 1)
            pe.wait_ge(folded, 1)
            for c in range(FEATURE_CHUNKS):
                pe.matmul(ps_v[0:PAIR, 0:DIM], ones[0:KC, 0:PAIR], w_fold[:, c, :],
                          start=(c == 0), stop=(c == FEATURE_CHUNKS - 1))
            pe.wait_ge(bias_out, 1)
            pe.matmul(ps_v[0:PAIR, DIM:2 * DIM], ones[0:1, 0:PAIR], bias_row[:, :], start=True, stop=True)\
                .then_inc(sums_ps, 1)

            def embed(k, p, known):
                pe.wait_ge(pixT_in[p], 8 * (k - p) + 16)
                if known is None or known >= 2:
                    pe.wait_ge(emb_raw, k - 1)
                for c in range(FEATURE_CHUNKS):
                    last = pe.matmul((ps_q, ps_a)[p][0:PAIR, 0:DIM], pixT[:, p, c, :], w_fold[:, c, :],
                                     start=(c == 0), stop=(c == FEATURE_CHUNKS - 1))
                last.then_inc(emb_ps, 1)

            for k in range(2):
                embed(k, k, k)
            with pe.Fori(1, PAIRS // 2) as pair:
                k = pair * 2
                embed(k, 0, None)
                embed(k + 1, 1, None)
            pe.wait_ge(attn_in, 16 * 3 * BLOCKS)
            pe.wait_ge(emb_raw, PAIRS)
            pe.wait_ge(sums_out, 2)
            pe.wait_ge(mpad_zero, 9)

            def heads():
                for g in range(GROUPS):
                    for r in range(ROWS):
                        yield g, r

            def step(block, n, p, known):
                base = block * IMAGES
                q = 1 - p
                if runs(known, 0):
                    pe.wait_ge(xn_ready, n + base + 1)
                    if known is None or known + base >= 1:
                        pe.wait_ge(aT_ready, n + base)
                    if block and (known is None or known >= 4):
                        pe.wait_ge(logit_read, n - 3)
                    if block and (known is None or known >= 5):
                        pe.wait_ge(rank_read, 2 * (n - 4))
                    for c in range(CHUNKS):
                        last = pe.transpose(ps_a[0:KC, c * SEQ:(c + 1) * SEQ], xn[:, p, c * KC:(c + 1) * KC],
                                            ident[0:SEQ, 0:SEQ])
                    last.then_inc(aT_ps, 1)
                if runs(known, 1):
                    pe.wait_ge(qm_ready, n + base)
                    for g, r in heads():
                        last = pe.matmul(ps_s[0:SEQ, r, g * SEQ:(g + 1) * SEQ],
                                         qk[SLOT * r:SLOT * (r + 1), q, 1, g, :],
                                         qm[SLOT * r:SLOT * (r + 1), q, g, :], start=True, stop=True)
                    last.then_inc(st_ps, 1)
                if runs(known, 2):
                    pe.wait_ge(o_ready, n + base - 1)
                    if known is None or known + base >= 3:
                        pe.wait_ge(att_done, n + base - 2)
                    for c in range(CHUNKS):
                        last = pe.transpose(ps_o[0:KC, c * SEQ:(c + 1) * SEQ],
                                            o[:, p].rearrange("s h d -> s (h d)")[:, c * KC:(c + 1) * KC],
                                            ident[0:SEQ, 0:SEQ])
                    last.then_inc(oT_ps, 1)
                if runs(known, 0):
                    pe.wait_ge(aT_ready, n + base + 1)
                    if known is None or known + base >= 2:
                        pe.wait_ge(o_ready, n + base - 1)
                    for a in range(2):
                        for g in range(GROUPS):
                            for c in range(CHUNKS):
                                last = pe.matmul(ps_q[:, (a * GROUPS + g) * SEQ:(a * GROUPS + g + 1) * SEQ],
                                                 w_qk[:, block, c, a, g, :], aT[:, p, c, :],
                                                 start=(c == 0), stop=(c == CHUNKS - 1))
                    last.then_inc(qk_ps, 1)
                    if known is None or known + base >= 1:
                        pe.wait_ge(qm_ready, n + base)
                    for c in range(CHUNKS):
                        last = pe.matmul(ps_v[0:SEQ, 0:DIM], aT[:, p, c, :], w_v[:, block, c, :],
                                         start=(c == 0), stop=(c == CHUNKS - 1))
                    last.then_inc(v_ps, 1)
                if runs(known, 2):
                    pe.wait_ge(oT_ready, n + base - 1)
                    for c in range(CHUNKS):
                        k = KC + 1 - c
                        last = pe.matmul(ps_o[0:SEQ, 0:DIM], oT[0:k, c, :], w_p[0:k, block, c, :],
                                         start=(c == 0), stop=(c == CHUNKS - 1))
                    last.then_inc(pr_ps, 1)
                if runs(known, 0):
                    pe.wait_ge(qk_ready, n + base + 1)
                    if known is None or known + base >= 1:
                        pe.wait_ge(p_ready, n + base)
                    for g, r in heads():
                        last = pe.matmul(ps_s[0:SEQ, r, g * SEQ:(g + 1) * SEQ],
                                         qk[SLOT * r:SLOT * (r + 1), p, 0, g, :],
                                         qk[SLOT * r:SLOT * (r + 1), p, 1, g, :], start=True, stop=True)
                    last.then_inc(s_ps, 1)
                if block and runs(known, 3):
                    pe.wait_ge(xh_ready, n - 2)
                    if known is not None and known >= IMAGES:
                        if known - 4 < IMAGES:
                            pe.wait_ge(logit_read, n - 3)
                        if known - 5 < IMAGES:
                            pe.wait_ge(rank_read, 2 * (n - 4))
                    for c in range(CHUNKS):
                        last = pe.transpose(ps_a[0:KC, c * SEQ:(c + 1) * SEQ], xh[:, q, c * KC:(c + 1) * KC],
                                            ident[0:SEQ, 0:SEQ])
                    last.then_inc(tT_ps, 1)
                for j, (g, r) in enumerate(heads()):
                    if j == 8 and runs(known, 0):
                        pe.wait_ge(max_ready, n + base + 1)
                        pe.wait_ge(v_ready, n + base + 1)
                        for gg in range(GROUPS):
                            last = pe.transpose(ps_v[:, gg * SEQ:(gg + 1) * SEQ],
                                                mpad[:, p, gg].rearrange("q r d -> q (r d)"), ident[0:SEQ, 0:SEQ])
                        last.then_inc(mT_ps, 1)
                    if not runs(known, 1):
                        continue
                    if j == 0:
                        pe.wait_ge(p_ready, n + base)
                        pe.wait_ge(v_ready, n + base)
                        if known is not None and known >= IMAGES:
                            pe.wait_ge(qk_ready, base + IMAGES)
                    h = ROWS * g + r
                    last = pe.matmul(ps_q[0:SEQ, h * (HEAD + 1):(h + 1) * (HEAD + 1)], probs[:, q, r, g, :],
                                     v1[:, q, h, :], start=True, stop=True)
                if runs(known, 1):
                    last.then_inc(av_ps, 1)

                if block and runs(known, 3):
                    pe.wait_ge(tT_ready, n - 2)
                    for c in range(CHUNKS):
                        k = KC + 1 - c
                        last = pe.matmul(ps_a[0:SEQ, LOGIT_AT:LOGIT_AT + EXPERTS], tT[0:k, c, :], w_gate[0:k, c, :],
                                         start=(c == 0), stop=(c == CHUNKS - 1))
                    last.then_inc(logit_ps, 1)
                if block and runs(known, 4):
                    i = n - 4
                    if known is not None and known - 3 >= IMAGES:
                        pe.wait_ge(logit_read, IMAGES)
                        pe.wait_ge(rank_read, 2 * i)
                    pe.wait_ge(hits_ready, i + 1)
                    if known is None or known >= 5:
                        pe.wait_ge(rank_read, 2 * i)
                    rank = ps_a[0:SEQ, RANK_AT:RANK_AT + EXPERTS]
                    pe.matmul(rank, before[:, :], hits[:, p], start=True, stop=False)
                    pe.matmul(rank, ones[0:SEQ, 0:SEQ], seen[:, p], start=False, stop=True).then_inc(rank_ps, 1)

            pe.wait_ge(route_in, 16 * ROUTE_LOADS)
            pe.wait_ge(consts, CONSTS)
            for b in range(BLOCKS):
                pipeline(pe, lambda n, p, known: step(b, n, p, known), lag_of(b))
            pe.wait_ge(rank_read, 2 * IMAGES)
            pe.matmul(ps_v[0:1, 0:EXPERTS], ones[0:SEQ, 0:1], seen[:, 0], start=True, stop=True).then_inc(total_ps, 1)

            def rows_in(j, p, known):
                pe.wait_ge(picked_in[p], 8 * (j - p) + 16)
                if known is None or known >= 1:
                    pe.wait_ge(pT_ready, j)
                for c in range(CHUNKS):
                    last = pe.transpose(ps_a[0:KC, c * TILE:(c + 1) * TILE], picked[:, p, c * KC:(c + 1) * KC],
                                        ident[:, :])
                last.then_inc(pT_ps, 1)

            def up(j, p, known):
                pe.wait_ge(pT_ready, j + 1)
                pe.wait_ge(expert_in[p], 24 * (j - p) + 48)
                if known is None or known >= 2:
                    pe.wait_ge(h_ready, j - 1)
                for m in range(HIDDEN_CHUNKS):
                    for c in range(CHUNKS):
                        k = KC + 1 - c
                        last = pe.matmul(ps_s[:, 2 * p + m // 4, (m % 4) * TILE:(m % 4 + 1) * TILE],
                                         e1[0:k, p, c, m * 128:(m + 1) * 128], pT[0:k, p, c, :],
                                         start=(c == 0), stop=(c == CHUNKS - 1))
                last.then_inc(h_ps, 1)

            def down(j, p, known):
                pe.wait_ge(h_ready, j + 1)
                if known is None or known >= 2:
                    pe.wait_ge(y_added, j - 1)
                for m in range(HIDDEN_CHUNKS):
                    last = pe.matmul((ps_q, ps_o)[p][:, 0:DIM], hid[:, p, m, :], e2[:, p, m, :],
                                     start=(m == 0), stop=(m == HIDDEN_CHUNKS - 1))
                last.then_inc(y_ps, 1)

            rows_in(0, 0, 0)
            rows_in(1, 1, 1)
            up(0, 0, 0)
            up(1, 1, 1)
            down(0, 0, 0)
            with pe.Fori(1, TILES // 2) as pair:
                for u in range(2):
                    j = pair * 2 + u
                    rows_in(j, u, None)
                    up(j, u, None)
                    down(j - 1, 1 - u, None)
            down(TILES - 1, 1, TILES - 1)




def _inputs(inputs):
    import numpy as np

    f = np.float32
    x = np.asarray(inputs["x"])
    side = x.shape[1]
    framed = np.zeros((IMAGES, side + 2, side + 2, CHANNELS), x.dtype)
    framed[:, 1:-1, 1:-1] = x
    r = PATCH
    rows = {}
    tokens = []
    for i in range(SIDE):
        for j in range(SIDE):
            win = framed[:, r * i:r * i + r + 2, r * j:r * j + r + 2]
            tokens.append(np.concatenate([win[:, 1:-1, 1:-1].reshape(IMAGES, -1), win[:, 0, 1:-1].reshape(IMAGES, -1),
                                          win[:, -1, 1:-1].reshape(IMAGES, -1), win[:, 1:-1, 0].reshape(IMAGES, -1),
                                          win[:, 1:-1, -1].reshape(IMAGES, -1)], axis=1))
    pix = np.stack(tokens, 1).reshape(PAIRS, PAIR, FEATURES)
    pixT = pix.reshape(PAIRS, PAIR, FEATURE_CHUNKS, KC).transpose(0, 3, 2, 1)

    def by_source(a):
        a = a.reshape(r, r, SHIFTS, CHANNELS, -1)
        n = a.shape[-1]
        own = np.zeros((SHIFTS, r, r, CHANNELS, n), a.dtype)
        own[0] = a[:, :, 0]
        own[1][:, :-1] = a[:, 1:, 1]
        own[2][:, 1:] = a[:, :-1, 2]
        own[3][:-1] = a[1:, :, 3]
        own[4][1:] = a[:-1, :, 4]
        halo = np.concatenate([x.reshape(-1, n) for x in (a[0, :, 3], a[-1, :, 4], a[:, 0, 1], a[:, -1, 2])])
        return (own.reshape(SHIFTS, CENTER_CHUNKS, KC, n).transpose(2, 0, 1, 3), halo.reshape(2, KC, n).transpose(1, 0, 2))

    w_center, w_halo = by_source(np.asarray(inputs["L0_tok_W"]))

    def per_feature(a):
        own, halo = by_source(np.asarray(a).reshape(-1, 1))
        return np.concatenate([own.reshape(KC, -1), halo.reshape(KC, -1)], axis=1)

    def chunked(w):
        return w.reshape(-1, KC, w.shape[-1]).transpose(1, 0, 2)

    def attention(w_qkv, w_proj, b_proj):
        w = np.asarray(w_qkv)
        qk = np.zeros((DIM, 2, GROUPS, ROWS, SLOT), w.dtype)
        qk[..., 0:HEAD] = w[0:2 * DIM].T.reshape(DIM, 2, GROUPS, ROWS, HEAD)
        p = np.zeros((KC + 1, CHUNKS, DIM), w.dtype)
        p[0:KC] = chunked(np.asarray(w_proj).T)
        p[KC, 0] = np.asarray(b_proj)
        return qk.reshape(CHUNKS, KC, 2, GROUPS, 128).transpose(1, 0, 2, 3, 4), chunked(w[2 * DIM:].T), p

    arrays = {"pix": pix, "pixT": pixT, "w_center": w_center, "w_halo": w_halo,
              "gain": per_feature(inputs["L0_tok_gamma"]), "shift": per_feature(inputs["L0_tok_beta"]),
              "tok_b": np.asarray(inputs["L0_tok_b"]).reshape(1, DIM),
              "txt": np.asarray(inputs["txt"]).transpose(1, 0, 2)}
    blocks = [attention(*(inputs[n] for n in names)) for names in (
        ("L0_attn_w_qkv", "L0_attn_w_proj", "L0_attn_b_proj"), ("L0_ffn_qkv_w", "L0_ffn_proj_w", "L0_ffn_proj_b"))]
    for name, parts in zip(("qk", "v", "p"), zip(*blocks)):
        arrays[name] = np.stack(parts)

    def with_bias(w, b):
        out = np.zeros((*w.shape[:-2], KC + 1, CHUNKS, w.shape[-1]), w.dtype)
        out[..., 0:KC, :, :] = w.reshape(*w.shape[:-2], CHUNKS, KC, w.shape[-1]).swapaxes(-3, -2)
        out[..., KC, 0, :] = b
        return out

    arrays["affine"] = np.stack([np.stack([np.asarray(inputs[f"L0_ffn_ln{i}_{x}"]).reshape(CHUNKS, KC).T for x in "gb"], 1)
                                 for i in (1, 2)], 1)
    arrays["gate"] = with_bias(np.asarray(inputs["L0_ffn_gate_w"]).T, np.asarray(inputs["L0_ffn_gate_b"]))
    arrays["e1"] = with_bias(np.asarray(inputs["L0_ffn_w1"]).swapaxes(1, 2), np.asarray(inputs["L0_ffn_b1"]))
    arrays["e2"] = np.asarray(inputs["L0_ffn_w2"]).swapaxes(1, 2).reshape(EXPERTS, HIDDEN_CHUNKS, 128, DIM)\
        .transpose(0, 2, 1, 3)
    arrays["eb"] = np.asarray(inputs["L0_ffn_b2"]).reshape(EXPERTS, 1, DIM)
    arrays["before"] = np.triu(np.ones((SEQ, SEQ), f), 1)
    arrays["iota"] = np.broadcast_to(np.arange(EXPERTS, dtype=f), (SEQ, TOP, EXPERTS))
    arrays["region"] = np.broadcast_to(np.arange(EXPERTS, dtype=f) * REGION, (SEQ, EXPERTS))
    arrays["dest"] = np.arange(SEQ, dtype=f)[:, None] + np.arange(TOP, dtype=f) * TOKENS
    pad = np.zeros((TILE, ROW), f)
    pad.view(np.uint32)[:, DIM + 1] = NOWHERE
    arrays["padding"] = pad
    arrays["jota"] = np.arange(TILES, dtype=f)[None]
    return {k: np.ascontiguousarray(v) for k, v in arrays.items()}


def kernel(**inputs):
    import concourse.bacc as _bacc
    from concourse.bass_utils import run_bass_kernel_spmd as _run

    nc = _bacc.Bacc("TRN2", target_bir_lowering=False, num_devices=1)
    arrays = _inputs(inputs)
    tensors = {name: nc.dram_tensor("in_" + name, a.shape, mybir.dt.from_np(a.dtype), kind="ExternalInput").ap()
               for name, a in arrays.items()}
    tensors["out"] = nc.dram_tensor("out", (IMAGES, SEQ, DIM), F32, kind="ExternalOutput").ap()
    tensors["routed"] = nc.dram_tensor("routed", (EXPERTS * REGION + TILE, ROW), F32, kind="Internal").ap()
    tensors["results"] = nc.dram_tensor("results", (TOP * TOKENS, DIM), F32, kind="Internal").ap()
    build(nc, tensors)
    r = _run(nc, [{"in_" + name: a for name, a in arrays.items()}], core_ids=[0])
    return r.results[0]["out"]
```

```python
from contextlib import ExitStack

import concourse.bass as bass
from concourse import mybir

ALU = mybir.AluOpType
ACT = mybir.ActivationFunctionType
AX = mybir.AxisListType
F32 = mybir.dt.float32
F16 = mybir.dt.float16
U32 = mybir.dt.uint32
I32 = mybir.dt.int32

IMAGES = 32
SIDE = 7
PATCHES = SIDE * SIDE
TEXT = 32
SEQ = PATCHES + TEXT
DIM = 192
KC = 96
CHUNKS = DIM // KC
HEADS = 12
HEAD = DIM // HEADS
ROWS = 4
GROUPS = HEADS // ROWS
SLOT = 32

PATCH = 16
CHANNELS = 3
CENTER = PATCH * PATCH * CHANNELS
HALO = 4 * PATCH * CHANNELS
FEATURES = CENTER + HALO
SHIFTS = 5
COPIED = SHIFTS * CENTER
CENTER_CHUNKS = CENTER // KC
FEATURE_CHUNKS = FEATURES // KC
PAIR = 2 * PATCHES
PAIRS = IMAGES // 2
BN = 6

EXPERTS = 8
TOP = 2
HIDDEN = 768
HIDDEN_CHUNKS = HIDDEN // 128
TOKENS = IMAGES * SEQ
TILE = 128
REGION = TOKENS + TILE
TILES = (TOP * TOKENS + EXPERTS * (TILE - 1)) // TILE
ROW = DIM + 2
NOWHERE = 1 << 20
LOGIT_AT, RANK_AT = 200, 216
BLOCKS = 2
ATTN_LOADS = 16 * (3 * BLOCKS + 1)
EPS = 1e-5
CONSTS = 6
ROUTE_LOADS = 8
SLOTS = 4
W1_SIZE = 2 * CHUNKS * HIDDEN
W2_SIZE = 2 * HIDDEN_CHUNKS * DIM
LISTED = TILES + 1
A_SCALE = 16.0
MAX_SCALE = 4096.0
W_SCALE = 256.0
PRODUCTS = ((0, 0), (0, 1), (1, 0))
HALVES = 2
PER_HALF = HIDDEN_CHUNKS // HALVES
COMBINE = 8


def build(nc, t):
    with ExitStack() as ctx:
        def sb(name, shape, dt=F32):
            return ctx.enter_context(nc.sbuf_tensor(name, shape, dt))

        def sem(name):
            return ctx.enter_context(nc.semaphore(name))

        stream = sb("stream", [SEQ, IMAGES, DIM])
        ident = sb("ident", [128, 128])
        ones = sb("ones", [128, 128])
        half = sb("half", [128, PAIRS])
        minus_one = sb("minus_one", [128, 1])
        eps = sb("eps", [128, 1])
        tick = sb("tick", [1, 1])

        gain = sb("gain", [KC, SHIFTS * CENTER_CHUNKS + 2])
        shift = sb("shift", [KC, SHIFTS * CENTER_CHUNKS + 2])
        b_row = sb("b_row", [1, DIM])
        bias_row = sb("bias_row", [1, DIM])
        colsum = sb("colsum", [PAIR, DIM])
        bias_all = sb("bias_all", [PAIR, DIM])
        bn_c = sb("bn_c", [PAIR, 2, 2 * BN])
        bn_h = sb("bn_h", [PAIR, 2, BN])
        bn_e = sb("bn_e", [PAIR, 2, 2 * BN])
        mv_k = sb("mv_k", [PAIR, 2, 3, 2])
        mv = sb("mv", [PAIR, PAIRS, 3, 2])
        stat = sb("stat", [PAIR, 8, PAIRS])
        affine = sb("affine", [KC, 2, 2, CHUNKS])
        seen = sb("seen", [SEQ, 2, EXPERTS])

        padding = sb("padding", [TILE, ROW])
        cnt = sb("cnt", [1, EXPERTS])
        cnt_i = sb("cnt_i", [1, EXPERTS], I32)
        need = sb("need", [1, EXPERTS])
        need_i = sb("need_i", [1, EXPERTS], I32)
        upto = sb("upto", [1, 2, EXPERTS])
        jota = sb("jota", [1, LISTED])
        past = sb("past", [1, LISTED, EXPERTS])
        tile_e = sb("tile_e", [1, LISTED])
        tile_s = sb("tile_s", [1, LISTED])
        tile_l = sb("tile_l", [1, LISTED])
        expert_i = sb("expert_i", [1, LISTED], I32)
        row_i = sb("row_i", [1, LISTED], I32)
        weights_i = sb("weights_i", [1, 2 * LISTED], I32)

        with ExitStack() as embedding:
            def tmp(name, shape):
                return embedding.enter_context(nc.sbuf_tensor(name, shape, F32))

            w_center = tmp("w_center", [KC, SHIFTS, CENTER_CHUNKS, DIM])
            w_halo = tmp("w_halo", [KC, FEATURE_CHUNKS - CENTER_CHUNKS, DIM])
            w_fold = tmp("w_fold", [KC, FEATURE_CHUNKS, DIM])
            pix = tmp("pix", [PAIR, 2, FEATURES])
            pixT = tmp("pixT", [KC, 2, FEATURE_CHUNKS, PAIR])
            raw = tmp("raw", [PAIR, PAIRS, DIM])
            with nc.sbuf_tensor("w_scaled", [KC, SHIFTS, CENTER_CHUNKS, DIM], F32) as w_scaled:
                pass
            w_qk = tmp("w_qk", [KC, BLOCKS, CHUNKS, 2, GROUPS, 128])
            w_v = tmp("w_v", [KC, BLOCKS, CHUNKS, DIM])
            w_p = tmp("w_p", [KC + 1, BLOCKS, CHUNKS, DIM])

        w1 = sb("w1", [KC + 1, EXPERTS * W1_SIZE], F16)
        w2 = sb("w2", [TILE, EXPERTS * W2_SIZE], F16)
        w1_parts = w1[:, :].rearrange("k (e p c n) -> k e p c n", e=EXPERTS, p=2, c=CHUNKS)
        w2_parts = w2[:, :].rearrange("k (e p c n) -> k e p c n", e=EXPERTS, p=2, c=HIDDEN_CHUNKS)
        w1_whole = sb("w1_whole", [KC + 1, CHUNKS, HIDDEN])
        w2_whole = sb("w2_whole", [TILE, HIDDEN_CHUNKS, DIM])

        with ExitStack() as attention:
            def tmp(name, shape, dt=F32):
                return attention.enter_context(nc.sbuf_tensor(name, shape, dt))

            probs = tmp("probs", [SEQ, 2, ROWS, GROUPS, SEQ])
            xn = tmp("xn", [SEQ, 2, DIM])
            w_qk16 = tmp("w_qk16", [KC, BLOCKS, 2, CHUNKS, 2, GROUPS, 128], F16)
            w_v16 = tmp("w_v16", [KC, BLOCKS, 2, CHUNKS, DIM], F16)
            w_p16 = tmp("w_p16", [KC + 1, BLOCKS, 2, CHUNKS, DIM], F16)
            slot_rows = tmp("slot_rows", [128, 3])
            bn_x = tmp("bn_x", [SEQ, 2, BN])
            mv_x = tmp("mv_x", [SEQ, 2, 2])
            veps = tmp("veps", [SEQ, 2, 1])
            rstd = tmp("rstd", [SEQ, 2, 1])
            rstd2 = tmp("rstd2", [SEQ, 2, 1])
            nmr = tmp("nmr", [SEQ, 2, 1])
            scale2 = tmp("scale2", [SEQ, 2, 1])
            nmr2 = tmp("nmr2", [SEQ, 2, 1])
            a32 = tmp("a32", [KC, 2, CHUNKS, SEQ])
            aT = tmp("aT", [KC, 2, 2, CHUNKS, SEQ], F16)
            hi = tmp("hi", [128, 2, 2, GROUPS, SEQ], F16)
            q_both = tmp("q_both", [128, 2, GROUPS, SEQ], F16)
            k_low = tmp("k_low", [128, 2, GROUPS, SEQ], F16)
            q_high = tmp("q_high", [128, 2, GROUPS, SEQ], F16)
            v1 = tmp("v1", [SEQ, 2, HEADS, HEAD + 1])
            mpad = tmp("mpad", [SEQ, 2, GROUPS, ROWS, SLOT])
            qm = tmp("qm", [128, 2, GROUPS, SEQ], F16)
            rec = tmp("rec", [SEQ, 2, HEADS, 1])
            o = tmp("o", [SEQ, 2, HEADS, HEAD])
            oT = tmp("oT", [KC + 1, 2, CHUNKS, SEQ], F16)

            inner = tmp("inner", [SEQ, IMAGES, DIM])
            w_gate = tmp("w_gate", [KC + 1, CHUNKS, EXPERTS])
            bn_t = tmp("bn_t", [SEQ, 2, BN])
            mv_t = tmp("mv_t", [SEQ, 2, 2])
            rstd_t = tmp("rstd_t", [SEQ, IMAGES, 1])
            nmr_t = tmp("nmr_t", [SEQ, IMAGES, 1])
            rstd_s = tmp("rstd_s", [SEQ, 2, 1])
            mr_s = tmp("mr_s", [SEQ, 2, 1])
            nmr_s = tmp("nmr_s", [SEQ, 2, 1])
            veps_t = tmp("veps_t", [SEQ, 2, 1])
            xh = tmp("xh", [SEQ, 2, DIM])
            tT = tmp("tT", [KC + 1, CHUNKS, SEQ])
            before = tmp("before", [SEQ, SEQ])
            iota = tmp("iota", [SEQ, TOP, EXPERTS])
            region = tmp("region", [SEQ, EXPERTS])
            logit = tmp("logit", [SEQ, 2, EXPERTS])
            best = tmp("best", [SEQ, 2, 8])
            best_at = tmp("best_at", [SEQ, 2, 8], U32)
            chosen = tmp("chosen", [SEQ, 2, TOP])
            mask = tmp("mask", [SEQ, 2, TOP, EXPERTS])
            hits = tmp("hits", [SEQ, 2, EXPERTS])
            gap = tmp("gap", [SEQ, 2, 1])
            egap = tmp("egap", [SEQ, 2, 1])
            esum = tmp("esum", [SEQ, 2, 1])
            place = tmp("place", [SEQ, 2, EXPERTS])
            placed = tmp("placed", [SEQ, 2, TOP, EXPERTS])
            slot_f = tmp("slot_f", [SEQ, 2, TOP])
            slot = tmp("slot", [SEQ, 2, TOP], U32)
            dest = tmp("dest", [SEQ, TOP])
            rows = tmp("rows", [SEQ, 2, TOP, ROW])


        b2 = sb("b2", [TILE, EXPERTS, DIM])
        picked = sb("picked", [TILE, SLOTS, ROW])
        x32 = sb("x32", [KC, 2, CHUNKS, TILE])
        xs = sb("xs", [KC + 1, 2, 2, CHUNKS, TILE], F16)
        h32 = sb("h32", [TILE, 2, HALVES, PER_HALF, TILE])
        hs = sb("hs", [TILE, 2, 2, HALVES, PER_HALF, TILE], F16)
        y = sb("y", [TILE, 2, DIM])
        ys = sb("ys", [TILE, SLOTS, DIM])
        got = sb("got", [SEQ, 2, TOP, COMBINE, DIM])

        ps_s = ctx.enter_context(nc.psum_tensor("ps_s", [128, ROWS, 512], F32))
        ps_q = ctx.enter_context(nc.psum_tensor("ps_q", [128, 512], F32))
        ps_a = ctx.enter_context(nc.psum_tensor("ps_a", [128, 512], F32))
        ps_o = ctx.enter_context(nc.psum_tensor("ps_o", [128, 512], F32))
        ps_v = ctx.enter_context(nc.psum_tensor("ps_v", [128, 512], F32))

        consts = sem("consts")
        ident_zero = sem("ident_zero")
        mpad_zero = sem("mpad_zero")
        small_in = sem("small_in")
        w_in = sem("w_in")
        pix_in = [sem(f"pix_in{p}") for p in range(2)]
        pixT_in = [sem(f"pixT_in{p}") for p in range(2)]
        pix_used = sem("pix_used")
        attn_in = sem("attn_in")
        text_in = sem("text_in")
        scaled = sem("scaled")
        scaled_pool = sem("scaled_pool")
        folded = sem("folded")
        bias_ps = sem("bias_ps")
        bias_out = sem("bias_out")
        sums_ps = sem("sums_ps")
        sums_out = sem("sums_out")
        emb_ps = sem("emb_ps")
        emb_raw = sem("emb_raw")
        dve_step = sem("dve_step")
        var_ready = sem("var_ready")
        rstd_ready = sem("rstd_ready")
        emb_done = sem("emb_done")
        emb_moved = [sem(f"emb_moved{p}") for p in range(2)]

        stats_ready = sem("stats_ready")
        pool_step = sem("pool_step")
        norm_ready = sem("norm_ready")
        xn_ready = sem("xn_ready")
        aT_ps = sem("aT_ps")
        a32_ready = sem("a32_ready")
        aT_hi_ready = sem("aT_hi_ready")
        oT_hi_ready = sem("oT_hi_ready")
        parts_ready = sem("parts_ready")
        operands = sem("operands")
        w_hi_ready = sem("w_hi_ready")
        w_lo_ready = sem("w_lo_ready")
        aT_ready = sem("aT_ready")
        qk_ps = sem("qk_ps")
        qk_ready = sem("qk_ready")
        v_ps = sem("v_ps")
        v_ready = sem("v_ready")
        s_ps = sem("s_ps")
        max_ready = sem("max_ready")
        mT_ps = sem("mT_ps")
        qm_ready = sem("qm_ready")
        st_ps = sem("st_ps")
        p_ready = sem("p_ready")
        av_ps = sem("av_ps")
        o_ready = sem("o_ready")
        oT_ps = sem("oT_ps")
        oT_ready = sem("oT_ready")
        pr_ps = sem("pr_ps")
        res_done = sem("res_done")

        bn_done = sem("bn_done")
        rec_done = sem("rec_done")
        route_in = sem("route_in")
        bn_t_done = sem("bn_t_done")
        stats_t = sem("stats_t")
        root_t = sem("root_t")
        kept = sem("kept")
        xh_ready = sem("xh_ready")
        tT_ps = sem("tT_ps")
        tT_ready = sem("tT_ready")
        logit_ps = sem("logit_ps")
        rank_ps = sem("rank_ps")
        logit_read = sem("logit_read")
        rank_read = sem("rank_read")
        route_step = sem("route_step")
        gap_ready = sem("gap_ready")
        egap_ready = sem("egap_ready")
        hits_ready = sem("hits_ready")
        rows_filled = sem("rows_filled")
        slots_ready = sem("slots_ready")
        place_step = sem("place_step")
        slot_step = sem("slot_step")
        att_done = sem("att_done")
        scattered = [sem(f"scattered{p}") for p in range(2)]
        total_ps = sem("total_ps")
        table_step = sem("table_step")
        tables = sem("tables")
        padded = sem("padded")
        b2_in = sem("b2_in")
        whole_in = sem("whole_in")
        hi_ready = sem("hi_ready")
        lo_ready = sem("lo_ready")
        picked_in = [sem(f"picked_in{u}") for u in range(SLOTS)]
        x_ps = sem("x_ps")
        x32_ready = sem("x32_ready")
        x_hi_ready = sem("x_hi_ready")
        x_ready = sem("x_ready")
        xs_ones = sem("xs_ones")
        h_ps = sem("h_ps")
        h32_ready = sem("h32_ready")
        h_hi_ready = sem("h_hi_ready")
        h_ready = sem("h_ready")
        y_ps = sem("y_ps")
        y_added = sem("y_added")
        ys_ready = sem("ys_ready")
        ticked = sem("ticked")
        ys_out = [sem(f"ys_out{u}") for u in range(SLOTS)]
        got_in = [sem(f"got_in{p}") for p in range(2)]
        summed = sem("summed")
        summing = sem("summing")
        out_done = sem("out_done")

        block = ctx.enter_context(nc.Block())

        def pipeline(eng, step, lags, split=None):
            first, last = lags + lags % 2, IMAGES - 2
            for n in range(first):
                step(n, n % 2, n)
            begin = first // 2
            if split:
                with eng.Fori(begin, begin + EXPERTS) as pair:
                    step(pair * 2, 0, None)
                    split(pair - begin)
                    step(pair * 2 + 1, 1, None)
                begin += EXPERTS
            with eng.Fori(begin, last // 2) as pair:
                step(pair * 2, 0, None)
                step(pair * 2 + 1, 1, None)
            for n in range(last, IMAGES + lags):
                step(n, n % 2, n)

        def tiles(eng, step, table=None, most=()):
            each = len(most)
            bounded = "the tables hold experts below EXPERTS, and rows of their regions or of the padding"

            def body(quad, known):
                values = ()
                if each:
                    loaded = nc.values_load_multi_w_load_instructions(
                        table[0:1, bass.ds(quad * (SLOTS * each), (SLOTS + 1) * each)], engines=(eng.engine,),
                        min_val=0, max_val=max(most), skip_runtime_bounds_check_because=bounded)[1]
                    values = [x if most[i % each] == max(most) else
                              nc.s_assert_within(x, 0, most[i % each],
                                                 skip_runtime_bounds_check_because=bounded)
                              for i, x in enumerate(loaded)]
                for u in range(SLOTS):
                    step(quad * SLOTS + u, u, quad, None if known is None else known * SLOTS + u,
                         values[u * each:(u + 2) * each])

            body(0, 0)
            with eng.Fori(1, TILES // SLOTS - 1) as quad:
                body(quad, None)
            body(TILES // SLOTS - 1, TILES // SLOTS - 1)

        def runs(known, lag):
            return known is None or 0 <= known - lag < IMAGES

        def lag_of(block):
            return (2, 5)[block]

        @block.sync
        def _(sp):
            sp.dma_start(gain[:, :], t["gain"]).then_inc(small_in, 16)
            sp.dma_start(shift[:, :], t["shift"]).then_inc(small_in, 16)
            sp.dma_start(b_row[:, :], t["tok_b"]).then_inc(small_in, 16)
            sp.dma_start(w_halo[:, :, :], t["w_halo"]).then_inc(w_in, 16)
            sp.dma_start(w_center[:, :, :, :], t["w_center"]).then_inc(w_in, 16)

            def load(k, p, known):
                if known is None or known >= 2:
                    sp.wait_ge(pix_used, k - 1)
                    sp.wait_ge(emb_ps, k - 1)
                sp.dma_start(pix[:, p, :], t["pix"][k]).then_inc(pix_in[p], 16)
                sp.dma_start(pixT[:, p, :, :], t["pixT"][k]).then_inc(pixT_in[p], 16)

            for name, tile in (("affine", affine), ("gate", w_gate), ("before", before), ("iota", iota),
                               ("region", region), ("dest", dest), ("padding", padding), ("jota", jota)):
                sp.dma_start(tile[:], t[name]).then_inc(route_in, 16)
            for k in range(2):
                load(k, k, k)
            with sp.Fori(1, PAIRS // 2) as pair:
                k = pair * 2
                load(k, 0, None)
                load(k + 1, 1, None)

            def move(k, p, known):
                sp.wait_ge(emb_done, k + 1)
                for half_ in range(2):
                    sp.dma_start(stream[0:PATCHES, 2 * k + half_, :],
                                 raw[half_ * PATCHES:(half_ + 1) * PATCHES, k, :]).then_inc(emb_moved[p], 16)

            for k in range(2):
                move(k, k, k)
            with sp.Fori(1, PAIRS // 2) as pair:
                k = pair * 2
                move(k, 0, None)
                move(k + 1, 1, None)
            for p in range(2):
                sp.wait_ge(emb_moved[p], 16 * PAIRS)
            sp.wait_ge(w_lo_ready, 3 * BLOCKS)

            def load_expert(e):
                sp.dma_start(w1_whole[:, :, :], t["e1"][e]).then_inc(whole_in, 16)
                sp.dma_start(w2_whole[:, :, :], t["e2"][e]).then_inc(whole_in, 16)

            load_expert(0)
            with sp.Fori(1, EXPERTS) as e:
                sp.wait_ge(lo_ready, e)
                load_expert(e)

            sp.wait_ge(tables, 5)
            sp.dma_start(b2[:, :, :], t["eb"].to_broadcast([TILE, EXPERTS, DIM])).then_inc(b2_in, 16)
            sp.wait_ge(route_in, 16 * ROUTE_LOADS)
            for e in range(EXPERTS):
                count = sp.value_load(cnt_i[0:1, e:e + 1], min_val=0, max_val=TOKENS)
                sp.dma_start(t["routed"][bass.ds(count + e * REGION, TILE), :], padding[:, :]).then_inc(padded, 16)
            sp.dma_start(t["routed"][EXPERTS * REGION:EXPERTS * REGION + TILE, :], padding[:, :]).then_inc(padded, 16)
            sp.wait_ge(padded, 16 * (EXPERTS + 1))
            for p in range(2):
                sp.wait_ge(scattered[p], 16 * TOP * IMAGES // 2)

            def fetch(j, u, quad, known, row):
                if known is None or known >= SLOTS:
                    sp.wait_ge(ys_out[u], quad * 16)
                sp.dma_start(picked[:, u, :], t["routed"][bass.ds(row[0], TILE), :]).then_inc(picked_in[u], 16)

            tiles(sp, fetch, row_i, (EXPERTS * REGION,))

            for u in range(SLOTS):
                sp.wait_ge(ys_out[u], 16 * TILES // SLOTS)
            for c in range(IMAGES // COMBINE):
                if c >= 2:
                    sp.wait_ge(summed, c - 1)
                for k in range(TOP):
                    sp.dma_start(got[:, c % 2, k], t["results"][k * TOKENS:(k + 1) * TOKENS, :]
                                 .rearrange("(b s) d -> s b d", s=SEQ)[:, c * COMBINE:(c + 1) * COMBINE, :])\
                        .then_inc(got_in[c % 2], 16)
            for c in range(IMAGES // COMBINE):
                sp.wait_ge(summed, c + 1)
                sp.dma_start(t["out"][c * COMBINE:(c + 1) * COMBINE].rearrange("b s d -> s b d"),
                             stream[:, c * COMBINE:(c + 1) * COMBINE, :]).then_inc(out_done, 16)
            sp.wait_ge(out_done, 16 * (IMAGES // COMBINE))

        @block.gpsimd
        def _(pool):
            nc.gpsimd.memset(ident[:, :], 0.0).then_inc(ident_zero, 1)
            nc.gpsimd.memset(ones[:, :], 1.0).then_inc(consts, 1)
            nc.gpsimd.memset(half[:, :], -0.5).then_inc(consts, 1)
            nc.gpsimd.memset(tick[:, :], 0.0).then_inc(ticked, 1)
            nc.gpsimd.memset(minus_one[:, :], -1.0).then_inc(consts, 1)
            nc.gpsimd.memset(eps[:, :], EPS).then_inc(consts, 1)
            pool.wait_ge(ident_zero, 1)
            nc.gpsimd.affine_select(out=ident[:, :], in_=ident[:, :], compare_op=ALU.not_equal, fill=1.0,
                                    base=0, pattern=[[-1, 128]], channel_multiplier=1).then_inc(consts, 1)
            nc.gpsimd.memset(mpad[:, :, :, :, :], 0.0).then_inc(mpad_zero, 1)
            nc.gpsimd.memset(v1[:, :, :, HEAD:HEAD + 1], A_SCALE).then_inc(mpad_zero, 1)
            pool.wait_ge(small_in, 48)
            pool.wait_ge(w_in, 32)
            n = SHIFTS * CENTER_CHUNKS
            nc.gpsimd.tensor_tensor(w_fold[:, CENTER_CHUNKS:, :], w_halo[:, :, :],
                                    gain[:, n:n + 2].unsqueeze(2).to_broadcast([KC, 2, DIM]), ALU.mult)\
                .then_inc(scaled_pool, 1)
            for s in (3, 4):
                nc.gpsimd.tensor_tensor(w_scaled[:, s], w_center[:, s],
                                        gain[:, s * CENTER_CHUNKS:(s + 1) * CENTER_CHUNKS].unsqueeze(2)
                                        .to_broadcast([KC, CENTER_CHUNKS, DIM]), ALU.mult).then_inc(scaled_pool, 1)
            pool.wait_ge(scaled_pool, 3)
            nc.gpsimd.tensor_tensor(w_scaled[:, 3], w_scaled[:, 3], w_scaled[:, 4], ALU.add).then_inc(scaled_pool, 1)
            pool.wait_ge(var_ready, 1)
            nc.gpsimd.tensor_tensor(stat[:, 7, :], stat[:, 6, :], half[0:PAIR, :], ALU.pow).then_inc(rstd_ready, 1)

            nc.gpsimd.memset(seen[:, :, :], 0.0).then_inc(consts, 1)
            pool_incs = [0]
            tt = nc.gpsimd.tensor_tensor

            def norm(block, i, p, known):
                base = block * IMAGES
                per = (3, 8)[block]
                at = pool_incs[0] + i * per
                steps = 0

                def then(instruction):
                    nonlocal steps
                    steps += 1
                    instruction.then_inc(pool_step, 1)
                    pool.wait_ge(pool_step, at + steps)

                if known is None or known + base >= 2:
                    pool.wait_ge(xn_ready, i + base - 1)
                pool.wait_ge(stats_ready, i + base + 1)
                then(tt(veps[:, p], mv_x[:, p, 1:2], eps[0:SEQ, :], ALU.add))
                then(tt(rstd[:, p], veps[:, p], half[0:SEQ, 0:1], ALU.pow))
                then(tt(veps[:, p], mv_x[:, p, 0:1], rstd[:, p], ALU.mult))
                last = tt(nmr[:, p], veps[:, p], minus_one[0:SEQ, :], ALU.mult)
                if block:
                    then(last)
                    then(tt(veps[:, p], mv_x[:, p, 1:2], rstd[:, p], ALU.mult))
                    then(tt(veps[:, p], veps[:, p], rstd[:, p], ALU.mult))
                    then(tt(veps[:, p], veps[:, p], eps[0:SEQ, :], ALU.add))
                    then(tt(rstd2[:, p], veps[:, p], half[0:SEQ, 0:1], ALU.pow))
                    tt(scale2[:, p], rstd[:, p], rstd2[:, p], ALU.mult)
                    last = tt(nmr2[:, p], nmr[:, p], rstd2[:, p], ALU.mult)
                last.then_inc(norm_ready, 1)

            for i in range(2):
                norm(0, i, i, i)
            with pool.Fori(1, IMAGES // 2) as pair:
                norm(0, pair * 2, 0, None)
                norm(0, pair * 2 + 1, 1, None)
            pool_incs[0] += 3 * IMAGES

            def root(i, p):
                pool.wait_ge(stats_t, i + 1)
                tt(veps_t[:, p], mv_t[:, p, 1:2], eps[0:SEQ, :], ALU.add).then_inc(root_t, 1)
                pool.wait_ge(root_t, 4 * i + 1)
                tt(rstd_s[:, p], veps_t[:, p], half[0:SEQ, 0:1], ALU.pow).then_inc(root_t, 1)
                pool.wait_ge(root_t, 4 * i + 2)
                tt(mr_s[:, p], mv_t[:, p, 0:1], rstd_s[:, p], ALU.mult).then_inc(root_t, 1)
                pool.wait_ge(root_t, 4 * i + 3)

            def keep(i, p):
                tt(nmr_t[:, i], mr_s[:, p], minus_one[0:SEQ, :], ALU.mult)
                tt(rstd_t[:, i], rstd_s[:, p], ones[0:SEQ, 0:1], ALU.mult).then_inc(kept, 1)
                tt(stream[:, i, :], stream[:, i, :], inner[:, i, :], ALU.add).then_inc(res_done, 1)

            norm(1, 0, 0, 0)

            def step(n, p, known):
                if runs(known, -1):
                    norm(1, n + 1, 1 - p, None if known is None else known + 1)
                if runs(known, 2):
                    root(n - 2, p)
                if runs(known, 5):
                    pool.wait_ge(slots_ready, n - 4)
                    pool.wait_ge(rows_filled, n - 4)
                if runs(known, 2):
                    tt(nmr_s[:, p], mr_s[:, p], minus_one[0:SEQ, :], ALU.mult).then_inc(root_t, 1)
                    keep(n - 2, p)
                if runs(known, 5):
                    for k in range(TOP):
                        nc.gpsimd.indirect_dma_start(
                            out=t["routed"], out_offset=bass.IndirectOffsetOnAxis(ap=slot[:, 1 - p, k:k + 1], axis=0),
                            in_=rows[:, 1 - p, k, :], in_offset=None).then_inc(scattered[1 - p], 16)

            pipeline(pool, step, 5)

            def send(j, u, quad, known, _):
                pool.wait_ge(ys_ready, j + 1)
                pool.wait_ge(ticked, j + 1)
                tt(tick[:, :], minus_one[0:1, :], eps[0:1, :], ALU.mult).then_inc(ticked, 1)
                nc.gpsimd.indirect_dma_start(
                    out=t["results"],
                    out_offset=bass.IndirectOffsetOnAxis(ap=picked[:, u, DIM + 1:DIM + 2].bitcast(U32), axis=0),
                    in_=ys[:, u, :], in_offset=None, bounds_check=TOP * TOKENS - 1, oob_is_err=False)\
                    .then_inc(ys_out[u], 16)

            tiles(pool, send)

        @block.scalar
        def _(act):
            act.dma_start(stream[PATCHES:SEQ, :, :], t["txt"]).then_inc(text_in, 16)
            act.dma_start(slot_rows[:, :], t["slot_rows"]).then_inc(attn_in, 16)
            act.wait_ge(folded, 1)
            for b in range(BLOCKS):
                act.dma_start(w_qk[:, b], t["qk"][b]).then_inc(attn_in, 16)
                act.dma_start(w_v[:, b], t["v"][b]).then_inc(attn_in, 16)
                act.dma_start(w_p[:, b], t["p"][b]).then_inc(attn_in, 16)
            act.wait_ge(bias_ps, 1)
            nc.scalar.copy(bias_row[:, :], ps_o[0:1, 0:DIM]).then_inc(bias_out, 1)
            act.wait_ge(sums_ps, 1)
            nc.scalar.copy(colsum[:, :], ps_v[0:PAIR, 0:DIM]).then_inc(sums_out, 1)
            nc.scalar.copy(bias_all[:, :], ps_v[0:PAIR, DIM:2 * DIM]).then_inc(sums_out, 1)

            def stage(k, p):
                act.wait_ge(emb_ps, k + 1)
                nc.scalar.copy(raw[:, k, :], (ps_q, ps_a)[p][0:PAIR, 0:DIM]).then_inc(emb_raw, 1)

            with act.Fori(0, PAIRS // 4) as pair:
                stage(pair * 2, 0)
                stage(pair * 2 + 1, 1)
            act.wait_ge(attn_in, ATTN_LOADS)
            for b in range(BLOCKS):
                for whole, parts in ((w_qk, w_qk16), (w_v, w_v16), (w_p, w_p16)):
                    nc.scalar.activation(parts[:, b, 0], whole[:, b], ACT.Copy, scale=A_SCALE).then_inc(w_hi_ready, 1)
            with act.Fori(PAIRS // 4, PAIRS // 2) as pair:
                stage(pair * 2, 0)
                stage(pair * 2 + 1, 1)
            act.wait_ge(mpad_zero, 5)
            def normalize(block, i, p):
                act.wait_ge(norm_ready, i + block * IMAGES + 1)
                if block == 0:
                    nc.scalar.activation(xn[:, p], stream[:, i, :], ACT.Identity,
                                         bias=nmr[:, p], scale=rstd[:, p]).then_inc(xn_ready, 1)
                    return
                nc.scalar.activation(inner[:, i, :], stream[:, i, :], ACT.Identity,
                                     bias=nmr[:, p], scale=rstd[:, p])
                nc.scalar.activation(xn[:, p], stream[:, i, :], ACT.Identity,
                                     bias=nmr2[:, p], scale=scale2[:, p]).then_inc(xn_ready, 1)

            def step(block, n, p, known):
                base = block * IMAGES
                if runs(known, 0):
                    act.wait_ge(aT_ps, n + base + 1)
                    src = ps_a[0:KC, 0:CHUNKS * SEQ].rearrange("k (c s) -> k c s", c=CHUNKS)
                    if block == 0:
                        nc.scalar.copy(aT[:, p, 0], src).then_inc(aT_hi_ready, 1)
                    else:
                        for c in range(CHUNKS):
                            last = nc.scalar.activation(a32[:, p, c], src[:, c], ACT.Identity,
                                                        bias=affine[:, 0, 1, c:c + 1], scale=affine[:, 0, 0, c:c + 1])
                        last.then_inc(a32_ready, 1)
                if runs(known, 1):
                    act.wait_ge(st_ps, n + base)
                    nc.scalar.activation(probs[:, 1 - p], ps_s[0:SEQ, :, 0:GROUPS * SEQ]
                                         .rearrange("k r (g q) -> k r g q", g=GROUPS),
                                         ACT.Exp, scale=HEAD ** -0.5 / A_SCALE ** 2).then_inc(p_ready, 1)
                if runs(known, 2):
                    act.wait_ge(oT_ps, n + base - 1)
                    nc.scalar.copy(oT[0:KC, 0], ps_o[0:KC, 0:CHUNKS * SEQ].rearrange("k (c s) -> k c s", c=CHUNKS))\
                        .then_inc(oT_hi_ready, 1)
                if block and runs(known, 4):
                    act.wait_ge(gap_ready, n - 3)
                    nc.scalar.activation(egap[:, p], gap[:, p], ACT.Exp).then_inc(egap_ready, 1)
                if runs(known, 0):
                    act.wait_ge(qk_ps, n + base + 1)
                    nc.scalar.copy(hi[:, p], ps_q[:, 0:2 * GROUPS * SEQ]
                                   .rearrange("k (a g s) -> k a g s", a=2, g=GROUPS)).then_inc(qk_ready, 1)
                if runs(known, -1):
                    normalize(block, n + 1, 1 - p)
                if block and runs(known, 3):
                    act.wait_ge(tT_ps, n - 2)
                    src = ps_a[0:KC, 0:CHUNKS * SEQ].rearrange("k (c s) -> k c s", c=CHUNKS)
                    for c in range(CHUNKS):
                        last = nc.scalar.activation(tT[0:KC, c], src[:, c], ACT.Identity,
                                                    bias=affine[:, 1, 1, c:c + 1], scale=affine[:, 1, 0, c:c + 1])
                    last.then_inc(tT_ready, 1)
                if block and runs(known, 4):
                    i = n - 4
                    if known is None or known >= 6:
                        act.wait_ge(scattered[p], 16 * (i - p))
                    act.wait_ge(kept, i + 1)
                    for k in range(TOP):
                        last = nc.scalar.activation(rows[:, p, k, 0:DIM], inner[:, i, :], ACT.Identity,
                                                    bias=nmr_t[:, i], scale=rstd_t[:, i])
                    last.then_inc(rows_filled, 1)
                if block and runs(known, 2):
                    i = n - 2
                    act.wait_ge(root_t, 4 * i + 4)
                    nc.scalar.activation(xh[:, p], inner[:, i, :], ACT.Identity,
                                         bias=nmr_s[:, p], scale=rstd_s[:, p]).then_inc(xh_ready, 1)

            def split(e):
                act.wait_ge(whole_in, e * 32 + 32)
                nc.scalar.activation(w1_parts[:, e, 0], w1_whole[:, :, :], ACT.Copy, scale=W_SCALE)
                nc.scalar.activation(w2_parts[:, e, 0], w2_whole[:, :, :], ACT.Copy, scale=W_SCALE).then_inc(hi_ready, 1)

            act.wait_ge(route_in, 16 * ROUTE_LOADS)
            for b in range(BLOCKS):
                normalize(b, 0, 0)
                pipeline(act, lambda n, p, known: step(b, n, p, known), lag_of(b), None if b else split)

            def activate(j, p, known):
                for half in range(HALVES):
                    if known is None or known >= 2:
                        act.wait_ge(h_ready, j * HALVES + (half + 1 - 2 * HALVES))
                    act.wait_ge(h_ps, j * HALVES + (half + 1))
                    nc.scalar.activation(h32[:, p, half], ps_s[:, 2 * p + half, 0:PER_HALF * TILE]
                                         .rearrange("h (c n) -> h c n", c=PER_HALF),
                                         ACT.Gelu, scale=1 / W_SCALE).then_inc(h32_ready, 1)
                    if known is None or known >= 2:
                        act.wait_ge(y_ps, j - 1)
                    act.wait_ge(h32_ready, j * HALVES + (half + 1))
                    nc.scalar.copy(hs[:, p, 0, half], h32[:, p, half]).then_inc(h_hi_ready, 1)

            def weigh(j, u, quad, known):
                if known is None or known >= SLOTS:
                    act.wait_ge(ys_out[u], quad * 16)
                act.wait_ge(picked_in[u], quad * 16 + 16)
                act.wait_ge(y_added, j + 1)
                nc.scalar.activation(ys[:, u, :], y[:, u % 2], ACT.Copy, scale=picked[:, u, DIM:DIM + 1])\
                    .then_inc(ys_ready, 1)

            def step(j, u, quad, known, _):
                if known is None or known + 1 < TILES:
                    activate(j + 1, (u + 1) % 2, None if known is None else known + 1)
                weigh(j, u, quad, known)

            activate(0, 0, 0)
            tiles(act, step)

        @block.vector
        def _(dve):
            steps = [0]

            def then(instruction):
                instruction.then_inc(dve_step, 1)
                steps[0] += 1
                dve.wait_ge(dve_step, steps[0])

            nc.vector.memset(oT[KC:KC + 1, 0, :, :], 1.0).then_inc(mpad_zero, 1)
            nc.vector.memset(oT[KC:KC + 1, 1, :, :], 0.0).then_inc(mpad_zero, 1)
            nc.vector.memset(tT[KC:KC + 1, :, :], 1.0).then_inc(mpad_zero, 1)
            dve.wait_ge(small_in, 48)
            dve.wait_ge(w_in, 32)
            for s in range(3):
                then(nc.vector.tensor_tensor(w_scaled[:, s], w_center[:, s],
                                             gain[:, s * CENTER_CHUNKS:(s + 1) * CENTER_CHUNKS].unsqueeze(2)
                                             .to_broadcast([KC, CENTER_CHUNKS, DIM]), ALU.mult))
                if s:
                    then(nc.vector.tensor_tensor(w_scaled[:, 0], w_scaled[:, 0], w_scaled[:, s], ALU.add))
            dve.wait_ge(scaled_pool, 4)
            nc.vector.tensor_tensor(w_fold[:, 0:CENTER_CHUNKS], w_scaled[:, 0], w_scaled[:, 3], ALU.add)\
                .then_inc(folded, 1)

            def statistics(k, p, base, known):
                dve.wait_ge(pix_in[p], 8 * (k - p) + 16)
                tile = pix[:, p, :]
                own = tile[:, 0:CENTER].rearrange("t (r c) -> t r c", r=PATCH)
                for h in range(2):
                    nc.vector.bn_stats(bn_c[:, p, h * BN:(h + 1) * BN], tile[:, h * CENTER // 2:(h + 1) * CENTER // 2])\
                        .then_inc(dve_step, 1)
                nc.vector.bn_stats(bn_h[:, p, :], tile[:, CENTER:FEATURES]).then_inc(dve_step, 1)
                nc.vector.bn_stats(bn_e[:, p, 0:BN], own[:, 0:PATCH:PATCH - 1, :]).then_inc(dve_step, 1)
                nc.vector.bn_stats(bn_e[:, p, BN:2 * BN], own.rearrange("t r (w c) -> t r w c", c=CHANNELS)
                                   [:, :, 0:PATCH:PATCH - 1, :]).then_inc(pix_used, 1)
                dve.wait_ge(dve_step, base + 4)
                dve.wait_ge(pix_used, k + 1)
                if known is None or known >= 1:
                    nc.vector.tensor_copy(mv[:, k - 1], mv_k[:, 1 - p]).then_inc(dve_step, 1)
                nc.vector.bn_aggr(mv_k[:, p, 0], bn_c[:, p, :]).then_inc(dve_step, 1)
                nc.vector.bn_aggr(mv_k[:, p, 1], bn_h[:, p, :]).then_inc(dve_step, 1)
                nc.vector.bn_aggr(mv_k[:, p, 2], bn_e[:, p, :]).then_inc(dve_step, 1)

            base = steps[0]
            for k in range(2):
                statistics(k, k, max(8 * k - 1, 0) + base, k)
            with dve.Fori(1, PAIRS // 2) as pair:
                k = pair * 2
                statistics(k, 0, k * 8 + (base - 1), None)
                statistics(k + 1, 1, k * 8 + (base + 7), None)
            steps[0] += 8 * PAIRS - 1
            dve.wait_ge(dve_step, steps[0])
            then(nc.vector.tensor_copy(mv[:, PAIRS - 1], mv_k[:, 1]))
            m_c, v_c = mv[:, :, 0, 0], mv[:, :, 0, 1]
            m_h, v_h = mv[:, :, 1, 0], mv[:, :, 1, 1]
            m_e, v_e = mv[:, :, 2, 0], mv[:, :, 2, 1]
            d_h, d_e, d, nmean, var = (stat[:, j, :] for j in range(5))
            share = HALO / COPIED
            then(nc.vector.tensor_tensor(d_h, m_h, m_c, ALU.subtract))
            then(nc.vector.tensor_tensor(d_e, m_e, m_c, ALU.subtract))
            then(nc.vector.tensor_tensor(d, m_h, m_e, ALU.subtract))
            then(nc.vector.scalar_tensor_tensor(out=nmean, in0=d, scalar=-share, in1=m_c,
                                                op0=ALU.mult, op1=ALU.subtract))
            then(nc.vector.tensor_tensor(d_h, d_h, d_h, ALU.mult))
            then(nc.vector.tensor_tensor(d_e, d_e, d_e, ALU.mult))
            then(nc.vector.tensor_tensor(d_h, d_h, v_h, ALU.add))
            then(nc.vector.tensor_tensor(d_e, d_e, v_e, ALU.add))
            then(nc.vector.tensor_tensor(d_h, d_h, d_e, ALU.subtract))
            then(nc.vector.scalar_tensor_tensor(out=var, in0=d_h, scalar=share, in1=v_c, op0=ALU.mult, op1=ALU.add))
            then(nc.vector.tensor_scalar(d, d, share, None, ALU.mult))
            then(nc.vector.tensor_tensor(d, d, d, ALU.mult))
            then(nc.vector.tensor_tensor(var, var, d, ALU.subtract))
            nc.vector.tensor_scalar(stat[:, 6, :], var, 1e-3, None, ALU.add).then_inc(var_ready, 1)
            dve.wait_ge(rstd_ready, 1)
            dve.wait_ge(sums_out, 2)

            dve.wait_ge(w_hi_ready, 3 * BLOCKS)
            for b in range(BLOCKS):
                for whole, parts in ((w_qk, w_qk16), (w_v, w_v16), (w_p, w_p16)):
                    nc.vector.scalar_tensor_tensor(out=parts[:, b, 1], in0=whole[:, b], scalar=A_SCALE,
                                                   in1=parts[:, b, 0], op0=ALU.mult, op1=ALU.subtract)\
                        .then_inc(w_lo_ready, 1)

            def finish(k):
                dve.wait_ge(emb_raw, k + 1)
                nc.vector.scalar_tensor_tensor(out=raw[:, k, :], in0=colsum[:, :], scalar=stat[:, 3:4, k],
                                               in1=raw[:, k, :], op0=ALU.mult, op1=ALU.add).then_inc(dve_step, 1)
                dve.wait_ge(dve_step, k + 1 + steps[0])
                nc.vector.scalar_tensor_tensor(out=raw[:, k, :], in0=raw[:, k, :], scalar=stat[:, 7:8, k],
                                               in1=bias_all[:, :], op0=ALU.mult, op1=ALU.add).then_inc(emb_done, 1)

            with dve.Fori(0, PAIRS // 2) as pair:
                k = pair * 2
                finish(k)
                finish(k + 1)
            steps[0] += PAIRS

            def experts(i, p):
                base = 4 * i
                nc.vector.max(best[:, p], logit[:, p]).then_inc(route_step, 1)
                dve.wait_ge(route_step, base + 1)
                nc.vector.tensor_tensor(gap[:, p], best[:, p, 1:2], best[:, p, 0:1], ALU.subtract).then_inc(gap_ready, 1)
                nc.vector.max_index(best_at[:, p], best[:, p], logit[:, p]).then_inc(route_step, 1)
                dve.wait_ge(route_step, base + 2)
                nc.vector.tensor_copy(chosen[:, p], best_at[:, p, 0:TOP]).then_inc(route_step, 1)
                dve.wait_ge(route_step, base + 3)
                nc.vector.tensor_tensor(mask[:, p], iota[:, :, :], chosen[:, p].unsqueeze(2)
                                        .to_broadcast([SEQ, TOP, EXPERTS]), ALU.is_equal).then_inc(route_step, 1)
                dve.wait_ge(route_step, base + 4)
                nc.vector.tensor_tensor(hits[:, p], mask[:, p, 0], mask[:, p, 1], ALU.add).then_inc(hits_ready, 1)

            def place_rows(i, p, known):
                dve.wait_ge(rank_read, 2 * i + 2)
                nc.vector.tensor_tensor(placed[:, p], mask[:, p], place[:, p].unsqueeze(1)
                                        .to_broadcast([SEQ, TOP, EXPERTS]), ALU.mult).then_inc(place_step, 1)
                dve.wait_ge(egap_ready, i + 1)
                nc.vector.tensor_scalar(esum[:, p], egap[:, p], 1.0, None, ALU.add).then_inc(place_step, 1)
                dve.wait_ge(place_step, 4 * i + 1)
                nc.vector.tensor_reduce(slot_f[:, p], placed[:, p], AX.X, ALU.add).then_inc(place_step, 1)
                if known is None or known >= 2:
                    dve.wait_ge(scattered[p], 16 * (i - p))
                dve.wait_ge(place_step, 4 * i + 2)
                nc.vector.reciprocal(rows[:, p, 0, DIM:DIM + 1], esum[:, p]).then_inc(place_step, 1)
                dve.wait_ge(place_step, 4 * i + 4)
                nc.vector.tensor_tensor(rows[:, p, 1, DIM:DIM + 1], rows[:, p, 0, DIM:DIM + 1], egap[:, p], ALU.mult)\
                    .then_inc(slot_step, 1)
                nc.vector.tensor_copy(rows[:, p, :, DIM + 1].bitcast(U32), dest[:, :]).then_inc(slot_step, 1)
                nc.vector.tensor_copy(slot[:, p], slot_f[:, p]).then_inc(slot_step, 1)
                dve.wait_ge(slot_step, 3 * i + 3)
                nc.vector.tensor_scalar(dest[:, :], dest[:, :], float(SEQ), None, ALU.add).then_inc(slots_ready, 1)

            dve.wait_ge(emb_moved[0], 16 * PAIRS)
            dve.wait_ge(emb_moved[1], 16 * PAIRS)
            dve.wait_ge(text_in, 16)
            dve.wait_ge(mpad_zero, 5)
            dve.wait_ge(consts, CONSTS)
            dve.wait_ge(route_in, 16 * ROUTE_LOADS)

            def step(block, n, p, known):
                base = block * IMAGES
                stt = nc.vector.scalar_tensor_tensor
                if runs(known, 0):
                    if block == 0:
                        dve.wait_ge(aT_hi_ready, n + 1)
                        nc.vector.tensor_tensor(aT[:, p, 1], ps_a[0:KC, 0:CHUNKS * SEQ]
                                                .rearrange("k (c s) -> k c s", c=CHUNKS),
                                                aT[:, p, 0], ALU.subtract).then_inc(aT_ready, 1)
                    else:
                        dve.wait_ge(a32_ready, n + 1)
                        nc.vector.tensor_copy(aT[:, p, 0], a32[:, p]).then_inc(aT_hi_ready, 1)
                        dve.wait_ge(aT_hi_ready, n + base + 1)
                        nc.vector.tensor_tensor(aT[:, p, 1], a32[:, p], aT[:, p, 0], ALU.subtract).then_inc(aT_ready, 1)
                if runs(known, 2):
                    dve.wait_ge(oT_hi_ready, n + base - 1)
                    nc.vector.tensor_tensor(oT[0:KC, 1], ps_o[0:KC, 0:CHUNKS * SEQ]
                                            .rearrange("k (c s) -> k c s", c=CHUNKS),
                                            oT[0:KC, 0], ALU.subtract).then_inc(oT_ready, 1)
                if runs(known, 0):
                    dve.wait_ge(qk_ready, n + base + 1)
                    of_q, of_k = (ps_q[:, a * GROUPS * SEQ:(a + 1) * GROUPS * SEQ]
                                  .rearrange("k (g s) -> k g s", g=GROUPS) for a in range(2))
                    stt(out=q_both[:, p], in0=hi[:, p, 0], scalar=slot_rows[:, 0:1], in1=of_q,
                        op0=ALU.mult, op1=ALU.add)
                    stt(out=k_low[:, p], in0=hi[:, p, 1], scalar=-1.0, in1=of_k,
                        op0=ALU.mult, op1=ALU.add).then_inc(parts_ready, 1)
                if runs(known, 0):
                    dve.wait_ge(v_ps, n + base + 1)
                    nc.vector.tensor_copy(v1[:, p, :, 0:HEAD], ps_v[0:SEQ, 0:DIM].rearrange("s (h d) -> s h d", h=HEADS))\
                        .then_inc(v_ready, 1)
                if runs(known, -1) and (known is None or known + base >= 1):
                    dve.wait_ge(norm_ready, n + base)
                if runs(known, 2):
                    dve.wait_ge(pr_ps, n + base - 1)
                    to = (stream, inner)[block][:, n - 2, :]
                    stt(out=to, in0=ps_o[0:SEQ, 0:DIM], scalar=1 / A_SCALE, in1=to,
                        op0=ALU.mult, op1=ALU.add).then_inc(att_done, 1)
                if runs(known, -1):
                    nc.vector.bn_stats(bn_x[:, 1 - p, :], stream[:, n + 1, :]).then_inc(bn_done, 1)
                    dve.wait_ge(bn_done, n + base + 2)
                if block and runs(known, 2):
                    dve.wait_ge(att_done, n + base - 1)
                if runs(known, 0):
                    dve.wait_ge(s_ps, n + base + 1)
                    nc.vector.tensor_reduce(mpad[:, p, :, :, HEAD].rearrange("q g r -> q r g"),
                                            ps_s[0:SEQ, :, 0:GROUPS * SEQ].rearrange("q r (g k) -> q r g k", g=GROUPS),
                                            AX.X, ALU.max, negate=True).then_inc(max_ready, 1)
                if runs(known, -1):
                    nc.vector.bn_aggr(mv_x[:, 1 - p, :], bn_x[:, 1 - p, :]).then_inc(stats_ready, 1)
                if block and runs(known, 2):
                    i = n - 2
                    nc.vector.bn_stats(bn_t[:, p, :], inner[:, i, :]).then_inc(bn_t_done, 1)
                    dve.wait_ge(bn_t_done, i + 1)
                    if known is None or known >= 4:
                        dve.wait_ge(kept, i - 1)
                if runs(known, 0):
                    dve.wait_ge(parts_ready, n + base + 1)
                    nc.vector.tensor_scalar(k_low[:, p], k_low[:, p], slot_rows[:, 1:2], slot_rows[:, 2:3],
                                            ALU.mult, ALU.add)
                    nc.vector.tensor_scalar(q_high[:, p], hi[:, p, 0], slot_rows[:, 1:2], None, ALU.mult)\
                        .then_inc(operands, 1)
                    dve.wait_ge(operands, n + base + 1)
                    dve.wait_ge(mT_ps, n + base + 1)
                    stt(out=qm[:, p], in0=ps_v[:, 0:GROUPS * SEQ].rearrange("k (g s) -> k g s", g=GROUPS),
                        scalar=1 / MAX_SCALE, in1=q_high[:, p], op0=ALU.mult, op1=ALU.add).then_inc(qm_ready, 1)
                if block and runs(known, 2):
                    nc.vector.bn_aggr(mv_t[:, p, :], bn_t[:, p, :]).then_inc(stats_t, 1)
                if runs(known, 1):
                    dve.wait_ge(av_ps, n + base)
                    av = ps_q[0:SEQ, 0:HEADS * (HEAD + 1)].rearrange("s (h d) -> s h d", h=HEADS)
                    nc.vector.reciprocal(rec[:, 1 - p], av[:, :, HEAD:HEAD + 1]).then_inc(rec_done, 1)
                    dve.wait_ge(rec_done, n + base)
                    nc.vector.tensor_tensor(o[:, 1 - p], av[:, :, 0:HEAD],
                                            rec[:, 1 - p].to_broadcast([SEQ, HEADS, HEAD]), ALU.mult)\
                        .then_inc(o_ready, 1)
                if block and runs(known, 4):
                    dve.wait_ge(rank_ps, n - 3)
                if block and runs(known, 3):
                    dve.wait_ge(logit_ps, n - 2)
                    nc.vector.tensor_copy(logit[:, 1 - p], ps_a[0:SEQ, LOGIT_AT:LOGIT_AT + EXPERTS])\
                        .then_inc(logit_read, 1)
                if block and runs(known, 4):
                    nc.vector.tensor_tensor(place[:, p], ps_a[0:SEQ, RANK_AT:RANK_AT + EXPERTS], region[:, :], ALU.add)\
                        .then_inc(rank_read, 1)
                if block and runs(known, 3):
                    dve.wait_ge(logit_read, n - 2)
                if block and runs(known, 4):
                    nc.vector.tensor_tensor(seen[:, 1 - p], seen[:, p], hits[:, p], ALU.add).then_inc(rank_read, 1)
                if block and runs(known, 3):
                    experts(n - 3, 1 - p)
                if block and runs(known, 4):
                    place_rows(n - 4, p, None if known is None else known - 4)

            def split(e):
                dve.wait_ge(hi_ready, e + 1)
                for whole, parts in ((w1_whole, w1_parts), (w2_whole, w2_parts)):
                    last = nc.vector.scalar_tensor_tensor(out=parts[:, e, 1], in0=whole[:, :, :], scalar=W_SCALE,
                                                          in1=parts[:, e, 0], op0=ALU.mult, op1=ALU.subtract)
                last.then_inc(lo_ready, 1)

            for b in range(BLOCKS):
                base = b * IMAGES
                if b:
                    dve.wait_ge(att_done, base)
                    dve.wait_ge(norm_ready, base)
                nc.vector.bn_stats(bn_x[:, 0, :], stream[:, 0, :]).then_inc(bn_done, 1)
                dve.wait_ge(bn_done, base + 1)
                nc.vector.bn_aggr(mv_x[:, 0, :], bn_x[:, 0, :]).then_inc(stats_ready, 1)
                pipeline(dve, lambda n, p, known: step(b, n, p, known), lag_of(b), None if b else split)

            count = [0]

            def then(instruction):
                count[0] += 1
                instruction.then_inc(table_step, 1)
                dve.wait_ge(table_step, count[0])

            dve.wait_ge(total_ps, 1)
            then(nc.vector.tensor_copy(cnt[:, :], ps_v[0:1, 0:EXPERTS]))
            nc.vector.tensor_copy(cnt_i[:, :], cnt[:, :]).then_inc(tables, 1)
            then(nc.vector.tensor_scalar(need[:, :], cnt[:, :], float(TILE - 1), None, ALU.add))
            then(nc.vector.tensor_copy(need_i[:, :], need[:, :]))
            then(nc.vector.tensor_scalar(need_i[:, :], need_i[:, :], 7, None, ALU.arith_shift_right))
            then(nc.vector.tensor_copy(need[:, :], need_i[:, :]))
            a, b = 0, 1
            then(nc.vector.tensor_copy(upto[:, a], need[:, :]))
            for d in (1, 2, 4):
                then(nc.vector.tensor_copy(upto[:, b, 0:d], upto[:, a, 0:d]))
                then(nc.vector.tensor_tensor(upto[:, b, d:], upto[:, a, d:], upto[:, a, 0:EXPERTS - d], ALU.add))
                a, b = b, a
            wide = [1, LISTED, EXPERTS]
            then(nc.vector.tensor_tensor(past[:, :, :], upto[:, a].unsqueeze(1).to_broadcast(wide),
                                         jota[:, :].unsqueeze(2).to_broadcast(wide), ALU.is_le))
            then(nc.vector.tensor_reduce(tile_e[:, :], past[:, :, :], AX.X, ALU.add))
            then(nc.vector.tensor_tensor(past[:, :, :], past[:, :, :], need[:, :].unsqueeze(1).to_broadcast(wide),
                                         ALU.mult))
            then(nc.vector.tensor_reduce(tile_s[:, :], past[:, :, :], AX.X, ALU.add))
            then(nc.vector.tensor_tensor(tile_l[:, :], jota[:, :], tile_s[:, :], ALU.subtract))
            then(nc.vector.tensor_scalar(tile_s[:, :], tile_e[:, :], float(EXPERTS), float(TILE), ALU.is_lt, ALU.mult))
            then(nc.vector.tensor_tensor(tile_l[:, :], tile_l[:, :], tile_s[:, :], ALU.mult))
            then(nc.vector.tensor_scalar(tile_s[:, :], tile_e[:, :], float(REGION), None, ALU.mult))
            then(nc.vector.tensor_tensor(tile_l[:, :], tile_l[:, :], tile_s[:, :], ALU.add))
            nc.vector.tensor_copy(row_i[:, :], tile_l[:, :]).then_inc(tables, 1)
            then(nc.vector.tensor_scalar(tile_e[:, :], tile_e[:, :], float(EXPERTS - 1), None, ALU.min))
            nc.vector.tensor_copy(expert_i[:, :], tile_e[:, :]).then_inc(tables, 1)
            for i, size in enumerate((W1_SIZE, W2_SIZE)):
                nc.vector.tensor_scalar(weights_i[:, i::2], tile_e[:, :], float(size), None, ALU.mult)\
                    .then_inc(tables, 1)

            for part in range(2):
                last = nc.vector.memset(xs[KC:KC + 1, :, part, :, :], 1.0 - part).then_inc(xs_ones, 1)

            def rows_in(j, p, known):
                dve.wait_ge(x_ps, j + 1)
                for c in range(CHUNKS):
                    last = nc.vector.tensor_scalar(x32[:, p, c], (ps_a, ps_v)[p][0:KC, c * TILE:(c + 1) * TILE],
                                                   affine[:, 1, 0, c:c + 1], affine[:, 1, 1, c:c + 1],
                                                   ALU.mult, ALU.add)
                last.then_inc(x32_ready, 1)
                if known is None or known >= 2:
                    dve.wait_ge(h_ps, j * HALVES + (HALVES - 2 * HALVES))
                dve.wait_ge(x32_ready, j + 1)
                nc.vector.tensor_copy(xs[0:KC, p, 0], x32[:, p]).then_inc(x_hi_ready, 1)
                dve.wait_ge(x_hi_ready, j + 1)
                nc.vector.tensor_tensor(xs[0:KC, p, 1], x32[:, p], xs[0:KC, p, 0], ALU.subtract).then_inc(x_ready, 1)

            def hidden_low(j, p, half):
                dve.wait_ge(h_hi_ready, j * HALVES + (half + 1))
                nc.vector.tensor_tensor(hs[:, p, 1, half], h32[:, p, half], hs[:, p, 0, half], ALU.subtract)\
                    .then_inc(h_ready, 1)

            def add_bias(j, p, known, expert):
                if known is None or known >= 2:
                    dve.wait_ge(ys_ready, j - 1)
                dve.wait_ge(y_ps, j + 1)
                nc.vector.scalar_tensor_tensor(out=y[:, p], in0=(ps_q, ps_o)[p][:, 0:DIM], scalar=1 / W_SCALE,
                                               in1=b2[:, expert, :], op0=ALU.mult, op1=ALU.add).then_inc(y_added, 1)

            def step(j, u, quad, known, expert):
                p = u % 2
                if known is None or known + 1 < TILES:
                    hidden_low(j + 1, 1 - p, 0)
                if known is None or known + 2 < TILES:
                    rows_in(j + 2, p, None if known is None else known + 2)
                if known is None or known + 1 < TILES:
                    hidden_low(j + 1, 1 - p, 1)
                add_bias(j, p, known, expert[0])

            dve.wait_ge(tables, 5)
            dve.wait_ge(b2_in, 16)
            rows_in(0, 0, 0)
            hidden_low(0, 0, 0)
            rows_in(1, 1, 1)
            hidden_low(0, 0, 1)
            tiles(dve, step, expert_i, (EXPERTS - 1,))

            dve.wait_ge(res_done, IMAGES)
            for c in range(IMAGES // COMBINE):
                dve.wait_ge(got_in[c % 2], 32 * (c // 2 + 1))
                to = stream[:, c * COMBINE:(c + 1) * COMBINE, :]
                nc.vector.tensor_tensor(to, to, got[:, c % 2, 0], ALU.add).then_inc(summing, 1)
                dve.wait_ge(summing, c + 1)
                nc.vector.tensor_tensor(to, to, got[:, c % 2, 1], ALU.add).then_inc(summed, 1)

        @block.tensor
        def _(pe):
            pe.wait_ge(small_in, 48)
            pe.wait_ge(w_in, 32)
            pe.wait_ge(consts, 5)
            row = ps_o[0:1, 0:DIM]
            for s in range(SHIFTS):
                for c in range(CENTER_CHUNKS):
                    j = s * CENTER_CHUNKS + c
                    pe.matmul(row, shift[:, j:j + 1], w_center[:, s, c, :], start=(j == 0), stop=False)
            for c in range(2):
                j = SHIFTS * CENTER_CHUNKS + c
                pe.matmul(row, shift[:, j:j + 1], w_halo[:, c, :], start=False, stop=False)
            pe.matmul(row, ones[0:1, 0:1], b_row[:, :], start=False, stop=True).then_inc(bias_ps, 1)
            pe.wait_ge(folded, 1)
            for c in range(FEATURE_CHUNKS):
                pe.matmul(ps_v[0:PAIR, 0:DIM], ones[0:KC, 0:PAIR], w_fold[:, c, :],
                          start=(c == 0), stop=(c == FEATURE_CHUNKS - 1))
            pe.wait_ge(bias_out, 1)
            pe.matmul(ps_v[0:PAIR, DIM:2 * DIM], ones[0:1, 0:PAIR], bias_row[:, :], start=True, stop=True)\
                .then_inc(sums_ps, 1)

            def embed(k, p, known):
                pe.wait_ge(pixT_in[p], 8 * (k - p) + 16)
                if known is None or known >= 2:
                    pe.wait_ge(emb_raw, k - 1)
                for c in range(FEATURE_CHUNKS):
                    last = pe.matmul((ps_q, ps_a)[p][0:PAIR, 0:DIM], pixT[:, p, c, :], w_fold[:, c, :],
                                     start=(c == 0), stop=(c == FEATURE_CHUNKS - 1))
                last.then_inc(emb_ps, 1)

            for k in range(2):
                embed(k, k, k)
            with pe.Fori(1, PAIRS // 2) as pair:
                k = pair * 2
                embed(k, 0, None)
                embed(k + 1, 1, None)
            pe.wait_ge(attn_in, ATTN_LOADS)
            pe.wait_ge(emb_raw, PAIRS)
            pe.wait_ge(sums_out, 2)
            pe.wait_ge(mpad_zero, 5)

            def heads():
                for g in range(GROUPS):
                    for r in range(ROWS):
                        yield g, r

            parts = [(w, x, c) for c in range(CHUNKS) for w in range(2) for x in range(2 - w)]

            def step(block, n, p, known):
                base = block * IMAGES
                q = 1 - p
                if runs(known, 0):
                    pe.wait_ge(xn_ready, n + base + 1)
                    if known is None or known + base >= 1:
                        pe.wait_ge(aT_ready, n + base)
                    if block and (known is None or known >= 4):
                        pe.wait_ge(logit_read, n - 3)
                    if block and (known is None or known >= 5):
                        pe.wait_ge(rank_read, 2 * (n - 4))
                    for c in range(CHUNKS):
                        last = pe.transpose(ps_a[0:KC, c * SEQ:(c + 1) * SEQ], xn[:, p, c * KC:(c + 1) * KC],
                                            ident[0:SEQ, 0:SEQ])
                    last.then_inc(aT_ps, 1)
                if runs(known, 1):
                    pe.wait_ge(qm_ready, n + base)
                    for g, r in heads():
                        rows_ = slice(SLOT * r, SLOT * (r + 1))
                        pe.matmul(ps_s[0:SEQ, r, g * SEQ:(g + 1) * SEQ], hi[rows_, q, 1, g, :],
                                  q_both[rows_, q, g, :], start=True, stop=False)
                        last = pe.matmul(ps_s[0:SEQ, r, g * SEQ:(g + 1) * SEQ], k_low[rows_, q, g, :],
                                         qm[rows_, q, g, :], start=False, stop=True)
                    last.then_inc(st_ps, 1)
                if runs(known, 2):
                    pe.wait_ge(o_ready, n + base - 1)
                    if known is None or known + base >= 3:
                        pe.wait_ge(att_done, n + base - 2)
                    for c in range(CHUNKS):
                        last = pe.transpose(ps_o[0:KC, c * SEQ:(c + 1) * SEQ],
                                            o[:, p].rearrange("s h d -> s (h d)")[:, c * KC:(c + 1) * KC],
                                            ident[0:SEQ, 0:SEQ])
                    last.then_inc(oT_ps, 1)
                if runs(known, 0):
                    pe.wait_ge(aT_ready, n + base + 1)
                    if known is None or known + base >= 2:
                        pe.wait_ge(o_ready, n + base - 1)
                    for a in range(2):
                        for g in range(GROUPS):
                            for i, (w, x, c) in enumerate(parts):
                                last = pe.matmul(ps_q[:, (a * GROUPS + g) * SEQ:(a * GROUPS + g + 1) * SEQ],
                                                 w_qk16[:, block, w, c, a, g, :], aT[:, p, x, c, :],
                                                 start=(i == 0), stop=(i == len(parts) - 1))
                    last.then_inc(qk_ps, 1)
                    if known is None or known + base >= 1:
                        pe.wait_ge(qm_ready, n + base)
                    for i, (x, w, c) in enumerate(parts):
                        last = pe.matmul(ps_v[0:SEQ, 0:DIM], aT[:, p, x, c, :], w_v16[:, block, w, c, :],
                                         start=(i == 0), stop=(i == len(parts) - 1))
                    last.then_inc(v_ps, 1)
                if runs(known, 2):
                    pe.wait_ge(oT_ready, n + base - 1)
                    for i, (x, w, c) in enumerate(parts):
                        k = KC + 1 - c
                        last = pe.matmul(ps_o[0:SEQ, 0:DIM], oT[0:k, x, c, :], w_p16[0:k, block, w, c, :],
                                         start=(i == 0), stop=(i == len(parts) - 1))
                    last.then_inc(pr_ps, 1)
                if runs(known, 0):
                    pe.wait_ge(qk_ready, n + base + 1)
                    if known is None or known + base >= 1:
                        pe.wait_ge(p_ready, n + base)
                    for g, r in heads():
                        last = pe.matmul(ps_s[0:SEQ, r, g * SEQ:(g + 1) * SEQ],
                                         hi[SLOT * r:SLOT * r + HEAD, p, 0, g, :],
                                         hi[SLOT * r:SLOT * r + HEAD, p, 1, g, :], start=True, stop=True)
                    last.then_inc(s_ps, 1)
                if block and runs(known, 3):
                    pe.wait_ge(xh_ready, n - 2)
                    if known is not None and known >= IMAGES:
                        if known - 4 < IMAGES:
                            pe.wait_ge(logit_read, n - 3)
                        if known - 5 < IMAGES:
                            pe.wait_ge(rank_read, 2 * (n - 4))
                    for c in range(CHUNKS):
                        last = pe.transpose(ps_a[0:KC, c * SEQ:(c + 1) * SEQ], xh[:, q, c * KC:(c + 1) * KC],
                                            ident[0:SEQ, 0:SEQ])
                    last.then_inc(tT_ps, 1)
                for j, (g, r) in enumerate(heads()):
                    if j == 8 and runs(known, 0):
                        pe.wait_ge(max_ready, n + base + 1)
                        pe.wait_ge(v_ready, n + base + 1)
                        for gg in range(GROUPS):
                            last = pe.transpose(ps_v[:, gg * SEQ:(gg + 1) * SEQ],
                                                mpad[:, p, gg].rearrange("q r d -> q (r d)"), ident[0:SEQ, 0:SEQ])
                        last.then_inc(mT_ps, 1)
                    if not runs(known, 1):
                        continue
                    if j == 0:
                        pe.wait_ge(p_ready, n + base)
                        pe.wait_ge(v_ready, n + base)
                        if known is None or known < IMAGES:
                            pe.wait_ge(parts_ready, n + base + 1)
                        else:
                            pe.wait_ge(parts_ready, base + IMAGES)
                    h = ROWS * g + r
                    last = pe.matmul(ps_q[0:SEQ, h * (HEAD + 1):(h + 1) * (HEAD + 1)], probs[:, q, r, g, :],
                                     v1[:, q, h, :], start=True, stop=True)
                if runs(known, 1):
                    last.then_inc(av_ps, 1)

                if block and runs(known, 3):
                    pe.wait_ge(tT_ready, n - 2)
                    for c in range(CHUNKS):
                        k = KC + 1 - c
                        last = pe.matmul(ps_a[0:SEQ, LOGIT_AT:LOGIT_AT + EXPERTS], tT[0:k, c, :], w_gate[0:k, c, :],
                                         start=(c == 0), stop=(c == CHUNKS - 1))
                    last.then_inc(logit_ps, 1)
                if block and runs(known, 4):
                    i = n - 4
                    if known is not None and known - 3 >= IMAGES:
                        pe.wait_ge(logit_read, IMAGES)
                        pe.wait_ge(rank_read, 2 * i)
                    pe.wait_ge(hits_ready, i + 1)
                    if known is None or known >= 5:
                        pe.wait_ge(rank_read, 2 * i)
                    rank = ps_a[0:SEQ, RANK_AT:RANK_AT + EXPERTS]
                    pe.matmul(rank, before[:, :], hits[:, p], start=True, stop=False)
                    pe.matmul(rank, ones[0:SEQ, 0:SEQ], seen[:, p], start=False, stop=True).then_inc(rank_ps, 1)

            pe.wait_ge(route_in, 16 * ROUTE_LOADS)
            pe.wait_ge(consts, CONSTS)
            for b in range(BLOCKS):
                pe.wait_ge(w_lo_ready, 3 * BLOCKS)
                pipeline(pe, lambda n, p, known: step(b, n, p, known), lag_of(b))
            pe.wait_ge(rank_read, 2 * IMAGES)
            pe.matmul(ps_v[0:1, 0:EXPERTS], ones[0:SEQ, 0:1], seen[:, 0], start=True, stop=True).then_inc(total_ps, 1)

            def rows_in(j, u, quad, known):
                p = u % 2
                if known is None or known >= 2:
                    pe.wait_ge(x32_ready, j - 1)
                pe.wait_ge(picked_in[u], quad * 16 + 16)
                for c in range(CHUNKS):
                    last = pe.transpose((ps_a, ps_v)[p][0:KC, c * TILE:(c + 1) * TILE],
                                        picked[:, u, c * KC:(c + 1) * KC], ident[:, :])
                last.then_inc(x_ps, 1)

            def up(j, p, known, first):
                pe.wait_ge(x_ready, j + 1)
                for half in range(HALVES):
                    if known is None or known >= 2:
                        pe.wait_ge(h32_ready, j * HALVES + (half + 1 - 2 * HALVES))
                    for m in range(PER_HALF):
                        steps = [(w, x, c) for c in range(CHUNKS) for w in range(2) for x in range(2 - w)]
                        for i, (w, x, c) in enumerate(steps):
                            k = KC + 1 - c
                            at = (w * CHUNKS + c) * HIDDEN + (half * PER_HALF + m) * 128
                            last = pe.matmul(ps_s[:, 2 * p + half, m * TILE:(m + 1) * TILE],
                                             w1[0:k, bass.ds(first + at, 128)], xs[0:k, p, x, c, :],
                                             start=(i == 0), stop=(i == len(steps) - 1))
                    last.then_inc(h_ps, 1)

            def down(j, p, known, first):
                if known is None or known >= 2:
                    pe.wait_ge(y_added, j - 1)
                for half in range(HALVES):
                    pe.wait_ge(h_ready, j * HALVES + (half + 1))
                    for m in range(PER_HALF):
                        for i, (h, w) in enumerate(((1, 0), (0, 0), (0, 1))):
                            at = (w * HIDDEN_CHUNKS + half * PER_HALF + m) * DIM
                            last = pe.matmul((ps_q, ps_o)[p][:, 0:DIM], hs[:, p, h, half, m, :],
                                             w2[:, bass.ds(first + at, DIM)],
                                             start=(half == m == i == 0),
                                             stop=(half == HALVES - 1 and m == PER_HALF - 1 and i == 2))
                last.then_inc(y_ps, 1)

            def step(j, u, quad, known, first):
                if known is None or known + 1 < TILES:
                    up(j + 1, (u + 1) % 2, None if known is None else known + 1, first[2])
                if known is None or known + 2 < TILES:
                    v = (u + 2) % SLOTS
                    rows_in(j + 2, v, quad + (u + 2) // SLOTS, None if known is None else known + 2)
                down(j, u % 2, known, first[1])

            pe.wait_ge(tables, 5)
            pe.wait_ge(lo_ready, EXPERTS)
            pe.wait_ge(xs_ones, 2)
            rows_in(0, 0, 0, 0)
            up(0, 0, 0, pe.value_load(weights_i[0:1, 0:1], min_val=0, max_val=W1_SIZE * (EXPERTS - 1)))
            rows_in(1, 1, 0, 1)
            tiles(pe, step, weights_i, (W1_SIZE * (EXPERTS - 1), W2_SIZE * (EXPERTS - 1)))


def _inputs(inputs):
    import numpy as np

    f = np.float32
    x = np.asarray(inputs["x"])
    side = x.shape[1]
    framed = np.zeros((IMAGES, side + 2, side + 2, CHANNELS), x.dtype)
    framed[:, 1:-1, 1:-1] = x
    r = PATCH
    rows = {}
    tokens = []
    for i in range(SIDE):
        for j in range(SIDE):
            win = framed[:, r * i:r * i + r + 2, r * j:r * j + r + 2]
            tokens.append(np.concatenate([win[:, 1:-1, 1:-1].reshape(IMAGES, -1), win[:, 0, 1:-1].reshape(IMAGES, -1),
                                          win[:, -1, 1:-1].reshape(IMAGES, -1), win[:, 1:-1, 0].reshape(IMAGES, -1),
                                          win[:, 1:-1, -1].reshape(IMAGES, -1)], axis=1))
    pix = np.stack(tokens, 1).reshape(PAIRS, PAIR, FEATURES)
    pixT = pix.reshape(PAIRS, PAIR, FEATURE_CHUNKS, KC).transpose(0, 3, 2, 1)

    def by_source(a):
        a = a.reshape(r, r, SHIFTS, CHANNELS, -1)
        n = a.shape[-1]
        own = np.zeros((SHIFTS, r, r, CHANNELS, n), a.dtype)
        own[0] = a[:, :, 0]
        own[1][:, :-1] = a[:, 1:, 1]
        own[2][:, 1:] = a[:, :-1, 2]
        own[3][:-1] = a[1:, :, 3]
        own[4][1:] = a[:-1, :, 4]
        halo = np.concatenate([x.reshape(-1, n) for x in (a[0, :, 3], a[-1, :, 4], a[:, 0, 1], a[:, -1, 2])])
        return (own.reshape(SHIFTS, CENTER_CHUNKS, KC, n).transpose(2, 0, 1, 3), halo.reshape(2, KC, n).transpose(1, 0, 2))

    w_center, w_halo = by_source(np.asarray(inputs["L0_tok_W"]))

    def per_feature(a):
        own, halo = by_source(np.asarray(a).reshape(-1, 1))
        return np.concatenate([own.reshape(KC, -1), halo.reshape(KC, -1)], axis=1)

    def chunked(w):
        return w.reshape(-1, KC, w.shape[-1]).transpose(1, 0, 2)

    def attention(w_qkv, w_proj, b_proj):
        w = np.asarray(w_qkv)
        qk = np.zeros((DIM, 2, GROUPS, ROWS, SLOT), w.dtype)
        for copy in range(SLOT // HEAD):
            qk[..., copy * HEAD:(copy + 1) * HEAD] = w[0:2 * DIM].T.reshape(DIM, 2, GROUPS, ROWS, HEAD)
        p = np.zeros((KC + 1, CHUNKS, DIM), w.dtype)
        p[0:KC] = chunked(np.asarray(w_proj).T)
        p[KC, 0] = np.asarray(b_proj)
        return qk.reshape(CHUNKS, KC, 2, GROUPS, 128).transpose(1, 0, 2, 3, 4), chunked(w[2 * DIM:].T), p

    arrays = {"pix": pix, "pixT": pixT, "w_center": w_center, "w_halo": w_halo,
              "gain": per_feature(inputs["L0_tok_gamma"]), "shift": per_feature(inputs["L0_tok_beta"]),
              "tok_b": np.asarray(inputs["L0_tok_b"]).reshape(1, DIM),
              "txt": np.asarray(inputs["txt"]).transpose(1, 0, 2)}
    blocks = [attention(*(inputs[n] for n in names)) for names in (
        ("L0_attn_w_qkv", "L0_attn_w_proj", "L0_attn_b_proj"), ("L0_ffn_qkv_w", "L0_ffn_proj_w", "L0_ffn_proj_b"))]
    for name, parts in zip(("qk", "v", "p"), zip(*blocks)):
        arrays[name] = np.stack(parts)

    def with_bias(w, b):
        out = np.zeros((*w.shape[:-2], KC + 1, CHUNKS, w.shape[-1]), w.dtype)
        out[..., 0:KC, :, :] = w.reshape(*w.shape[:-2], CHUNKS, KC, w.shape[-1]).swapaxes(-3, -2)
        out[..., KC, 0, :] = b
        return out

    arrays["affine"] = np.stack([np.stack([np.asarray(inputs[f"L0_ffn_ln{i}_{x}"]).reshape(CHUNKS, KC).T for x in "gb"], 1)
                                 for i in (1, 2)], 1)
    arrays["gate"] = with_bias(np.asarray(inputs["L0_ffn_gate_w"]).T, np.asarray(inputs["L0_ffn_gate_b"]))
    arrays["e1"] = with_bias(np.asarray(inputs["L0_ffn_w1"]).swapaxes(1, 2), np.asarray(inputs["L0_ffn_b1"]))
    arrays["e2"] = np.asarray(inputs["L0_ffn_w2"]).swapaxes(1, 2).reshape(EXPERTS, HIDDEN_CHUNKS, 128, DIM)\
        .transpose(0, 2, 1, 3)
    arrays["eb"] = np.asarray(inputs["L0_ffn_b2"]).reshape(1, EXPERTS, DIM)
    arrays["before"] = np.triu(np.ones((SEQ, SEQ), f), 1)
    arrays["iota"] = np.broadcast_to(np.arange(EXPERTS, dtype=f), (SEQ, TOP, EXPERTS))
    arrays["region"] = np.broadcast_to(np.arange(EXPERTS, dtype=f) * REGION, (SEQ, EXPERTS))
    arrays["dest"] = np.arange(SEQ, dtype=f)[:, None] + np.arange(TOP, dtype=f) * TOKENS
    pad = np.zeros((TILE, ROW), f)
    pad.view(np.uint32)[:, DIM + 1] = NOWHERE
    arrays["padding"] = pad
    row = np.arange(128) % SLOT
    arrays["slot_rows"] = np.stack([-(row >= HEAD).astype(f), (row < HEAD).astype(f), MAX_SCALE * (row == HEAD)], 1)\
        .astype(f)
    arrays["jota"] = np.arange(LISTED, dtype=f)[None]
    return {k: np.ascontiguousarray(v) for k, v in arrays.items()}


def kernel(**inputs):
    import concourse.bacc as _bacc
    from concourse.bass_utils import run_bass_kernel_spmd as _run

    nc = _bacc.Bacc("TRN2", target_bir_lowering=False, num_devices=1)
    arrays = _inputs(inputs)
    tensors = {name: nc.dram_tensor("in_" + name, a.shape, mybir.dt.from_np(a.dtype), kind="ExternalInput").ap()
               for name, a in arrays.items()}
    tensors["out"] = nc.dram_tensor("out", (IMAGES, SEQ, DIM), F32, kind="ExternalOutput").ap()
    tensors["routed"] = nc.dram_tensor("routed", (EXPERTS * REGION + TILE, ROW), F32, kind="Internal").ap()
    tensors["results"] = nc.dram_tensor("results", (TOP * TOKENS, DIM), F32, kind="Internal").ap()
    build(nc, tensors)
    r = _run(nc, [{"in_" + name: a for name, a in arrays.items()}], core_ids=[0])
    return r.results[0]["out"]
```

```python
from contextlib import ExitStack

import concourse.bass as bass
from concourse import mybir

ALU = mybir.AluOpType
ACT = mybir.ActivationFunctionType
AX = mybir.AxisListType
F32 = mybir.dt.float32
F16 = mybir.dt.float16
U32 = mybir.dt.uint32
I32 = mybir.dt.int32

IMAGES = 32
SIDE = 7
PATCHES = SIDE * SIDE
TEXT = 32
SEQ = PATCHES + TEXT
DIM = 192
KC = 96
CHUNKS = DIM // KC
HEADS = 12
HEAD = DIM // HEADS
ROWS = 4
GROUPS = HEADS // ROWS
SLOT = 32

PATCH = 16
CHANNELS = 3
CENTER = PATCH * PATCH * CHANNELS
HALO = 4 * PATCH * CHANNELS
FEATURES = CENTER + HALO
SHIFTS = 5
COPIED = SHIFTS * CENTER
CENTER_CHUNKS = CENTER // KC
FEATURE_CHUNKS = FEATURES // KC
PAIR = 2 * PATCHES
PAIRS = IMAGES // 2
BN = 6

EXPERTS = 8
TOP = 2
HIDDEN = 768
HIDDEN_CHUNKS = HIDDEN // 128
TOKENS = IMAGES * SEQ
TILE = 128
REGION = TOKENS + TILE
TILES = (TOP * TOKENS + EXPERTS * (TILE - 1)) // TILE
ROW = DIM + 2
NOWHERE = 1 << 20
LOGIT_AT, RANK_AT, MAX_AT = 200, 216, 224
BLOCKS = 2
ARRIVAL = (0, 3, 1, 4, 2)
BEHIND = PAIRS - 3 * BLOCKS
MOVE_BEHIND = BEHIND + 2
EARLY = IMAGES - 4
ATTN_LOADS = 16 * (3 * BLOCKS + 1)
EPS = 1e-5
CONSTS = 6
ROUTE_LOADS = 8
SLOTS = 4
W1_SIZE = 2 * CHUNKS * HIDDEN
W2_SIZE = 2 * HIDDEN_CHUNKS * DIM
LISTED = TILES + 1
A_SCALE = 16.0
MAX_SCALE = 4096.0
AV = 2 * HEAD + 1
W_SCALE = 256.0
HALVES = 2
PER_HALF = HIDDEN_CHUNKS // HALVES
COMBINE = 8
DVE_SHARE = 6


def build(nc, t):
    with ExitStack() as ctx:
        def sb(name, shape, dt=F32):
            return ctx.enter_context(nc.sbuf_tensor(name, shape, dt))

        def sem(name):
            return ctx.enter_context(nc.semaphore(name))

        stream = sb("stream", [SEQ, IMAGES, DIM])
        ident = sb("ident", [128, 128])
        ones = sb("ones", [128, 128])
        half = sb("half", [128, PAIRS])
        minus_one = sb("minus_one", [128, 1])
        eps = sb("eps", [128, 1])
        tick = sb("tick", [1, 1])

        gain = sb("gain", [KC, SHIFTS * CENTER_CHUNKS + 2])
        shift = sb("shift", [KC, SHIFTS * CENTER_CHUNKS + 2])
        b_row = sb("b_row", [1, DIM])
        colsum = sb("colsum", [PAIR, DIM])
        bias_all = sb("bias_all", [PAIR, DIM])
        bn_c = sb("bn_c", [PAIR, 2, 2 * BN])
        bn_h = sb("bn_h", [PAIR, 2, BN])
        bn_e = sb("bn_e", [PAIR, 2, 2 * BN])
        mv_k = sb("mv_k", [PAIR, 2, 3, 2])
        mv = sb("mv", [PAIR, PAIRS, 3, 2])
        stat = sb("stat", [PAIR, 8, PAIRS])
        affine = sb("affine", [KC, 2, 2, CHUNKS])
        seen = sb("seen", [SEQ, 2, EXPERTS])

        padding = sb("padding", [TILE, ROW])
        cnt = sb("cnt", [1, EXPERTS])
        cnt_i = sb("cnt_i", [1, EXPERTS], I32)
        need = sb("need", [1, EXPERTS])
        need_i = sb("need_i", [1, EXPERTS], I32)
        upto = sb("upto", [1, 2, EXPERTS])
        jota = sb("jota", [1, LISTED])
        past = sb("past", [1, LISTED, EXPERTS])
        tile_e = sb("tile_e", [1, LISTED])
        tile_s = sb("tile_s", [1, LISTED])
        tile_l = sb("tile_l", [1, LISTED])
        expert_i = sb("expert_i", [1, LISTED], I32)
        row_i = sb("row_i", [1, LISTED], I32)
        weights_i = sb("weights_i", [1, 2 * LISTED], I32)

        with ExitStack() as embedding:
            def tmp(name, shape):
                return embedding.enter_context(nc.sbuf_tensor(name, shape, F32))

            w_center = tmp("w_center", [KC, SHIFTS, CENTER_CHUNKS, DIM])
            w_halo = tmp("w_halo", [KC, FEATURE_CHUNKS - CENTER_CHUNKS, DIM])
            w_fold = tmp("w_fold", [KC, FEATURE_CHUNKS, DIM])
            pix = tmp("pix", [PAIR, 2, FEATURES])
            pixT = tmp("pixT", [KC, 2, FEATURE_CHUNKS, PAIR])
            raw = tmp("raw", [PAIR, PAIRS, DIM])
            with nc.sbuf_tensor("w_scaled", [KC, SHIFTS, CENTER_CHUNKS, DIM], F32) as w_scaled:
                pass
            w_qk = tmp("w_qk", [KC, BLOCKS, CHUNKS, 2, GROUPS, 128])
            w_v = tmp("w_v", [KC, BLOCKS, CHUNKS, DIM])
            w_p = tmp("w_p", [KC + 1, BLOCKS, CHUNKS, DIM])

        w1 = sb("w1", [KC + 1, EXPERTS * W1_SIZE], F16)
        w2 = sb("w2", [TILE, EXPERTS * W2_SIZE], F16)
        w1_parts = w1[:, :].rearrange("k (e p c n) -> k e p c n", e=EXPERTS, p=2, c=CHUNKS)
        w2_parts = w2[:, :].rearrange("k (e p c n) -> k e p c n", e=EXPERTS, p=2, c=HIDDEN_CHUNKS)
        w1_whole = sb("w1_whole", [KC + 1, CHUNKS, HIDDEN])
        w2_whole = sb("w2_whole", [TILE, HIDDEN_CHUNKS, DIM])

        with ExitStack() as attention:
            def tmp(name, shape, dt=F32):
                return attention.enter_context(nc.sbuf_tensor(name, shape, dt))

            probs = tmp("probs", [SEQ, ROWS, GROUPS, SEQ])
            p_hi = tmp("p_hi", [SEQ, 2, ROWS, GROUPS, SEQ], F16)
            p_lo = tmp("p_lo", [SEQ, 2, ROWS, GROUPS, SEQ], F16)
            xn = tmp("xn", [SEQ, 2, DIM])
            w_qk16 = tmp("w_qk16", [KC, BLOCKS, 2, CHUNKS, 2, GROUPS, 128], F16)
            w_v16 = tmp("w_v16", [KC, BLOCKS, 2, CHUNKS, DIM], F16)
            w_p16 = tmp("w_p16", [KC + 1, BLOCKS, 2, CHUNKS, DIM], F16)
            slot_rows = tmp("slot_rows", [128, 3])
            bn_x = tmp("bn_x", [SEQ, 2, BN])
            mv_x = tmp("mv_x", [SEQ, 2, 2])
            veps = tmp("veps", [SEQ, 2, 1])
            rstd = tmp("rstd", [SEQ, 2, 1])
            nmr = tmp("nmr", [SEQ, 2, 1])
            mv2 = tmp("mv2", [SEQ, IMAGES, 2])
            rstd_b = tmp("rstd_b", [SEQ, IMAGES, 1])
            nmr_b = tmp("nmr_b", [SEQ, IMAGES, 1])
            scale2_b = tmp("scale2_b", [SEQ, IMAGES, 1])
            nmr2_b = tmp("nmr2_b", [SEQ, IMAGES, 1])
            work_b = tmp("work_b", [SEQ, IMAGES, 1])
            a32 = tmp("a32", [KC, CHUNKS, SEQ])
            aT = tmp("aT", [KC, 2, 2, CHUNKS, SEQ], F16)
            hi = tmp("hi", [128, 2, 2, GROUPS, SEQ], F16)
            q_both = tmp("q_both", [128, 2, GROUPS, SEQ], F16)
            k_low = tmp("k_low", [128, 2, GROUPS, SEQ], F16)
            q_high = tmp("q_high", [128, 2, GROUPS, SEQ], F16)
            values = tmp("values", [SEQ, 2, HEADS, AV], F16)
            o_sum = tmp("o_sum", [SEQ, 2, HEADS, HEAD])
            mpad = tmp("mpad", [SEQ, 2, GROUPS, ROWS, SLOT])
            qm = tmp("qm", [128, 2, GROUPS, SEQ], F16)
            rec = tmp("rec", [SEQ, 2, HEADS, 1])
            o = tmp("o", [SEQ, 2, HEADS, HEAD])
            oT = tmp("oT", [KC + 1, 2, CHUNKS, SEQ], F16)

            inner = tmp("inner", [SEQ, IMAGES, DIM])
            w_gate = tmp("w_gate", [KC + 1, CHUNKS, EXPERTS])
            bn_t = tmp("bn_t", [SEQ, 2, BN])
            mv_t = tmp("mv_t", [SEQ, 2, 2])
            rstd_t = tmp("rstd_t", [SEQ, IMAGES, 1])
            nmr_t = tmp("nmr_t", [SEQ, IMAGES, 1])
            rstd_s = tmp("rstd_s", [SEQ, 2, 1])
            mr_s = tmp("mr_s", [SEQ, 2, 1])
            nmr_s = tmp("nmr_s", [SEQ, 2, 1])
            veps_t = tmp("veps_t", [SEQ, 2, 1])
            xh = tmp("xh", [SEQ, 2, DIM])
            tT = tmp("tT", [KC + 1, CHUNKS, SEQ])
            before = tmp("before", [SEQ, SEQ])
            iota = tmp("iota", [SEQ, TOP, EXPERTS])
            region = tmp("region", [SEQ, EXPERTS])
            logit = tmp("logit", [SEQ, 2, EXPERTS])
            best = tmp("best", [SEQ, 2, 8])
            best_at = tmp("best_at", [SEQ, 2, 8], U32)
            chosen = tmp("chosen", [SEQ, 2, TOP])
            mask = tmp("mask", [SEQ, 2, TOP, EXPERTS])
            hits = tmp("hits", [SEQ, 2, EXPERTS])
            gap = tmp("gap", [SEQ, 2, 1])
            egap = tmp("egap", [SEQ, 2, 1])
            esum = tmp("esum", [SEQ, 2, 1])
            place = tmp("place", [SEQ, 2, EXPERTS])
            placed = tmp("placed", [SEQ, 2, TOP, EXPERTS])
            slot_f = tmp("slot_f", [SEQ, 2, TOP])
            slot = tmp("slot", [SEQ, 2, TOP], U32)
            dest = tmp("dest", [SEQ, TOP])
            rows = tmp("rows", [SEQ, 2, TOP, ROW])

        b2 = sb("b2", [TILE, EXPERTS, DIM])
        picked = sb("picked", [TILE, SLOTS, ROW])
        x32 = sb("x32", [KC, 2, CHUNKS, TILE])
        xs = sb("xs", [KC + 1, 2, 2, CHUNKS, TILE], F16)
        h32 = sb("h32", [TILE, 2, HALVES, PER_HALF, TILE])
        hs = sb("hs", [TILE, 2, 2, HALVES, PER_HALF, TILE], F16)
        y = sb("y", [TILE, 2, DIM])
        ys = sb("ys", [TILE, SLOTS, DIM])
        got = sb("got", [SEQ, 2, TOP, COMBINE, DIM])

        ps_s = ctx.enter_context(nc.psum_tensor("ps_s", [128, ROWS, 512], F32))
        ps_q = ctx.enter_context(nc.psum_tensor("ps_q", [128, 512], F32))
        ps_a = ctx.enter_context(nc.psum_tensor("ps_a", [128, 512], F32))
        ps_o = ctx.enter_context(nc.psum_tensor("ps_o", [128, 512], F32))
        ps_v = ctx.enter_context(nc.psum_tensor("ps_v", [128, 512], F32))

        consts = sem("consts")
        ident_zero = sem("ident_zero")
        mpad_zero = sem("mpad_zero")
        small_in = sem("small_in")
        halo_in = sem("halo_in")
        shift_in = [sem(f"shift_in{s}") for s in range(SHIFTS)]
        whole_scaled = sem("whole_scaled")
        finishing = sem("finishing")
        pix_in = [sem(f"pix_in{p}") for p in range(2)]
        pixT_in = [sem(f"pixT_in{p}") for p in range(2)]
        pix_used = sem("pix_used")
        attn_in = sem("attn_in")
        text_in = sem("text_in")
        scaled_pool = sem("scaled_pool")
        folded = sem("folded")
        offset_step = sem("offset_step")
        sums_ps = sem("sums_ps")
        sums_out = sem("sums_out")
        emb_ps = sem("emb_ps")
        emb_raw = sem("emb_raw")
        dve_step = sem("dve_step")
        var_ready = sem("var_ready")
        rstd_ready = sem("rstd_ready")
        emb_done = sem("emb_done")
        emb_moved = [sem(f"emb_moved{p}") for p in range(2)]
        moved_late = [sem(f"moved_late{p}") for p in range(2)]

        stats_ready = sem("stats_ready")
        pool_step = sem("pool_step")
        norm_ready = sem("norm_ready")
        mv2_ready = sem("mv2_ready")
        norms_ready = sem("norms_ready")
        xn_ready = sem("xn_ready")
        aT_ps = sem("aT_ps")
        a32_ready = sem("a32_ready")
        aT_hi_ready = sem("aT_hi_ready")
        oT_hi_ready = sem("oT_hi_ready")
        parts_ready = sem("parts_ready")
        operands = sem("operands")
        w_hi_ready = sem("w_hi_ready")
        w_lo_ready = sem("w_lo_ready")
        aT_ready = sem("aT_ready")
        qk_ps = sem("qk_ps")
        qk_ready = sem("qk_ready")
        v_ps = sem("v_ps")
        v_ready = sem("v_ready")
        s_ps = sem("s_ps")
        max_ready = sem("max_ready")
        mT_ps = sem("mT_ps")
        qm_ready = sem("qm_ready")
        st_ps = sem("st_ps")
        p_ready = sem("p_ready")
        p_lo_ready = sem("p_lo_ready")
        v_hi_ready = sem("v_hi_ready")
        av_ps = sem("av_ps")
        o_ready = sem("o_ready")
        oT_ps = sem("oT_ps")
        oT_ready = sem("oT_ready")
        pr_ps = sem("pr_ps")
        res_done = sem("res_done")

        bn_done = sem("bn_done")
        rec_done = sem("rec_done")
        route_in = sem("route_in")
        bn_t_done = sem("bn_t_done")
        stats_t = sem("stats_t")
        root_t = sem("root_t")
        inner_ready = sem("inner_ready")
        kept = sem("kept")
        xh_ready = sem("xh_ready")
        tT_ps = sem("tT_ps")
        tT_ready = sem("tT_ready")
        logit_ps = sem("logit_ps")
        rank_ps = sem("rank_ps")
        logit_read = sem("logit_read")
        rank_read = sem("rank_read")
        seen_ready = sem("seen_ready")
        route_step = sem("route_step")
        gap_ready = sem("gap_ready")
        egap_ready = sem("egap_ready")
        hits_ready = sem("hits_ready")
        rows_filled = sem("rows_filled")
        slots_ready = sem("slots_ready")
        place_step = sem("place_step")
        slot_step = sem("slot_step")
        att_done = sem("att_done")
        scattered = [sem(f"scattered{p}") for p in range(2)]
        total_ps = sem("total_ps")
        table_step = sem("table_step")
        tables = sem("tables")
        padded = sem("padded")
        b2_in = sem("b2_in")
        whole_in = sem("whole_in")
        hi_ready = sem("hi_ready")
        lo_ready = sem("lo_ready")
        picked_in = [sem(f"picked_in{u}") for u in range(SLOTS)]
        x_ps = sem("x_ps")
        x32_ready = sem("x32_ready")
        x_hi_ready = sem("x_hi_ready")
        x_ready = sem("x_ready")
        xs_ones = sem("xs_ones")
        h_ps = sem("h_ps")
        h32_ready = sem("h32_ready")
        h_hi_ready = sem("h_hi_ready")
        h_ready = sem("h_ready")
        y_ps = sem("y_ps")
        y_added = sem("y_added")
        ys_ready = sem("ys_ready")
        ticked = sem("ticked")
        ys_out = [sem(f"ys_out{u}") for u in range(SLOTS)]
        got_in = [sem(f"got_in{p}") for p in range(2)]
        summed_dve = sem("summed_dve")
        summed_pool = sem("summed_pool")
        summing_dve = sem("summing_dve")
        summing_pool = sem("summing_pool")
        out_done = sem("out_done")

        block = ctx.enter_context(nc.Block())

        def pipeline(eng, step, lags, split=None):
            first, last = lags + lags % 2, IMAGES - 2
            for n in range(first):
                step(n, n % 2, n)
            begin = first // 2
            if split:
                with eng.Fori(begin, begin + EXPERTS) as pair:
                    step(pair * 2, 0, None)
                    split(pair - begin)
                    step(pair * 2 + 1, 1, None)
                begin += EXPERTS
            with eng.Fori(begin, last // 2) as pair:
                step(pair * 2, 0, None)
                step(pair * 2 + 1, 1, None)
            for n in range(last, IMAGES + lags):
                step(n, n % 2, n)

        def tiles(eng, step, table=None, most=()):
            each = len(most)
            bounded = "the tables hold experts below EXPERTS, and rows of their regions or of the padding"

            def body(quad, known):
                values = ()
                if each:
                    loaded = nc.values_load_multi_w_load_instructions(
                        table[0:1, bass.ds(quad * (SLOTS * each), (SLOTS + 1) * each)], engines=(eng.engine,),
                        min_val=0, max_val=max(most), skip_runtime_bounds_check_because=bounded)[1]
                    values = [x if most[i % each] == max(most) else
                              nc.s_assert_within(x, 0, most[i % each],
                                                 skip_runtime_bounds_check_because=bounded)
                              for i, x in enumerate(loaded)]
                for u in range(SLOTS):
                    step(quad * SLOTS + u, u, quad, None if known is None else known * SLOTS + u,
                         values[u * each:(u + 2) * each])

            body(0, 0)
            with eng.Fori(1, TILES // SLOTS - 1) as quad:
                body(quad, None)
            body(TILES // SLOTS - 1, TILES // SLOTS - 1)

        def runs(known, lag):
            return known is None or 0 <= known - lag < IMAGES

        def lag_of(block):
            return (3, 5)[block]

        def combine(eng, engine, share, summing, summed):
            eng.wait_ge(res_done, IMAGES)
            for c in range(IMAGES // COMBINE):
                eng.wait_ge(got_in[c % 2], 16 * TOP * (c // 2 + 1))
                to = stream[:, c * COMBINE + share.start:c * COMBINE + share.stop, :]
                engine.tensor_tensor(to, to, got[:, c % 2, 0, share], ALU.add).then_inc(summing, 1)
                eng.wait_ge(summing, c + 1)
                engine.tensor_tensor(to, to, got[:, c % 2, 1, share], ALU.add).then_inc(summed, 1)

        by_tile = stream[0:PATCHES].rearrange("s (k i) d -> s k i d", i=2)

        def move(eng, k, second, moved, count=1):
            eng.wait_ge(emb_done, k + count)
            eng.dma_start(by_tile[:, bass.ds(k, count), second, :],
                          raw[second * PATCHES:(second + 1) * PATCHES, bass.ds(k, count), :]).then_inc(moved, 16)

        @block.sync
        def _(sp):
            sp.dma_start(gain[:, :], t["gain"]).then_inc(small_in, 16)
            sp.dma_start(shift[:, :], t["shift"]).then_inc(small_in, 16)
            sp.dma_start(b_row[:, :], t["tok_b"]).then_inc(small_in, 16)
            sp.dma_start(w_halo[:, :, :], t["w_halo"]).then_inc(halo_in, 16)
            for s in ARRIVAL:
                sp.dma_start(w_center[:, s], t["w_center"][:, s]).then_inc(shift_in[s], 16)

            def load(k, p, known):
                if known is None or known >= 2:
                    sp.wait_ge(pix_used, k - 1)
                    sp.wait_ge(emb_ps, k - 1)
                sp.dma_start(pix[:, p, :], t["pix"][k]).then_inc(pix_in[p], 16)
                sp.dma_start(pixT[:, p, :, :], t["pixT"][k]).then_inc(pixT_in[p], 16)

            for name, tile in (("affine", affine), ("gate", w_gate), ("before", before), ("iota", iota),
                               ("region", region), ("dest", dest), ("padding", padding), ("jota", jota)):
                sp.dma_start(tile[:], t[name]).then_inc(route_in, 16)
            for k in range(2):
                load(k, k, k)
            with sp.Fori(1, MOVE_BEHIND // 2) as pair:
                load(pair * 2, 0, None)
                load(pair * 2 + 1, 1, None)
            with sp.Fori(MOVE_BEHIND // 2, PAIRS // 2) as pair:
                for p in range(2):
                    load(pair * 2 + p, p, None)
                    move(sp, pair * 2 + (p - MOVE_BEHIND), 0, emb_moved[0])
            with sp.Fori((PAIRS - MOVE_BEHIND) // 2, PAIRS // 2) as pair:
                move(sp, pair * 2, 0, moved_late[0], 2)
            for p in range(2):
                sp.wait_ge(emb_moved[p], 16 * (PAIRS - MOVE_BEHIND))
                sp.wait_ge(moved_late[p], 16 * MOVE_BEHIND // 2)
            sp.wait_ge(w_lo_ready, 3 * BLOCKS)

            def load_expert(e):
                sp.dma_start(w1_whole[:, :, :], t["e1"][e]).then_inc(whole_in, 16)
                sp.dma_start(w2_whole[:, :, :], t["e2"][e]).then_inc(whole_in, 16)

            load_expert(0)
            with sp.Fori(1, EXPERTS) as e:
                sp.wait_ge(lo_ready, e)
                load_expert(e)

            sp.wait_ge(tables, 1)
            sp.wait_ge(route_in, 16 * ROUTE_LOADS)
            counts = nc.values_load_multi_w_load_instructions(
                cnt_i[0:1, :], engines=(sp.engine,), min_val=0, max_val=TOKENS,
                skip_runtime_bounds_check_because="an expert gets a token at most once")[1]
            for e in range(EXPERTS):
                sp.dma_start(t["routed"][bass.ds(counts[e] + e * REGION, TILE), :], padding[:, :]).then_inc(padded, 16)
            sp.dma_start(t["routed"][EXPERTS * REGION:EXPERTS * REGION + TILE, :], padding[:, :]).then_inc(padded, 16)
            sp.wait_ge(padded, 16 * (EXPERTS + 1))
            for p in range(2):
                sp.wait_ge(scattered[p], 16 * TOP * IMAGES // 2)
            sp.wait_ge(tables, 5)

            def fetch(j, u, quad, known, row):
                if known is None or known >= SLOTS:
                    sp.wait_ge(ys_out[u], quad * 16)
                sp.dma_start(picked[:, u, :], t["routed"][bass.ds(row[0], TILE), :]).then_inc(picked_in[u], 16)

            tiles(sp, fetch, row_i, (EXPERTS * REGION,))

            for u in range(SLOTS):
                sp.wait_ge(ys_out[u], 16 * TILES // SLOTS)
            for c in range(IMAGES // COMBINE):
                if c >= 2:
                    sp.wait_ge(summed_dve, c - 1)
                    sp.wait_ge(summed_pool, c - 1)
                for k in range(TOP):
                    sp.dma_start(got[:, c % 2, k], t["results"][k * TOKENS:(k + 1) * TOKENS, :]
                                 .rearrange("(b s) d -> s b d", s=SEQ)[:, c * COMBINE:(c + 1) * COMBINE, :])\
                        .then_inc(got_in[c % 2], 16)
            for c in range(IMAGES // COMBINE):
                sp.wait_ge(summed_dve, c + 1)
                sp.wait_ge(summed_pool, c + 1)
                sp.dma_start(t["out"][c * COMBINE:(c + 1) * COMBINE].rearrange("b s d -> s b d"),
                             stream[:, c * COMBINE:(c + 1) * COMBINE, :]).then_inc(out_done, 16)
            sp.wait_ge(out_done, 16 * (IMAGES // COMBINE))

        @block.gpsimd
        def _(pool):
            nc.gpsimd.memset(ident[:, :], 0.0).then_inc(ident_zero, 1)
            nc.gpsimd.memset(ones[:, :], 1.0).then_inc(consts, 1)
            nc.gpsimd.memset(half[:, :], -0.5).then_inc(consts, 1)
            nc.gpsimd.memset(tick[:, :], 0.0).then_inc(ticked, 1)
            nc.gpsimd.memset(minus_one[:, :], -1.0).then_inc(consts, 1)
            nc.gpsimd.memset(eps[:, :], EPS).then_inc(consts, 1)
            pool.wait_ge(ident_zero, 1)
            nc.gpsimd.affine_select(out=ident[:, :], in_=ident[:, :], compare_op=ALU.not_equal, fill=1.0,
                                    base=0, pattern=[[-1, 128]], channel_multiplier=1).then_inc(consts, 1)
            nc.gpsimd.memset(mpad[:, :, :, :, :], 0.0).then_inc(mpad_zero, 1)
            nc.gpsimd.memset(values[:, :, :, HEAD:HEAD + 1], A_SCALE).then_inc(mpad_zero, 1)
            pool.wait_ge(small_in, 48)
            for s in (3, 4):
                pool.wait_ge(shift_in[s], 16)
                nc.gpsimd.tensor_tensor(w_scaled[:, s], w_center[:, s],
                                        gain[:, s * CENTER_CHUNKS:(s + 1) * CENTER_CHUNKS].unsqueeze(2)
                                        .to_broadcast([KC, CENTER_CHUNKS, DIM]), ALU.mult).then_inc(scaled_pool, 1)
            pool.wait_ge(scaled_pool, 2)
            nc.gpsimd.tensor_tensor(w_scaled[:, 3], w_scaled[:, 3], w_scaled[:, 4], ALU.add).then_inc(scaled_pool, 1)
            pool.wait_ge(halo_in, 16)
            n = SHIFTS * CENTER_CHUNKS
            nc.gpsimd.tensor_tensor(w_fold[:, CENTER_CHUNKS:, :], w_halo[:, :, :],
                                    gain[:, n:n + 2].unsqueeze(2).to_broadcast([KC, 2, DIM]), ALU.mult)\
                .then_inc(scaled_pool, 1)
            pool.wait_ge(folded, 1)
            nc.gpsimd.tensor_tensor(w_halo[:, :, :], w_halo[:, :, :],
                                    shift[:, n:n + 2].unsqueeze(2).to_broadcast([KC, 2, DIM]), ALU.mult)\
                .then_inc(offset_step, 1)
            for s in range(SHIFTS):
                nc.gpsimd.tensor_tensor(w_center[:, s], w_center[:, s],
                                        shift[:, s * CENTER_CHUNKS:(s + 1) * CENTER_CHUNKS].unsqueeze(2)
                                        .to_broadcast([KC, CENTER_CHUNKS, DIM]), ALU.mult).then_inc(offset_step, 1)
            for i, (to, of) in enumerate(((0, 1), (2, 3), (0, 4), (0, 2))):
                pool.wait_ge(offset_step, 1 + SHIFTS + i)
                nc.gpsimd.tensor_tensor(w_center[:, to], w_center[:, to], w_center[:, of], ALU.add)\
                    .then_inc(offset_step, 1)
            beta, total = w_center[:, 0], w_center[:, 1]
            rest = CENTER_CHUNKS // 2
            for i, (beta_by, total_of, total_by) in enumerate((
                    (beta[:, rest:], w_fold[:, 0:rest], w_fold[:, rest:CENTER_CHUNKS]),
                    (beta[:, 2:4], total[:, 0:2], total[:, 2:4]),
                    (w_halo[:, :], total[:, 0:2], w_fold[:, CENTER_CHUNKS:]),
                    (beta[:, 1:2], total[:, 0:1], total[:, 1:2]))):
                pool.wait_ge(offset_step, 5 + SHIFTS + 2 * i)
                n = total_of.shape[1]
                nc.gpsimd.tensor_tensor(beta[:, 0:n], beta[:, 0:n], beta_by, ALU.add).then_inc(offset_step, 1)
                nc.gpsimd.tensor_tensor(total[:, 0:n], total_of, total_by, ALU.add).then_inc(offset_step, 1)

            def reciprocal_root(part):
                at = slice(part * PAIRS // 2, (part + 1) * PAIRS // 2)
                pool.wait_ge(var_ready, part + 1)
                nc.gpsimd.tensor_tensor(stat[:, 7, at], stat[:, 6, at], half[0:PAIR, at], ALU.pow).then_inc(rstd_ready, 1)

            reciprocal_root(0)
            for b in range(BLOCKS):
                for i, (whole, parts) in enumerate(((w_qk, w_qk16), (w_v, w_v16), (w_p, w_p16))):
                    pool.wait_ge(w_hi_ready, 3 * b + i + 1)
                    nc.gpsimd.tensor_tensor(parts[:, b, 1], whole[:, b], parts[:, b, 0], ALU.subtract)\
                        .then_inc(w_lo_ready, 1)
            reciprocal_root(1)

            nc.gpsimd.memset(seen[:, :, :], 0.0).then_inc(consts, 1)
            tt = nc.gpsimd.tensor_tensor

            def then(instruction, count):
                instruction.then_inc(pool_step, 1)
                pool.wait_ge(pool_step, count)

            def norm(i, p, known):
                if known is None or known >= 2:
                    pool.wait_ge(xn_ready, i - 1)
                pool.wait_ge(stats_ready, i + 1)
                then(tt(veps[:, p], mv_x[:, p, 1:2], eps[0:SEQ, :], ALU.add), 3 * i + 1)
                then(tt(rstd[:, p], veps[:, p], half[0:SEQ, 0:1], ALU.pow), 3 * i + 2)
                then(tt(veps[:, p], mv_x[:, p, 0:1], rstd[:, p], ALU.mult), 3 * i + 3)
                tt(nmr[:, p], veps[:, p], minus_one[0:SEQ, :], ALU.mult).then_inc(norm_ready, 1)

            def low_part(block, i, p):
                pool.wait_ge(p_ready, i + block * IMAGES + 1)
                tt(p_lo[:, p], probs[:, :, :, :], p_hi[:, p], ALU.subtract).then_inc(p_lo_ready, 1)

            def step(n, p, known):
                if runs(known, 1):
                    low_part(0, n - 1, 1 - p)
                if runs(known, -1):
                    norm(n + 1, 1 - p, None if known is None else known + 1)

            norm(0, 0, 0)
            pipeline(pool, step, lag_of(0))

            at = 3 * IMAGES
            for first, last in ((0, EARLY), (EARLY, IMAGES)):
                pool.wait_ge(mv2_ready, last)
                n = slice(first, last)
                mean, var = mv2[:, n, 0], mv2[:, n, 1]
                r1, m1, v, r2 = rstd_b[:, n, 0], nmr_b[:, n, 0], work_b[:, n, 0], scale2_b[:, n, 0]
                by, of, power = (x[0:SEQ, 0:1].to_broadcast([SEQ, last - first]) for x in (eps, minus_one, half))
                for out, a, b, op in ((v, var, by, ALU.add), (r1, v, power, ALU.pow), (m1, mean, r1, ALU.mult),
                                      (m1, m1, of, ALU.mult), (v, var, r1, ALU.mult), (v, v, r1, ALU.mult),
                                      (v, v, by, ALU.add), (r2, v, power, ALU.pow),
                                      (nmr2_b[:, n, 0], m1, r2, ALU.mult)):
                    at += 1
                    then(tt(out, a, b, op), at)
                tt(r2, r2, r1, ALU.mult).then_inc(norms_ready, 1)

            def root(i, p):
                pool.wait_ge(stats_t, i + IMAGES + 1)
                tt(veps_t[:, p], mv_t[:, p, 1:2], eps[0:SEQ, :], ALU.add).then_inc(root_t, 1)
                pool.wait_ge(root_t, 4 * i + 1)
                tt(rstd_s[:, p], veps_t[:, p], half[0:SEQ, 0:1], ALU.pow).then_inc(root_t, 1)
                pool.wait_ge(root_t, 4 * i + 2)
                tt(mr_s[:, p], mv_t[:, p, 0:1], rstd_s[:, p], ALU.mult).then_inc(root_t, 1)
                pool.wait_ge(root_t, 4 * i + 3)

            def keep(i, p):
                tt(nmr_t[:, i], mr_s[:, p], minus_one[0:SEQ, :], ALU.mult)
                tt(rstd_t[:, i], rstd_s[:, p], ones[0:SEQ, 0:1], ALU.mult).then_inc(kept, 1)
                tt(stream[:, i, :], stream[:, i, :], inner[:, i, :], ALU.add).then_inc(res_done, 1)

            def step(n, p, known):
                if runs(known, 1):
                    low_part(1, n - 1, 1 - p)
                if runs(known, 2):
                    root(n - 2, p)
                if runs(known, 5):
                    pool.wait_ge(slots_ready, n - 4)
                    pool.wait_ge(rows_filled, n - 4)
                if runs(known, 2):
                    tt(nmr_s[:, p], mr_s[:, p], minus_one[0:SEQ, :], ALU.mult).then_inc(root_t, 1)
                    keep(n - 2, p)
                if runs(known, 5):
                    for k in range(TOP):
                        nc.gpsimd.indirect_dma_start(
                            out=t["routed"], out_offset=bass.IndirectOffsetOnAxis(ap=slot[:, 1 - p, k:k + 1], axis=0),
                            in_=rows[:, 1 - p, k, :], in_offset=None).then_inc(scattered[1 - p], 16)

            pipeline(pool, step, 5)

            def send(j, u, quad, known, _):
                pool.wait_ge(ys_ready, j + 1)
                pool.wait_ge(ticked, j + 1)
                tt(tick[:, :], minus_one[0:1, :], eps[0:1, :], ALU.mult).then_inc(ticked, 1)
                nc.gpsimd.indirect_dma_start(
                    out=t["results"],
                    out_offset=bass.IndirectOffsetOnAxis(ap=picked[:, u, DIM + 1:DIM + 2].bitcast(U32), axis=0),
                    in_=ys[:, u, :], in_offset=None, bounds_check=TOP * TOKENS - 1, oob_is_err=False)\
                    .then_inc(ys_out[u], 16)

            tiles(pool, send)
            combine(pool, nc.gpsimd, slice(DVE_SHARE, COMBINE), summing_pool, summed_pool)

        @block.scalar
        def _(act):
            act.dma_start(stream[PATCHES:SEQ, :, :], t["txt"]).then_inc(text_in, 16)
            act.dma_start(slot_rows[:, :], t["slot_rows"]).then_inc(attn_in, 16)
            act.wait_ge(folded, 1)
            for b in range(BLOCKS):
                act.dma_start(w_qk[:, b], t["qk"][b]).then_inc(attn_in, 16)
                act.dma_start(w_v[:, b], t["v"][b]).then_inc(attn_in, 16)
                act.dma_start(w_p[:, b], t["p"][b]).then_inc(attn_in, 16)

            def stage(k, p):
                act.wait_ge(emb_ps, k + 1)
                nc.scalar.copy(raw[:, k, :], (ps_q, ps_a)[p][0:PAIR, 0:DIM]).then_inc(emb_raw, 1)

            with act.Fori(0, BEHIND // 2) as pair:
                stage(pair * 2, 0)
                stage(pair * 2 + 1, 1)
            act.wait_ge(sums_ps, 1)
            nc.scalar.copy(colsum[:, :], ps_v[0:PAIR, 0:DIM]).then_inc(sums_out, 1)
            nc.scalar.copy(bias_all[:, :], ps_v[0:PAIR, DIM:2 * DIM]).then_inc(sums_out, 1)
            act.wait_ge(attn_in, ATTN_LOADS)
            weights = [(b, whole, parts) for b in range(BLOCKS)
                       for whole, parts in ((w_qk, w_qk16), (w_v, w_v16), (w_p, w_p16))]
            for i, (b, whole, parts) in enumerate(weights):
                stage(BEHIND + i, i % 2)
                nc.scalar.activation(whole[:, b], whole[:, b], ACT.Copy, scale=A_SCALE).then_inc(whole_scaled, 1)
                act.wait_ge(whole_scaled, i + 1)
                nc.scalar.copy(parts[:, b, 0], whole[:, b]).then_inc(w_hi_ready, 1)
                if BEHIND + i >= MOVE_BEHIND:
                    move(act, BEHIND + i - MOVE_BEHIND, 1, emb_moved[1])
            with act.Fori((PAIRS - MOVE_BEHIND) // 2, PAIRS // 2) as pair:
                move(act, pair * 2, 1, moved_late[1], 2)

            act.wait_ge(mpad_zero, 5)

            def normalize(block, i, p):
                if block == 0:
                    act.wait_ge(norm_ready, i + 1)
                    nc.scalar.activation(xn[:, p], stream[:, i, :], ACT.Identity,
                                         bias=nmr[:, p], scale=rstd[:, p]).then_inc(xn_ready, 1)
                    return
                nc.scalar.activation(xn[:, p], stream[:, i, :], ACT.Identity,
                                     bias=nmr2_b[:, i], scale=scale2_b[:, i]).then_inc(xn_ready, 1)
                nc.scalar.activation(inner[:, i, :], stream[:, i, :], ACT.Identity,
                                     bias=nmr_b[:, i], scale=rstd_b[:, i]).then_inc(inner_ready, 1)

            def step(block, n, p, known):
                base = block * IMAGES
                if block and known == lag_of(block):
                    act.wait_ge(norms_ready, 2)
                if runs(known, 0):
                    act.wait_ge(aT_ps, n + base + 1)
                    src = ps_a[0:KC, 0:CHUNKS * SEQ].rearrange("k (c s) -> k c s", c=CHUNKS)
                    if block == 0:
                        nc.scalar.copy(aT[:, p, 0], src).then_inc(aT_hi_ready, 1)
                    else:
                        for c in range(CHUNKS):
                            last = nc.scalar.activation(a32[:, c], src[:, c], ACT.Identity,
                                                        bias=affine[:, 0, 1, c:c + 1], scale=affine[:, 0, 0, c:c + 1])
                        last.then_inc(a32_ready, 1)
                if runs(known, 1):
                    act.wait_ge(st_ps, n + base)
                    scores = ps_s[0:SEQ, :, 0:GROUPS * SEQ].rearrange("k r (g q) -> k r g q", g=GROUPS)
                    nc.scalar.activation(p_hi[:, 1 - p], scores, ACT.Exp, scale=HEAD ** -0.5 / A_SCALE ** 2)
                if runs(known, 2):
                    act.wait_ge(oT_ps, n + base - 1)
                    nc.scalar.copy(oT[0:KC, 0], ps_o[0:KC, 0:CHUNKS * SEQ].rearrange("k (c s) -> k c s", c=CHUNKS))\
                        .then_inc(oT_hi_ready, 1)
                if runs(known, 1):
                    if known is None or known + base >= 2:
                        act.wait_ge(p_lo_ready, n + base - 1)
                    nc.scalar.activation(probs[:, :, :, :], scores, ACT.Exp, scale=HEAD ** -0.5 / A_SCALE ** 2)\
                        .then_inc(p_ready, 1)
                if runs(known, 0):
                    act.wait_ge(qk_ps, n + base + 1)
                    nc.scalar.copy(hi[:, p], ps_q[:, 0:2 * GROUPS * SEQ]
                                   .rearrange("k (a g s) -> k a g s", a=2, g=GROUPS)).then_inc(qk_ready, 1)
                if runs(known, -1):
                    normalize(block, n + 1, 1 - p)
                if block and runs(known, 4):
                    act.wait_ge(gap_ready, n - 3)
                    nc.scalar.activation(egap[:, p], gap[:, p], ACT.Exp).then_inc(egap_ready, 1)
                if block and runs(known, 3):
                    act.wait_ge(tT_ps, n - 2)
                    src = ps_a[0:KC, 0:CHUNKS * SEQ].rearrange("k (c s) -> k c s", c=CHUNKS)
                    for c in range(CHUNKS):
                        last = nc.scalar.activation(tT[0:KC, c], src[:, c], ACT.Identity,
                                                    bias=affine[:, 1, 1, c:c + 1], scale=affine[:, 1, 0, c:c + 1])
                    last.then_inc(tT_ready, 1)
                if block and runs(known, 4):
                    i = n - 4
                    if known is None or known >= 6:
                        act.wait_ge(scattered[p], 16 * (i - p))
                    act.wait_ge(kept, i + 1)
                    for k in range(TOP):
                        last = nc.scalar.activation(rows[:, p, k, 0:DIM], inner[:, i, :], ACT.Identity,
                                                    bias=nmr_t[:, i], scale=rstd_t[:, i])
                    last.then_inc(rows_filled, 1)
                if block and runs(known, 2):
                    i = n - 2
                    act.wait_ge(root_t, 4 * i + 4)
                    nc.scalar.activation(xh[:, p], inner[:, i, :], ACT.Identity,
                                         bias=nmr_s[:, p], scale=rstd_s[:, p]).then_inc(xh_ready, 1)

            def split(e):
                act.wait_ge(whole_in, e * 32 + 32)
                nc.scalar.activation(w1_parts[:, e, 0], w1_whole[:, :, :], ACT.Copy, scale=W_SCALE)
                nc.scalar.activation(w2_parts[:, e, 0], w2_whole[:, :, :], ACT.Copy, scale=W_SCALE).then_inc(hi_ready, 1)

            act.wait_ge(route_in, 16 * ROUTE_LOADS)
            for b in range(BLOCKS):
                if b:
                    act.wait_ge(norms_ready, 1)
                normalize(b, 0, 0)
                pipeline(act, lambda n, p, known: step(b, n, p, known), lag_of(b), None if b else split)

            act.wait_ge(tables, 1)
            act.dma_start(b2[:, :, :], t["eb"].to_broadcast([TILE, EXPERTS, DIM])).then_inc(b2_in, 16)

            def activate(j, p, known):
                for half in range(HALVES):
                    if known is None or known >= 2:
                        act.wait_ge(h_ready, j * HALVES + (half + 1 - 2 * HALVES))
                    act.wait_ge(h_ps, j * HALVES + (half + 1))
                    nc.scalar.activation(h32[:, p, half], ps_s[:, 2 * p + half, 0:PER_HALF * TILE]
                                         .rearrange("h (c n) -> h c n", c=PER_HALF),
                                         ACT.Gelu, scale=1 / W_SCALE).then_inc(h32_ready, 1)
                    if known is None or known >= 2:
                        act.wait_ge(y_ps, j - 1)
                    act.wait_ge(h32_ready, j * HALVES + (half + 1))
                    nc.scalar.copy(hs[:, p, 0, half], h32[:, p, half]).then_inc(h_hi_ready, 1)

            def weigh(j, u, quad, known):
                if known is None or known >= SLOTS:
                    act.wait_ge(ys_out[u], quad * 16)
                act.wait_ge(picked_in[u], quad * 16 + 16)
                act.wait_ge(y_added, j + 1)
                nc.scalar.activation(ys[:, u, :], y[:, u % 2], ACT.Copy, scale=picked[:, u, DIM:DIM + 1])\
                    .then_inc(ys_ready, 1)

            def step(j, u, quad, known, _):
                if known is None or known + 1 < TILES:
                    activate(j + 1, (u + 1) % 2, None if known is None else known + 1)
                weigh(j, u, quad, known)

            activate(0, 0, 0)
            tiles(act, step)

        @block.vector
        def _(dve):
            steps = [0]

            def then(instruction):
                instruction.then_inc(dve_step, 1)
                steps[0] += 1
                dve.wait_ge(dve_step, steps[0])

            nc.vector.memset(oT[KC:KC + 1, 0, :, :], 1.0).then_inc(mpad_zero, 1)
            nc.vector.memset(oT[KC:KC + 1, 1, :, :], 0.0).then_inc(mpad_zero, 1)
            nc.vector.memset(tT[KC:KC + 1, :, :], 1.0).then_inc(mpad_zero, 1)
            dve.wait_ge(small_in, 48)
            dve.wait_ge(shift_in[0], 16)
            then(nc.vector.tensor_tensor(w_scaled[:, 0], w_center[:, 0], gain[:, 0:CENTER_CHUNKS].unsqueeze(2)
                                         .to_broadcast([KC, CENTER_CHUNKS, DIM]), ALU.mult))
            for s in (1, 2):
                dve.wait_ge(shift_in[s], 16)
                for c in range(CENTER_CHUNKS):
                    at = s * CENTER_CHUNKS + c
                    last = nc.vector.scalar_tensor_tensor(out=w_scaled[:, 0, c], in0=w_center[:, s, c],
                                                          scalar=gain[:, at:at + 1], in1=w_scaled[:, 0, c],
                                                          op0=ALU.mult, op1=ALU.add)
                then(last)
            dve.wait_ge(scaled_pool, 4)
            nc.vector.tensor_tensor(w_fold[:, 0:CENTER_CHUNKS], w_scaled[:, 0], w_scaled[:, 3], ALU.add)\
                .then_inc(folded, 1)

            def statistics(k, p, base, known):
                dve.wait_ge(pix_in[p], 8 * (k - p) + 16)
                tile = pix[:, p, :]
                own = tile[:, 0:CENTER].rearrange("t (r c) -> t r c", r=PATCH)
                for h in range(2):
                    nc.vector.bn_stats(bn_c[:, p, h * BN:(h + 1) * BN], tile[:, h * CENTER // 2:(h + 1) * CENTER // 2])\
                        .then_inc(dve_step, 1)
                nc.vector.bn_stats(bn_h[:, p, :], tile[:, CENTER:FEATURES]).then_inc(dve_step, 1)
                nc.vector.bn_stats(bn_e[:, p, 0:BN], own[:, 0:PATCH:PATCH - 1, :]).then_inc(dve_step, 1)
                nc.vector.bn_stats(bn_e[:, p, BN:2 * BN], own.rearrange("t r (w c) -> t r w c", c=CHANNELS)
                                   [:, :, 0:PATCH:PATCH - 1, :]).then_inc(pix_used, 1)
                dve.wait_ge(dve_step, base + 4)
                dve.wait_ge(pix_used, k + 1)
                if known is None or known >= 1:
                    nc.vector.tensor_copy(mv[:, k - 1], mv_k[:, 1 - p]).then_inc(dve_step, 1)
                nc.vector.bn_aggr(mv_k[:, p, 0], bn_c[:, p, :]).then_inc(dve_step, 1)
                nc.vector.bn_aggr(mv_k[:, p, 1], bn_h[:, p, :]).then_inc(dve_step, 1)
                nc.vector.bn_aggr(mv_k[:, p, 2], bn_e[:, p, :]).then_inc(dve_step, 1)

            def factors(at):
                (m_c, v_c), (m_h, v_h), (m_e, v_e) = ((mv[:, at, j, 0], mv[:, at, j, 1]) for j in range(3))
                d_h, d_e, d, nmean, var = (stat[:, j, at] for j in range(5))
                share = HALO / COPIED
                stt = nc.vector.scalar_tensor_tensor
                then(nc.vector.tensor_tensor(d_h, m_h, m_c, ALU.subtract))
                then(nc.vector.tensor_tensor(d_e, m_e, m_c, ALU.subtract))
                then(nc.vector.tensor_tensor(d, m_h, m_e, ALU.subtract))
                then(stt(out=nmean, in0=d, scalar=-share, in1=m_c, op0=ALU.mult, op1=ALU.subtract))
                then(nc.vector.tensor_tensor(d_h, d_h, d_h, ALU.mult))
                then(nc.vector.tensor_tensor(d_e, d_e, d_e, ALU.mult))
                then(nc.vector.tensor_tensor(d_h, d_h, v_h, ALU.add))
                then(nc.vector.tensor_tensor(d_e, d_e, v_e, ALU.add))
                then(nc.vector.tensor_tensor(d_h, d_h, d_e, ALU.subtract))
                then(stt(out=var, in0=d_h, scalar=share, in1=v_c, op0=ALU.mult, op1=ALU.add))
                then(nc.vector.tensor_scalar(d, d, share, None, ALU.mult))
                then(nc.vector.tensor_tensor(d, d, d, ALU.mult))
                then(nc.vector.tensor_tensor(var, var, d, ALU.subtract))
                nc.vector.tensor_scalar(stat[:, 6, at], var, 1e-3, None, ALU.add).then_inc(var_ready, 1)

            def finish(first, count):
                for k in [first + i for i in range(count)]:
                    dve.wait_ge(emb_raw, k + 1)
                    nc.vector.scalar_tensor_tensor(out=raw[:, k, :], in0=colsum[:, :], scalar=stat[:, 3:4, k],
                                                   in1=raw[:, k, :], op0=ALU.mult, op1=ALU.add).then_inc(finishing, 1)
                for k in [first + i for i in range(count)]:
                    dve.wait_ge(finishing, k + 1)
                    nc.vector.scalar_tensor_tensor(out=raw[:, k, :], in0=raw[:, k, :], scalar=stat[:, 7:8, k],
                                                   in1=bias_all[:, :], op0=ALU.mult, op1=ALU.add).then_inc(emb_done, 1)

            middle = PAIRS // 2
            base = steps[0]
            for k in range(2):
                statistics(k, k, max(8 * k - 1, 0) + base, k)
            with dve.Fori(1, middle // 2) as pair:
                k = pair * 2
                statistics(k, 0, k * 8 + (base - 1), None)
                statistics(k + 1, 1, k * 8 + (base + 7), None)
            steps[0] += 8 * middle - 1
            dve.wait_ge(dve_step, steps[0])
            then(nc.vector.tensor_copy(mv[:, middle - 1], mv_k[:, 1]))
            factors(slice(0, middle))
            base = steps[0] - 8 * middle
            for k in range(middle, BEHIND):
                statistics(k, k % 2, k * 8 + base, k)
            dve.wait_ge(rstd_ready, 1)
            dve.wait_ge(sums_out, 2)
            with dve.Fori(BEHIND // 2, PAIRS // 2) as pair:
                k = pair * 2
                statistics(k, 0, k * 8 + base, None)
                finish(k - BEHIND, 1)
                statistics(k + 1, 1, k * 8 + (base + 8), None)
                finish(k + (1 - BEHIND), 1)
            steps[0] += 8 * middle
            dve.wait_ge(dve_step, steps[0])
            then(nc.vector.tensor_copy(mv[:, PAIRS - 1], mv_k[:, 1]))
            factors(slice(middle, PAIRS))
            finish(PAIRS - BEHIND, middle - (PAIRS - BEHIND))
            dve.wait_ge(rstd_ready, 2)
            with dve.Fori(middle // 2, PAIRS // 2) as pair:
                finish(pair * 2, 2)

            def experts(i, p):
                base = 4 * i
                nc.vector.max(best[:, p], logit[:, p]).then_inc(route_step, 1)
                dve.wait_ge(route_step, base + 1)
                nc.vector.tensor_tensor(gap[:, p], best[:, p, 1:2], best[:, p, 0:1], ALU.subtract).then_inc(gap_ready, 1)
                nc.vector.max_index(best_at[:, p], best[:, p], logit[:, p]).then_inc(route_step, 1)
                dve.wait_ge(route_step, base + 2)
                nc.vector.tensor_copy(chosen[:, p], best_at[:, p, 0:TOP]).then_inc(route_step, 1)
                dve.wait_ge(route_step, base + 3)
                nc.vector.tensor_tensor(mask[:, p], iota[:, :, :], chosen[:, p].unsqueeze(2)
                                        .to_broadcast([SEQ, TOP, EXPERTS]), ALU.is_equal).then_inc(route_step, 1)
                dve.wait_ge(route_step, base + 4)
                nc.vector.tensor_tensor(hits[:, p], mask[:, p, 0], mask[:, p, 1], ALU.add).then_inc(hits_ready, 1)

            def place_rows(i, p, known):
                dve.wait_ge(rank_read, i + 1)
                nc.vector.tensor_tensor(placed[:, p], mask[:, p], place[:, p].unsqueeze(1)
                                        .to_broadcast([SEQ, TOP, EXPERTS]), ALU.mult).then_inc(place_step, 1)
                dve.wait_ge(egap_ready, i + 1)
                nc.vector.tensor_scalar(esum[:, p], egap[:, p], 1.0, None, ALU.add).then_inc(place_step, 1)
                dve.wait_ge(place_step, 4 * i + 1)
                nc.vector.tensor_reduce(slot_f[:, p], placed[:, p], AX.X, ALU.add).then_inc(place_step, 1)
                if known is None or known >= 2:
                    dve.wait_ge(scattered[p], 16 * (i - p))
                dve.wait_ge(place_step, 4 * i + 2)
                nc.vector.reciprocal(rows[:, p, 0, DIM:DIM + 1], esum[:, p]).then_inc(place_step, 1)
                dve.wait_ge(place_step, 4 * i + 4)
                nc.vector.tensor_tensor(rows[:, p, 1, DIM:DIM + 1], rows[:, p, 0, DIM:DIM + 1], egap[:, p], ALU.mult)\
                    .then_inc(slot_step, 1)
                nc.vector.tensor_copy(rows[:, p, :, DIM + 1].bitcast(U32), dest[:, :]).then_inc(slot_step, 1)
                nc.vector.tensor_copy(slot[:, p], slot_f[:, p]).then_inc(slot_step, 1)
                dve.wait_ge(slot_step, 3 * i + 3)
                nc.vector.tensor_scalar(dest[:, :], dest[:, :], float(SEQ), None, ALU.add).then_inc(slots_ready, 1)

            for p in range(2):
                dve.wait_ge(emb_moved[p], 16 * (PAIRS - MOVE_BEHIND))
            dve.wait_ge(text_in, 16)
            dve.wait_ge(mpad_zero, 5)
            dve.wait_ge(consts, CONSTS)
            dve.wait_ge(route_in, 16 * ROUTE_LOADS)

            def step(block, n, p, known):
                base = block * IMAGES
                stt = nc.vector.scalar_tensor_tensor
                if block == 0 and known == lag_of(0):
                    for half in range(2):
                        dve.wait_ge(moved_late[half], 16 * MOVE_BEHIND // 2)
                if runs(known, 0):
                    if block == 0:
                        dve.wait_ge(aT_hi_ready, n + 1)
                        nc.vector.tensor_tensor(aT[:, p, 1], ps_a[0:KC, 0:CHUNKS * SEQ]
                                                .rearrange("k (c s) -> k c s", c=CHUNKS),
                                                aT[:, p, 0], ALU.subtract).then_inc(aT_ready, 1)
                    else:
                        dve.wait_ge(a32_ready, n + 1)
                        nc.vector.tensor_copy(aT[:, p, 0], a32[:, :]).then_inc(aT_hi_ready, 1)
                        dve.wait_ge(aT_hi_ready, n + base + 1)
                        nc.vector.tensor_tensor(aT[:, p, 1], a32[:, :], aT[:, p, 0], ALU.subtract).then_inc(aT_ready, 1)
                if block == 0 and runs(known, -1) and (known is None or known >= 1):
                    dve.wait_ge(norm_ready, n)
                if runs(known, 1):
                    dve.wait_ge(v_ps, n + base)
                    whole = ps_v[0:SEQ, 0:DIM].rearrange("s (h d) -> s h d", h=HEADS)
                    nc.vector.tensor_copy(values[:, 1 - p, :, 0:HEAD], whole).then_inc(v_hi_ready, 1)
                    dve.wait_ge(v_hi_ready, n + base)
                    nc.vector.tensor_tensor(values[:, 1 - p, :, HEAD + 1:AV], whole, values[:, 1 - p, :, 0:HEAD],
                                            ALU.subtract).then_inc(v_ready, 1)
                if runs(known, 2):
                    dve.wait_ge(oT_hi_ready, n + base - 1)
                    nc.vector.tensor_tensor(oT[0:KC, 1], ps_o[0:KC, 0:CHUNKS * SEQ]
                                            .rearrange("k (c s) -> k c s", c=CHUNKS),
                                            oT[0:KC, 0], ALU.subtract).then_inc(oT_ready, 1)
                if block == 0 and runs(known, -1):
                    nc.vector.bn_stats(bn_x[:, 1 - p, :], stream[:, n + 1, :]).then_inc(bn_done, 1)
                    dve.wait_ge(bn_done, n + 2)
                if block == 0 and runs(known, 3):
                    dve.wait_ge(stats_t, n - 2)
                if block and runs(known, 4):
                    dve.wait_ge(logit_read, n - 3)
                if block and runs(known, 5):
                    nc.vector.tensor_tensor(seen[:, p], seen[:, 1 - p], hits[:, 1 - p], ALU.add).then_inc(seen_ready, 1)
                if block and runs(known, 4):
                    experts(n - 4, p)
                if block and runs(known, 5):
                    place_rows(n - 5, 1 - p, None if known is None else known - 5)
                if runs(known, 0):
                    dve.wait_ge(qk_ready, n + base + 1)
                    of_q, of_k = (ps_q[:, a * GROUPS * SEQ:(a + 1) * GROUPS * SEQ]
                                  .rearrange("k (g s) -> k g s", g=GROUPS) for a in range(2))
                    stt(out=q_both[:, p], in0=hi[:, p, 0], scalar=slot_rows[:, 0:1], in1=of_q,
                        op0=ALU.mult, op1=ALU.add)
                    stt(out=k_low[:, p], in0=hi[:, p, 1], scalar=-1.0, in1=of_k,
                        op0=ALU.mult, op1=ALU.add).then_inc(parts_ready, 1)
                if block == 0 and runs(known, -1):
                    nc.vector.bn_aggr(mv_x[:, 1 - p, :], bn_x[:, 1 - p, :]).then_inc(stats_ready, 1)
                if block == 0 and runs(known, 3):
                    nc.vector.tensor_copy(mv2[:, n - 3, :], mv_t[:, 1 - p, :]).then_inc(mv2_ready, 1)
                if runs(known, 2):
                    dve.wait_ge(pr_ps, n + base - 1)
                    to = (stream, inner)[block][:, n - 2, :]
                    stt(out=to, in0=ps_o[0:SEQ, 0:DIM], scalar=1 / A_SCALE, in1=to,
                        op0=ALU.mult, op1=ALU.add).then_inc(att_done, 1)
                    dve.wait_ge(att_done, n + base - 1)
                if runs(known, 0):
                    dve.wait_ge(s_ps, n + base + 1)
                    nc.vector.tensor_reduce(mpad[:, p, :, :, HEAD].rearrange("q g r -> q r g"),
                                            ps_s[0:SEQ, :, 0:GROUPS * SEQ].rearrange("q r (g k) -> q r g k", g=GROUPS),
                                            AX.X, ALU.max, negate=True).then_inc(max_ready, 1)
                    dve.wait_ge(parts_ready, n + base + 1)
                    nc.vector.tensor_scalar(k_low[:, p], k_low[:, p], slot_rows[:, 1:2], slot_rows[:, 2:3],
                                            ALU.mult, ALU.add)
                    nc.vector.tensor_scalar(q_high[:, p], hi[:, p, 0], slot_rows[:, 1:2], None, ALU.mult)\
                        .then_inc(operands, 1)
                if runs(known, 2):
                    nc.vector.bn_stats(bn_t[:, p, :], (stream, inner)[block][:, n - 2, :]).then_inc(bn_t_done, 1)
                    dve.wait_ge(bn_t_done, n + base - 1)
                    if block == 0 and (known is None or known >= 4):
                        dve.wait_ge(mv2_ready, n - 3)
                    if block and (known is None or known >= 4):
                        dve.wait_ge(kept, n - 3)
                if runs(known, 0):
                    dve.wait_ge(operands, n + base + 1)
                    dve.wait_ge(mT_ps, n + base + 1)
                    stt(out=qm[:, p], in0=ps_a[:, MAX_AT:MAX_AT + GROUPS * SEQ].rearrange("k (g s) -> k g s", g=GROUPS),
                        scalar=1 / MAX_SCALE, in1=q_high[:, p], op0=ALU.mult, op1=ALU.add).then_inc(qm_ready, 1)
                if runs(known, 2):
                    nc.vector.bn_aggr(mv_t[:, p, :], bn_t[:, p, :]).then_inc(stats_t, 1)
                if block and runs(known, 4):
                    dve.wait_ge(rank_ps, n - 3)
                if block and runs(known, 3):
                    dve.wait_ge(logit_ps, n - 2)
                    nc.vector.tensor_copy(logit[:, 1 - p], ps_a[0:SEQ, LOGIT_AT:LOGIT_AT + EXPERTS])\
                        .then_inc(logit_read, 1)
                if block and runs(known, 4):
                    nc.vector.tensor_tensor(place[:, p], ps_a[0:SEQ, RANK_AT:RANK_AT + EXPERTS], region[:, :], ALU.add)\
                        .then_inc(rank_read, 1)
                if runs(known, 1):
                    dve.wait_ge(av_ps, n + base)
                    av = ps_q[0:SEQ, 0:HEADS * AV].rearrange("s (h d) -> s h d", h=HEADS)
                    nc.vector.reciprocal(rec[:, 1 - p], av[:, :, HEAD:HEAD + 1]).then_inc(rec_done, 1)
                    nc.vector.tensor_copy(o_sum[:, 1 - p], av[:, :, 0:HEAD]).then_inc(rec_done, 1)
                    dve.wait_ge(rec_done, (n + base) * 3 - 1)
                    nc.vector.tensor_tensor(o_sum[:, 1 - p], o_sum[:, 1 - p], av[:, :, HEAD + 1:AV], ALU.add)\
                        .then_inc(rec_done, 1)
                    dve.wait_ge(rec_done, (n + base) * 3)
                    nc.vector.tensor_tensor(o[:, 1 - p], o_sum[:, 1 - p],
                                            rec[:, 1 - p].to_broadcast([SEQ, HEADS, HEAD]), ALU.mult)\
                        .then_inc(o_ready, 1)

            def split(e):
                dve.wait_ge(hi_ready, e + 1)
                for whole, parts in ((w1_whole, w1_parts), (w2_whole, w2_parts)):
                    last = nc.vector.scalar_tensor_tensor(out=parts[:, e, 1], in0=whole[:, :, :], scalar=W_SCALE,
                                                          in1=parts[:, e, 0], op0=ALU.mult, op1=ALU.subtract)
                last.then_inc(lo_ready, 1)

            for b in range(BLOCKS):
                if b == 0:
                    nc.vector.bn_stats(bn_x[:, 0, :], stream[:, 0, :]).then_inc(bn_done, 1)
                    dve.wait_ge(bn_done, 1)
                    nc.vector.bn_aggr(mv_x[:, 0, :], bn_x[:, 0, :]).then_inc(stats_ready, 1)
                pipeline(dve, lambda n, p, known: step(b, n, p, known), lag_of(b), None if b else split)

            count = [0]

            def then(instruction):
                count[0] += 1
                instruction.then_inc(table_step, 1)
                dve.wait_ge(table_step, count[0])

            dve.wait_ge(total_ps, 1)
            then(nc.vector.tensor_copy(cnt[:, :], ps_v[0:1, 0:EXPERTS]))
            nc.vector.tensor_copy(cnt_i[:, :], cnt[:, :]).then_inc(tables, 1)
            then(nc.vector.tensor_scalar(need[:, :], cnt[:, :], float(TILE - 1), None, ALU.add))
            then(nc.vector.tensor_copy(need_i[:, :], need[:, :]))
            then(nc.vector.tensor_scalar(need_i[:, :], need_i[:, :], 7, None, ALU.arith_shift_right))
            then(nc.vector.tensor_copy(need[:, :], need_i[:, :]))
            a, b = 0, 1
            then(nc.vector.tensor_copy(upto[:, a], need[:, :]))
            for d in (1, 2, 4):
                then(nc.vector.tensor_copy(upto[:, b, 0:d], upto[:, a, 0:d]))
                then(nc.vector.tensor_tensor(upto[:, b, d:], upto[:, a, d:], upto[:, a, 0:EXPERTS - d], ALU.add))
                a, b = b, a
            wide = [1, LISTED, EXPERTS]
            then(nc.vector.tensor_tensor(past[:, :, :], upto[:, a].unsqueeze(1).to_broadcast(wide),
                                         jota[:, :].unsqueeze(2).to_broadcast(wide), ALU.is_le))
            then(nc.vector.tensor_reduce(tile_e[:, :], past[:, :, :], AX.X, ALU.add))
            then(nc.vector.tensor_tensor(past[:, :, :], past[:, :, :], need[:, :].unsqueeze(1).to_broadcast(wide),
                                         ALU.mult))
            then(nc.vector.tensor_reduce(tile_s[:, :], past[:, :, :], AX.X, ALU.add))
            then(nc.vector.tensor_tensor(tile_l[:, :], jota[:, :], tile_s[:, :], ALU.subtract))
            then(nc.vector.tensor_scalar(tile_s[:, :], tile_e[:, :], float(EXPERTS), float(TILE), ALU.is_lt, ALU.mult))
            then(nc.vector.tensor_tensor(tile_l[:, :], tile_l[:, :], tile_s[:, :], ALU.mult))
            then(nc.vector.tensor_scalar(tile_s[:, :], tile_e[:, :], float(REGION), None, ALU.mult))
            then(nc.vector.tensor_tensor(tile_l[:, :], tile_l[:, :], tile_s[:, :], ALU.add))
            nc.vector.tensor_copy(row_i[:, :], tile_l[:, :]).then_inc(tables, 1)
            then(nc.vector.tensor_scalar(tile_e[:, :], tile_e[:, :], float(EXPERTS - 1), None, ALU.min))
            nc.vector.tensor_copy(expert_i[:, :], tile_e[:, :]).then_inc(tables, 1)
            for i, size in enumerate((W1_SIZE, W2_SIZE)):
                nc.vector.tensor_scalar(weights_i[:, i::2], tile_e[:, :], float(size), None, ALU.mult)\
                    .then_inc(tables, 1)

            for part in range(2):
                last = nc.vector.memset(xs[KC:KC + 1, :, part, :, :], 1.0 - part).then_inc(xs_ones, 1)

            def rows_in(j, p, known):
                dve.wait_ge(x_ps, j + 1)
                for c in range(CHUNKS):
                    last = nc.vector.tensor_scalar(x32[:, p, c], (ps_a, ps_v)[p][0:KC, c * TILE:(c + 1) * TILE],
                                                   affine[:, 1, 0, c:c + 1], affine[:, 1, 1, c:c + 1],
                                                   ALU.mult, ALU.add)
                last.then_inc(x32_ready, 1)
                if known is None or known >= 2:
                    dve.wait_ge(h_ps, j * HALVES + (HALVES - 2 * HALVES))
                dve.wait_ge(x32_ready, j + 1)
                nc.vector.tensor_copy(xs[0:KC, p, 0], x32[:, p]).then_inc(x_hi_ready, 1)
                dve.wait_ge(x_hi_ready, j + 1)
                nc.vector.tensor_tensor(xs[0:KC, p, 1], x32[:, p], xs[0:KC, p, 0], ALU.subtract).then_inc(x_ready, 1)

            def hidden_low(j, p, half):
                dve.wait_ge(h_hi_ready, j * HALVES + (half + 1))
                nc.vector.tensor_tensor(hs[:, p, 1, half], h32[:, p, half], hs[:, p, 0, half], ALU.subtract)\
                    .then_inc(h_ready, 1)

            def add_bias(j, p, known, expert):
                if known is None or known >= 2:
                    dve.wait_ge(ys_ready, j - 1)
                dve.wait_ge(y_ps, j + 1)
                nc.vector.scalar_tensor_tensor(out=y[:, p], in0=(ps_q, ps_o)[p][:, 0:DIM], scalar=1 / W_SCALE,
                                               in1=b2[:, expert, :], op0=ALU.mult, op1=ALU.add).then_inc(y_added, 1)

            def step(j, u, quad, known, expert):
                p = u % 2
                if known is None or known + 1 < TILES:
                    hidden_low(j + 1, 1 - p, 0)
                if known is None or known + 2 < TILES:
                    rows_in(j + 2, p, None if known is None else known + 2)
                if known is None or known + 1 < TILES:
                    hidden_low(j + 1, 1 - p, 1)
                add_bias(j, p, known, expert[0])

            dve.wait_ge(tables, 5)
            dve.wait_ge(b2_in, 16)
            rows_in(0, 0, 0)
            hidden_low(0, 0, 0)
            rows_in(1, 1, 1)
            hidden_low(0, 0, 1)
            tiles(dve, step, expert_i, (EXPERTS - 1,))

            combine(dve, nc.vector, slice(0, DVE_SHARE), summing_dve, summed_dve)

        @block.tensor
        def _(pe):
            pe.wait_ge(small_in, 48)
            pe.wait_ge(consts, 5)

            def embed(k, p, known):
                pe.wait_ge(pixT_in[p], 8 * (k - p) + 16)
                if known is None or known >= 2:
                    pe.wait_ge(emb_raw, k - 1)
                for c in range(FEATURE_CHUNKS):
                    last = pe.matmul((ps_q, ps_a)[p][0:PAIR, 0:DIM], pixT[:, p, c, :], w_fold[:, c, :],
                                     start=(c == 0), stop=(c == FEATURE_CHUNKS - 1))
                last.then_inc(emb_ps, 1)

            pe.wait_ge(folded, 1)
            for k in range(2):
                embed(k, k, k)
            with pe.Fori(1, BEHIND // 2) as pair:
                embed(pair * 2, 0, None)
                embed(pair * 2 + 1, 1, None)
            pe.wait_ge(offset_step, 5 + SHIFTS + 8)
            pe.matmul(ps_v[0:PAIR, 0:DIM], ones[0:KC, 0:PAIR], w_center[:, 1, 0, :], start=True, stop=True)
            pe.matmul(ps_v[0:PAIR, DIM:2 * DIM], ones[0:KC, 0:PAIR], w_center[:, 0, 0, :], start=True, stop=False)
            pe.matmul(ps_v[0:PAIR, DIM:2 * DIM], ones[0:1, 0:PAIR], b_row[:, :], start=False, stop=True)\
                .then_inc(sums_ps, 1)
            with pe.Fori(BEHIND // 2, PAIRS // 2) as pair:
                embed(pair * 2, 0, None)
                embed(pair * 2 + 1, 1, None)
            pe.wait_ge(emb_raw, PAIRS)
            pe.wait_ge(sums_out, 2)
            pe.wait_ge(mpad_zero, 5)

            def heads():
                for g in range(GROUPS):
                    for r in range(ROWS):
                        yield g, r

            parts = [(w, x, c) for c in range(CHUNKS) for w in range(2) for x in range(2 - w)]

            def step(block, n, p, known):
                base = block * IMAGES
                q = 1 - p
                if runs(known, 0):
                    pe.wait_ge(xn_ready, n + base + 1)
                    if known is None or known + base >= 1:
                        pe.wait_ge(qm_ready, n + base)
                    if block and (known is None or known >= 4):
                        pe.wait_ge(logit_read, n - 3)
                    if block and (known is None or known >= 5):
                        pe.wait_ge(rank_read, n - 4)
                    for c in range(CHUNKS):
                        last = pe.transpose(ps_a[0:KC, c * SEQ:(c + 1) * SEQ], xn[:, p, c * KC:(c + 1) * KC],
                                            ident[0:SEQ, 0:SEQ])
                    last.then_inc(aT_ps, 1)
                if runs(known, 1):
                    pe.wait_ge(qm_ready, n + base)
                    for g, r in heads():
                        of_head = slice(SLOT * r, SLOT * (r + 1))
                        pe.matmul(ps_s[0:SEQ, r, g * SEQ:(g + 1) * SEQ], hi[of_head, q, 1, g, :],
                                  q_both[of_head, q, g, :], start=True, stop=False)
                        last = pe.matmul(ps_s[0:SEQ, r, g * SEQ:(g + 1) * SEQ], k_low[of_head, q, g, :],
                                         qm[of_head, q, g, :], start=False, stop=True)
                    last.then_inc(st_ps, 1)
                if runs(known, 2):
                    pe.wait_ge(o_ready, n + base - 1)
                    if known is None or known + base >= 3:
                        pe.wait_ge(att_done, n + base - 2)
                    for c in range(CHUNKS):
                        last = pe.transpose(ps_o[0:KC, c * SEQ:(c + 1) * SEQ],
                                            o[:, p].rearrange("s h d -> s (h d)")[:, c * KC:(c + 1) * KC],
                                            ident[0:SEQ, 0:SEQ])
                    last.then_inc(oT_ps, 1)
                if runs(known, 0):
                    pe.wait_ge(aT_ready, n + base + 1)
                    if known is None or known + base >= 2:
                        pe.wait_ge(o_ready, n + base - 1)
                    for a in range(2):
                        for g in range(GROUPS):
                            for i, (w, x, c) in enumerate(parts):
                                last = pe.matmul(ps_q[:, (a * GROUPS + g) * SEQ:(a * GROUPS + g + 1) * SEQ],
                                                 w_qk16[:, block, w, c, a, g, :], aT[:, p, x, c, :],
                                                 start=(i == 0), stop=(i == len(parts) - 1))
                    last.then_inc(qk_ps, 1)
                if runs(known, 2):
                    pe.wait_ge(oT_ready, n + base - 1)
                    for i, (x, w, c) in enumerate(parts):
                        k = KC + 1 - c
                        last = pe.matmul(ps_o[0:SEQ, 0:DIM], oT[0:k, x, c, :], w_p16[0:k, block, w, c, :],
                                         start=(i == 0), stop=(i == len(parts) - 1))
                    last.then_inc(pr_ps, 1)
                if runs(known, 0):
                    if known is None or known + base >= 1:
                        pe.wait_ge(v_ready, n + base)
                    for i, (x, w, c) in enumerate(parts):
                        last = pe.matmul(ps_v[0:SEQ, 0:DIM], aT[:, p, x, c, :], w_v16[:, block, w, c, :],
                                         start=(i == 0), stop=(i == len(parts) - 1))
                    last.then_inc(v_ps, 1)
                if runs(known, 0):
                    pe.wait_ge(qk_ready, n + base + 1)
                    if known is None or known + base >= 1:
                        pe.wait_ge(p_ready, n + base)
                    for g, r in heads():
                        last = pe.matmul(ps_s[0:SEQ, r, g * SEQ:(g + 1) * SEQ],
                                         hi[SLOT * r:SLOT * r + HEAD, p, 0, g, :],
                                         hi[SLOT * r:SLOT * r + HEAD, p, 1, g, :], start=True, stop=True)
                    last.then_inc(s_ps, 1)
                if block and runs(known, 3):
                    pe.wait_ge(xh_ready, n - 2)
                    if known is not None and known >= IMAGES:
                        if known - 4 < IMAGES:
                            pe.wait_ge(logit_read, n - 3)
                        if known - 5 < IMAGES:
                            pe.wait_ge(rank_read, n - 4)
                    for c in range(CHUNKS):
                        last = pe.transpose(ps_a[0:KC, c * SEQ:(c + 1) * SEQ], xh[:, q, c * KC:(c + 1) * KC],
                                            ident[0:SEQ, 0:SEQ])
                    last.then_inc(tT_ps, 1)
                for j, (g, r) in enumerate(heads()):
                    if j == 8 and runs(known, 0):
                        pe.wait_ge(max_ready, n + base + 1)
                        if block and runs(known, 3):
                            pe.wait_ge(tT_ready, n - 2)
                        for gg in range(GROUPS):
                            last = pe.transpose(ps_a[:, MAX_AT + gg * SEQ:MAX_AT + (gg + 1) * SEQ],
                                                mpad[:, p, gg].rearrange("q r d -> q (r d)"), ident[0:SEQ, 0:SEQ])
                        last.then_inc(mT_ps, 1)
                    if not runs(known, 1):
                        continue
                    if j == 0:
                        pe.wait_ge(p_lo_ready, n + base)
                        pe.wait_ge(v_ready, n + base)
                        if known is None or known < IMAGES:
                            pe.wait_ge(parts_ready, n + base + 1)
                        else:
                            pe.wait_ge(parts_ready, base + IMAGES)
                    h = ROWS * g + r
                    pe.matmul(ps_q[0:SEQ, h * AV:(h + 1) * AV], p_hi[:, q, r, g, :], values[:, q, h, :],
                              start=True, stop=False)
                    last = pe.matmul(ps_q[0:SEQ, h * AV:h * AV + HEAD + 1], p_lo[:, q, r, g, :],
                                     values[:, q, h, 0:HEAD + 1], start=False, stop=True)
                if runs(known, 1):
                    last.then_inc(av_ps, 1)

                if block and runs(known, 3):
                    pe.wait_ge(tT_ready, n - 2)
                    if runs(known, 0):
                        pe.wait_ge(qm_ready, n + base + 1)
                    for c in range(CHUNKS):
                        k = KC + 1 - c
                        last = pe.matmul(ps_a[0:SEQ, LOGIT_AT:LOGIT_AT + EXPERTS], tT[0:k, c, :], w_gate[0:k, c, :],
                                         start=(c == 0), stop=(c == CHUNKS - 1))
                    last.then_inc(logit_ps, 1)
                if block and runs(known, 4):
                    i = n - 4
                    if known is not None and known - 3 >= IMAGES:
                        pe.wait_ge(logit_read, IMAGES)
                        pe.wait_ge(rank_read, i)
                    pe.wait_ge(hits_ready, i + 1)
                    if known is None or known >= 5:
                        pe.wait_ge(seen_ready, i)
                    rank = ps_a[0:SEQ, RANK_AT:RANK_AT + EXPERTS]
                    pe.matmul(rank, before[:, :], hits[:, p], start=True, stop=False)
                    pe.matmul(rank, ones[0:SEQ, 0:SEQ], seen[:, p], start=False, stop=True).then_inc(rank_ps, 1)

            pe.wait_ge(route_in, 16 * ROUTE_LOADS)
            pe.wait_ge(consts, CONSTS)
            pe.wait_ge(w_lo_ready, 3 * BLOCKS)
            for b in range(BLOCKS):
                pipeline(pe, lambda n, p, known: step(b, n, p, known), lag_of(b))
            pe.wait_ge(seen_ready, IMAGES)
            pe.matmul(ps_v[0:1, 0:EXPERTS], ones[0:SEQ, 0:1], seen[:, 0], start=True, stop=True).then_inc(total_ps, 1)

            def rows_in(j, u, quad, known):
                p = u % 2
                if known is None or known >= 2:
                    pe.wait_ge(x32_ready, j - 1)
                pe.wait_ge(picked_in[u], quad * 16 + 16)
                for c in range(CHUNKS):
                    last = pe.transpose((ps_a, ps_v)[p][0:KC, c * TILE:(c + 1) * TILE],
                                        picked[:, u, c * KC:(c + 1) * KC], ident[:, :])
                last.then_inc(x_ps, 1)

            def up(j, p, known, first):
                pe.wait_ge(x_ready, j + 1)
                for half in range(HALVES):
                    if known is None or known >= 2:
                        pe.wait_ge(h32_ready, j * HALVES + (half + 1 - 2 * HALVES))
                    for m in range(PER_HALF):
                        steps = [(w, x, c) for c in range(CHUNKS) for w in range(2) for x in range(2 - w)]
                        for i, (w, x, c) in enumerate(steps):
                            k = KC + 1 - c
                            at = (w * CHUNKS + c) * HIDDEN + (half * PER_HALF + m) * 128
                            last = pe.matmul(ps_s[:, 2 * p + half, m * TILE:(m + 1) * TILE],
                                             w1[0:k, bass.ds(first + at, 128)], xs[0:k, p, x, c, :],
                                             start=(i == 0), stop=(i == len(steps) - 1))
                    last.then_inc(h_ps, 1)

            def down(j, p, known, first):
                if known is None or known >= 2:
                    pe.wait_ge(y_added, j - 1)
                for half in range(HALVES):
                    pe.wait_ge(h_ready, j * HALVES + (half + 1))
                    for m in range(PER_HALF):
                        for i, (h, w) in enumerate(((1, 0), (0, 0), (0, 1))):
                            at = (w * HIDDEN_CHUNKS + half * PER_HALF + m) * DIM
                            last = pe.matmul((ps_q, ps_o)[p][:, 0:DIM], hs[:, p, h, half, m, :],
                                             w2[:, bass.ds(first + at, DIM)],
                                             start=(half == m == i == 0),
                                             stop=(half == HALVES - 1 and m == PER_HALF - 1 and i == 2))
                last.then_inc(y_ps, 1)

            def step(j, u, quad, known, first):
                if known is None or known + 1 < TILES:
                    up(j + 1, (u + 1) % 2, None if known is None else known + 1, first[2])
                if known is None or known + 2 < TILES:
                    v = (u + 2) % SLOTS
                    rows_in(j + 2, v, quad + (u + 2) // SLOTS, None if known is None else known + 2)
                down(j, u % 2, known, first[1])

            pe.wait_ge(tables, 5)
            pe.wait_ge(lo_ready, EXPERTS)
            pe.wait_ge(xs_ones, 2)
            rows_in(0, 0, 0, 0)
            up(0, 0, 0, pe.value_load(weights_i[0:1, 0:1], min_val=0, max_val=W1_SIZE * (EXPERTS - 1)))
            rows_in(1, 1, 0, 1)
            tiles(pe, step, weights_i, (W1_SIZE * (EXPERTS - 1), W2_SIZE * (EXPERTS - 1)))


def _inputs(inputs):
    import numpy as np

    f = np.float32
    x = np.asarray(inputs["x"])
    side = x.shape[1]
    framed = np.zeros((IMAGES, side + 2, side + 2, CHANNELS), x.dtype)
    framed[:, 1:-1, 1:-1] = x
    r = PATCH
    tokens = []
    for i in range(SIDE):
        for j in range(SIDE):
            win = framed[:, r * i:r * i + r + 2, r * j:r * j + r + 2]
            tokens.append(np.concatenate([win[:, 1:-1, 1:-1].reshape(IMAGES, -1), win[:, 0, 1:-1].reshape(IMAGES, -1),
                                          win[:, -1, 1:-1].reshape(IMAGES, -1), win[:, 1:-1, 0].reshape(IMAGES, -1),
                                          win[:, 1:-1, -1].reshape(IMAGES, -1)], axis=1))
    pix = np.stack(tokens, 1).reshape(PAIRS, PAIR, FEATURES)
    pixT = pix.reshape(PAIRS, PAIR, FEATURE_CHUNKS, KC).transpose(0, 3, 2, 1)

    def by_source(a):
        a = a.reshape(r, r, SHIFTS, CHANNELS, -1)
        n = a.shape[-1]
        own = np.zeros((SHIFTS, r, r, CHANNELS, n), a.dtype)
        own[0] = a[:, :, 0]
        own[1][:, :-1] = a[:, 1:, 1]
        own[2][:, 1:] = a[:, :-1, 2]
        own[3][:-1] = a[1:, :, 3]
        own[4][1:] = a[:-1, :, 4]
        halo = np.concatenate([x.reshape(-1, n) for x in (a[0, :, 3], a[-1, :, 4], a[:, 0, 1], a[:, -1, 2])])
        return (own.reshape(SHIFTS, CENTER_CHUNKS, KC, n).transpose(2, 0, 1, 3), halo.reshape(2, KC, n).transpose(1, 0, 2))

    w_center, w_halo = by_source(np.asarray(inputs["L0_tok_W"]))

    def per_feature(a):
        own, halo = by_source(np.asarray(a).reshape(-1, 1))
        return np.concatenate([own.reshape(KC, -1), halo.reshape(KC, -1)], axis=1)

    def chunked(w):
        return w.reshape(-1, KC, w.shape[-1]).transpose(1, 0, 2)

    def attention(w_qkv, w_proj, b_proj):
        w = np.asarray(w_qkv)
        qk = np.zeros((DIM, 2, GROUPS, ROWS, SLOT), w.dtype)
        for copy in range(SLOT // HEAD):
            qk[..., copy * HEAD:(copy + 1) * HEAD] = w[0:2 * DIM].T.reshape(DIM, 2, GROUPS, ROWS, HEAD)
        p = np.zeros((KC + 1, CHUNKS, DIM), w.dtype)
        p[0:KC] = chunked(np.asarray(w_proj).T)
        p[KC, 0] = np.asarray(b_proj)
        return qk.reshape(CHUNKS, KC, 2, GROUPS, 128).transpose(1, 0, 2, 3, 4), chunked(w[2 * DIM:].T), p

    arrays = {"pix": pix, "pixT": pixT, "w_center": w_center, "w_halo": w_halo,
              "gain": per_feature(inputs["L0_tok_gamma"]), "shift": per_feature(inputs["L0_tok_beta"]),
              "tok_b": np.asarray(inputs["L0_tok_b"]).reshape(1, DIM),
              "txt": np.asarray(inputs["txt"]).transpose(1, 0, 2)}
    blocks = [attention(*(inputs[n] for n in names)) for names in (
        ("L0_attn_w_qkv", "L0_attn_w_proj", "L0_attn_b_proj"), ("L0_ffn_qkv_w", "L0_ffn_proj_w", "L0_ffn_proj_b"))]
    for name, parts in zip(("qk", "v", "p"), zip(*blocks)):
        arrays[name] = np.stack(parts)

    def with_bias(w, b):
        out = np.zeros((*w.shape[:-2], KC + 1, CHUNKS, w.shape[-1]), w.dtype)
        out[..., 0:KC, :, :] = w.reshape(*w.shape[:-2], CHUNKS, KC, w.shape[-1]).swapaxes(-3, -2)
        out[..., KC, 0, :] = b
        return out

    arrays["affine"] = np.stack([np.stack([np.asarray(inputs[f"L0_ffn_ln{i}_{x}"]).reshape(CHUNKS, KC).T for x in "gb"], 1)
                                 for i in (1, 2)], 1)
    arrays["gate"] = with_bias(np.asarray(inputs["L0_ffn_gate_w"]).T, np.asarray(inputs["L0_ffn_gate_b"]))
    arrays["e1"] = with_bias(np.asarray(inputs["L0_ffn_w1"]).swapaxes(1, 2), np.asarray(inputs["L0_ffn_b1"]))
    arrays["e2"] = np.asarray(inputs["L0_ffn_w2"]).swapaxes(1, 2).reshape(EXPERTS, HIDDEN_CHUNKS, 128, DIM)\
        .transpose(0, 2, 1, 3)
    arrays["eb"] = np.asarray(inputs["L0_ffn_b2"]).reshape(1, EXPERTS, DIM)
    arrays["before"] = np.triu(np.ones((SEQ, SEQ), f), 1)
    arrays["iota"] = np.broadcast_to(np.arange(EXPERTS, dtype=f), (SEQ, TOP, EXPERTS))
    arrays["region"] = np.broadcast_to(np.arange(EXPERTS, dtype=f) * REGION, (SEQ, EXPERTS))
    arrays["dest"] = np.arange(SEQ, dtype=f)[:, None] + np.arange(TOP, dtype=f) * TOKENS
    pad = np.zeros((TILE, ROW), f)
    pad.view(np.uint32)[:, DIM + 1] = NOWHERE
    arrays["padding"] = pad
    row = np.arange(128) % SLOT
    arrays["slot_rows"] = np.stack([-(row >= HEAD).astype(f), (row < HEAD).astype(f), MAX_SCALE * (row == HEAD)], 1)\
        .astype(f)
    arrays["jota"] = np.arange(LISTED, dtype=f)[None]
    return {k: np.ascontiguousarray(v) for k, v in arrays.items()}


def kernel(**inputs):
    import concourse.bacc as _bacc
    from concourse.bass_utils import run_bass_kernel_spmd as _run

    nc = _bacc.Bacc("TRN2", target_bir_lowering=False, num_devices=1)
    arrays = _inputs(inputs)
    tensors = {name: nc.dram_tensor("in_" + name, a.shape, mybir.dt.from_np(a.dtype), kind="ExternalInput").ap()
               for name, a in arrays.items()}
    tensors["out"] = nc.dram_tensor("out", (IMAGES, SEQ, DIM), F32, kind="ExternalOutput").ap()
    tensors["routed"] = nc.dram_tensor("routed", (EXPERTS * REGION + TILE, ROW), F32, kind="Internal").ap()
    tensors["results"] = nc.dram_tensor("results", (TOP * TOKENS, DIM), F32, kind="Internal").ap()
    build(nc, tensors)
    r = _run(nc, [{"in_" + name: a for name, a in arrays.items()}], core_ids=[0])
    return r.results[0]["out"]
```
